# Optimizing a Trainium2 kernel written in Bass

```python
import numpy as np
import jax
import jax.numpy as jnp

def _softmax(x, axis=-1):
    return jax.nn.softmax(x, axis=axis)

def _gelu(x):
    return jax.nn.gelu(x, approximate=True)

def _silu(x):
    return jax.nn.silu(x)

def _sigmoid(x):
    return jax.nn.sigmoid(x)

def _layernorm(x, axis=-1, eps=1e-05):
    m = jnp.mean(x, axis=axis, keepdims=True)
    v = jnp.var(x, axis=axis, keepdims=True)
    return (x - m) / jnp.sqrt(v + eps)

def _scatter_add(tgt, idx, src, axis=0):
    return tgt.at[idx].add(src)

def _segment_sum(src, seg, n):
    return jax.ops.segment_sum(src, seg, n)
kernel_name = 'mk_gps_d2_gnn_r8_c15e41'

def setup_inputs(seed: int=0):
    np.random.seed(seed)
    _w = jnp.asarray

    def _rec_inputs():
        import jax
        import jax.numpy as jnp
        _gk = jax.random.key(seed)
        x = -0.0003713 + 1 * jax.random.normal(jax.random.fold_in(_gk, 1), (6250, 256), jnp.float32)
        src = jax.random.randint(jax.random.fold_in(_gk, 2), (100000,), 0, 6250, jnp.int32)
        dst = jnp.minimum((6250 * jax.random.uniform(jax.random.fold_in(_gk, 3), (100000,)) ** 2.0).astype(jnp.int32), 49999)
        _o = jnp.argsort(dst, stable=True)
        src = src[_o]
        dst = dst[_o]
        return (x, src, dst)
    x, src, dst = _rec_inputs()

    def _L0_gnn_setup():
        import jax, jax.numpy as jnp
        import numpy as np
        N, E, D_IN, D_OUT = (6250, 200000, 256, 256)
        key = jax.random.key(seed)
        k1, k2, k3, k4, k5, k6 = jax.random.split(key, 6)
        x = jax.random.normal(k1, (N, D_IN), dtype=jnp.float32)
        edge_index = jax.random.randint(k2, (2, E), 0, N, dtype=jnp.int64)
        s = 1.0 / np.sqrt(D_IN)
        W1 = jax.random.uniform(k3, (D_OUT, D_IN), minval=-s, maxval=s, dtype=jnp.float32)
        b1 = jax.random.uniform(k4, (D_OUT,), minval=-s, maxval=s, dtype=jnp.float32)
        W2 = jax.random.uniform(k5, (D_OUT, D_IN), minval=-s, maxval=s, dtype=jnp.float32)
        b2 = jax.random.uniform(k6, (D_OUT,), minval=-s, maxval=s, dtype=jnp.float32)
        return {'x': x, 'W1': W1, 'b1': b1, 'W2': W2, 'b2': b2, 'edge_index': edge_index}
    _L0_gnn_all = _L0_gnn_setup()
    _L0_gnn_in = {k: v for k, v in _L0_gnn_all.items() if k in ('W1', 'b1', 'W2', 'b2')}
    del _L0_gnn_all

    def _L0_mix_setup():
        import jax, jax.numpy as jnp
        import numpy as np
        EMB, HEADS, DEPTH, SEQ, BATCH = (256, 8, 4, 1024, 4)
        DH = EMB // HEADS
        FF = 4 * EMB
        EPS = 1e-05

        def _layernorm(x, g, b):
            mu = x.mean(-1, keepdims=True)
            var = ((x - mu) ** 2).mean(-1, keepdims=True)
            return (x - mu) * jax.lax.rsqrt(var + EPS) * g + b

        def _linear_attn(x, Wq, Wk, Wv, Wo, bo):
            b, n, dm = x.shape
            split = lambda t: t.reshape(b, n, HEADS, DH).transpose(0, 2, 1, 3)
            scale = DH ** (-0.25)
            q = jax.nn.softmax(split(x @ Wq) * scale, axis=-1)
            k = jax.nn.softmax(split(x @ Wk) * scale, axis=-2)
            v = split(x @ Wv)
            context = jnp.einsum('bhnd,bhne->bhde', k, v)
            out = jnp.einsum('bhnd,bhde->bhne', q, context)
            out = out.transpose(0, 2, 1, 3).reshape(b, n, dm)
            return out @ Wo + bo

        def _forward(x, Wq, Wk, Wv, Wo, bo, ln1_g, ln1_b, W1, b1, W2, b2, ln2_g, ln2_b):
            for i in range(DEPTH):
                h = _layernorm(x, ln1_g[i], ln1_b[i])
                x = x + _linear_attn(h, Wq[i], Wk[i], Wv[i], Wo[i], bo[i])
                h = _layernorm(x, ln2_g[i], ln2_b[i])
                x = x + (jax.nn.gelu(h @ W1[i] + b1[i], approximate=False) @ W2[i] + b2[i])
            return x
        key = jax.random.key(seed)
        ks = jax.random.split(key, 8)
        w = lambda k, shape: jax.random.normal(k, shape, dtype=jnp.float32) * 0.02
        D = DEPTH
        return {'x': jax.random.normal(ks[0], (BATCH, SEQ, EMB), dtype=jnp.float32), 'Wq': w(ks[1], (D, EMB, EMB)), 'Wk': w(ks[2], (D, EMB, EMB)), 'Wv': w(ks[3], (D, EMB, EMB)), 'Wo': w(ks[4], (D, EMB, EMB)), 'bo': jnp.zeros((D, EMB), jnp.float32), 'ln1_g': jnp.ones((D, EMB), jnp.float32), 'ln1_b': jnp.zeros((D, EMB), jnp.float32), 'W1': w(ks[5], (D, EMB, FF)), 'b1': jnp.zeros((D, FF), jnp.float32), 'W2': w(ks[6], (D, FF, EMB)), 'b2': jnp.zeros((D, EMB), jnp.float32), 'ln2_g': jnp.ones((D, EMB), jnp.float32), 'ln2_b': jnp.zeros((D, EMB), jnp.float32)}
    _L0_mix_all = _L0_mix_setup()
    _L0_mix_in = {k: v for k, v in _L0_mix_all.items() if k in ('Wq', 'Wk', 'Wv', 'Wo', 'bo', 'ln1_g', 'ln1_b', 'W1', 'b1', 'W2', 'b2', 'ln2_g', 'ln2_b')}
    del _L0_mix_all

    def _L0_ffn_setup():
        import jax, jax.numpy as jnp
        import numpy as np
        B, A = (512, 8)
        IN, OUT = (256, 256)
        SH1, SH2 = (256, 128)
        EH1, EH2 = (128, 64)
        E, TOPK = (4, 2)

        def _shared_mlp(x, W1, b1, W2, b2, W3, b3):
            h = jax.nn.relu(x @ W1 + b1)
            h = jax.nn.relu(h @ W2 + b2)
            return h @ W3 + b3

        def _experts_mlp(x, eW1, eb1, eW2, eb2, eW3, eb3):
            h = jax.nn.relu(jnp.einsum('baf,efh->ebah', x, eW1) + eb1[:, None, None, :])
            h = jax.nn.relu(jnp.einsum('ebah,ehg->ebag', h, eW2) + eb2[:, None, None, :])
            o = jnp.einsum('ebag,ego->ebao', h, eW3) + eb3[:, None, None, :]
            return jnp.moveaxis(o, 0, -1)
        key = jax.random.key(seed)
        ks = jax.random.split(key, 16)
        s = 0.05
        return {'x': jax.random.normal(ks[0], (B, A, IN), jnp.float32), 'sW1': jax.random.normal(ks[1], (IN, SH1), jnp.float32) * s, 'sb1': jnp.zeros((SH1,), jnp.float32), 'sW2': jax.random.normal(ks[2], (SH1, SH2), jnp.float32) * s, 'sb2': jnp.zeros((SH2,), jnp.float32), 'sW3': jax.random.normal(ks[3], (SH2, OUT), jnp.float32) * s, 'sb3': jnp.zeros((OUT,), jnp.float32), 'eW1': jax.random.normal(ks[4], (E, IN, EH1), jnp.float32) * s, 'eb1': jnp.zeros((E, EH1), jnp.float32), 'eW2': jax.random.normal(ks[5], (E, EH1, EH2), jnp.float32) * s, 'eb2': jnp.zeros((E, EH2), jnp.float32), 'eW3': jax.random.normal(ks[6], (E, EH2, OUT), jnp.float32) * s, 'eb3': jnp.zeros((E, OUT), jnp.float32), 'gW': jax.random.normal(ks[7], (IN, E), jnp.float32) * s, 'gb': jnp.zeros((E,), jnp.float32)}
    _L0_ffn_all = _L0_ffn_setup()
    _L0_ffn_in = {k: v for k, v in _L0_ffn_all.items() if k in ('sW1', 'sb1', 'sW2', 'sb2', 'sW3', 'sb3', 'eW1', 'eb1', 'eW2', 'eb2', 'eW3', 'eb3', 'gW', 'gb')}
    del _L0_ffn_all

    def _L1_gnn_setup():
        import math
        import jax, jax.numpy as jnp
        import numpy as np
        N = 2500
        E = 40000
        D_IN = 256
        D_OUT = 256
        H = 8
        DK = D_OUT // H
        key = jax.random.key(seed)
        ks = jax.random.split(key, 16)
        h = jax.random.normal(ks[0], (N, D_IN), dtype=jnp.float32)
        src = jax.random.randint(ks[1], (E,), 0, N, dtype=jnp.int32)
        dst = jax.random.randint(ks[2], (E,), 0, N, dtype=jnp.int32)
        s = 1.0 / math.sqrt(D_IN)
        Wk = jax.random.uniform(ks[3], (D_OUT, D_IN), jnp.float32, -s, s)
        bk = jnp.zeros((D_OUT,), jnp.float32)
        Wq = jax.random.uniform(ks[4], (D_OUT, D_IN), jnp.float32, -s, s)
        bq = jnp.zeros((D_OUT,), jnp.float32)
        Wv = jax.random.uniform(ks[5], (D_OUT, D_IN), jnp.float32, -s, s)
        bv = jnp.zeros((D_OUT,), jnp.float32)
        so = 1.0 / math.sqrt(D_OUT)
        Wa = jax.random.uniform(ks[6], (D_OUT, D_OUT), jnp.float32, -so, so)
        ba = jnp.zeros((D_OUT,), jnp.float32)
        bound = math.sqrt(6.0 / (DK + DK))
        rel_att = jax.random.uniform(ks[7], (H, DK, DK), jnp.float32, -bound, bound)
        rel_msg = jax.random.uniform(ks[8], (H, DK, DK), jnp.float32, -bound, bound)
        rel_pri = jnp.ones((H,), jnp.float32)
        skip = jnp.ones((), jnp.float32)
        return {'h': h, 'src': src, 'dst': dst, 'Wk': Wk, 'bk': bk, 'Wq': Wq, 'bq': bq, 'Wv': Wv, 'bv': bv, 'Wa': Wa, 'ba': ba, 'rel_att': rel_att, 'rel_msg': rel_msg, 'rel_pri': rel_pri, 'skip': skip}
    _L1_gnn_all = _L1_gnn_setup()
    _L1_gnn_in = {k: v for k, v in _L1_gnn_all.items() if k in ('Wk', 'bk', 'Wq', 'bq', 'Wv', 'bv', 'Wa', 'ba', 'rel_att', 'rel_msg', 'rel_pri', 'skip')}
    del _L1_gnn_all

    def _L1_mix_setup():
        import jax, jax.numpy as jnp
        import numpy as np
        HEADS = 4
        DIM_HEAD = 32
        key = jax.random.key(seed)
        k1, k2, k3 = jax.random.split(key, 3)
        B, L, D = (16, 1024, 256)
        hidden = HEADS * DIM_HEAD
        x = jax.random.normal(k1, (B, L, D), dtype=jnp.float32)
        W_qkv = jax.random.normal(k2, (D, 3 * hidden), dtype=jnp.float32) * D ** (-0.5)
        W_out = jax.random.normal(k3, (hidden, D), dtype=jnp.float32) * hidden ** (-0.5)
        b_out = jnp.zeros((D,), dtype=jnp.float32)
        return {'x': x, 'W_qkv': W_qkv, 'W_out': W_out, 'b_out': b_out}
    _L1_mix_all = _L1_mix_setup()
    _L1_mix_in = {k: v for k, v in _L1_mix_all.items() if k in ('W_qkv', 'W_out', 'b_out')}
    del _L1_mix_all

    def _L1_ffn_setup():
        import jax, jax.numpy as jnp
        import numpy as np
        DIM = 256
        H = 8
        D = 64
        G = 64
        INNER = H * D
        SCALE = D ** (-0.5)
        key = jax.random.key(seed)
        ks = jax.random.split(key, 12)
        B, N = (4, 2048)
        x = jax.random.normal(ks[0], (B, N, DIM), dtype=jnp.float32)
        s = lambda fan_in: 1.0 / np.sqrt(fan_in)
        W_fx = jax.random.normal(ks[1], (DIM, INNER), dtype=jnp.float32) * s(DIM)
        b_fx = jnp.zeros((INNER,), dtype=jnp.float32)
        W_x = jax.random.normal(ks[2], (DIM, INNER), dtype=jnp.float32) * s(DIM)
        b_x = jnp.zeros((INNER,), dtype=jnp.float32)
        A = jax.random.normal(ks[3], (G, D), dtype=jnp.float32)
        Q, _ = jnp.linalg.qr(A.T)
        W_slice = Q[:, :G].astype(jnp.float32)
        b_slice = jnp.zeros((G,), dtype=jnp.float32)
        W_q = jax.random.normal(ks[4], (D, D), dtype=jnp.float32) * s(D)
        W_k = jax.random.normal(ks[5], (D, D), dtype=jnp.float32) * s(D)
        W_v = jax.random.normal(ks[6], (D, D), dtype=jnp.float32) * s(D)
        W_out = jax.random.normal(ks[7], (INNER, DIM), dtype=jnp.float32) * s(INNER)
        b_out = jnp.zeros((DIM,), dtype=jnp.float32)
        temperature = jnp.ones((1, H, 1, 1), dtype=jnp.float32) * 0.5
        return {'x': x, 'W_fx': W_fx, 'b_fx': b_fx, 'W_x': W_x, 'b_x': b_x, 'W_slice': W_slice, 'b_slice': b_slice, 'W_q': W_q, 'W_k': W_k, 'W_v': W_v, 'W_out': W_out, 'b_out': b_out, 'temperature': temperature}
    _L1_ffn_all = _L1_ffn_setup()
    _L1_ffn_in = {k: v for k, v in _L1_ffn_all.items() if k in ('W_fx', 'b_fx', 'W_x', 'b_x', 'W_slice', 'b_slice', 'W_q', 'W_k', 'W_v', 'W_out', 'b_out', 'temperature')}
    del _L1_ffn_all
    return {'x': x, 'src': src, 'dst': dst, 'L0_gnn_W1': _L0_gnn_in['W1'], 'L0_gnn_b1': _L0_gnn_in['b1'], 'L0_gnn_W2': _L0_gnn_in['W2'], 'L0_gnn_b2': _L0_gnn_in['b2'], 'L0_mix_Wq': _L0_mix_in['Wq'], 'L0_mix_Wk': _L0_mix_in['Wk'], 'L0_mix_Wv': _L0_mix_in['Wv'], 'L0_mix_Wo': _L0_mix_in['Wo'], 'L0_mix_bo': _L0_mix_in['bo'], 'L0_mix_ln1_g': _L0_mix_in['ln1_g'], 'L0_mix_ln1_b': _L0_mix_in['ln1_b'], 'L0_mix_W1': _L0_mix_in['W1'], 'L0_mix_b1': _L0_mix_in['b1'], 'L0_mix_W2': _L0_mix_in['W2'], 'L0_mix_b2': _L0_mix_in['b2'], 'L0_mix_ln2_g': _L0_mix_in['ln2_g'], 'L0_mix_ln2_b': _L0_mix_in['ln2_b'], 'L0_ffn_sW1': _L0_ffn_in['sW1'], 'L0_ffn_sb1': _L0_ffn_in['sb1'], 'L0_ffn_sW2': _L0_ffn_in['sW2'], 'L0_ffn_sb2': _L0_ffn_in['sb2'], 'L0_ffn_sW3': _L0_ffn_in['sW3'], 'L0_ffn_sb3': _L0_ffn_in['sb3'], 'L0_ffn_eW1': _L0_ffn_in['eW1'], 'L0_ffn_eb1': _L0_ffn_in['eb1'], 'L0_ffn_eW2': _L0_ffn_in['eW2'], 'L0_ffn_eb2': _L0_ffn_in['eb2'], 'L0_ffn_eW3': _L0_ffn_in['eW3'], 'L0_ffn_eb3': _L0_ffn_in['eb3'], 'L0_ffn_gW': _L0_ffn_in['gW'], 'L0_ffn_gb': _L0_ffn_in['gb'], 'L1_gnn_Wk': _L1_gnn_in['Wk'], 'L1_gnn_bk': _L1_gnn_in['bk'], 'L1_gnn_Wq': _L1_gnn_in['Wq'], 'L1_gnn_bq': _L1_gnn_in['bq'], 'L1_gnn_Wv': _L1_gnn_in['Wv'], 'L1_gnn_bv': _L1_gnn_in['bv'], 'L1_gnn_Wa': _L1_gnn_in['Wa'], 'L1_gnn_ba': _L1_gnn_in['ba'], 'L1_gnn_rel_att': _L1_gnn_in['rel_att'], 'L1_gnn_rel_msg': _L1_gnn_in['rel_msg'], 'L1_gnn_rel_pri': _L1_gnn_in['rel_pri'], 'L1_gnn_skip': _L1_gnn_in['skip'], 'L1_mix_W_qkv': _L1_mix_in['W_qkv'], 'L1_mix_W_out': _L1_mix_in['W_out'], 'L1_mix_b_out': _L1_mix_in['b_out'], 'L1_ffn_W_fx': _L1_ffn_in['W_fx'], 'L1_ffn_b_fx': _L1_ffn_in['b_fx'], 'L1_ffn_W_x': _L1_ffn_in['W_x'], 'L1_ffn_b_x': _L1_ffn_in['b_x'], 'L1_ffn_W_slice': _L1_ffn_in['W_slice'], 'L1_ffn_b_slice': _L1_ffn_in['b_slice'], 'L1_ffn_W_q': _L1_ffn_in['W_q'], 'L1_ffn_W_k': _L1_ffn_in['W_k'], 'L1_ffn_W_v': _L1_ffn_in['W_v'], 'L1_ffn_W_out': _L1_ffn_in['W_out'], 'L1_ffn_b_out': _L1_ffn_in['b_out'], 'L1_ffn_temperature': _L1_ffn_in['temperature']}

def reference(x, src, dst, L0_gnn_W1, L0_gnn_b1, L0_gnn_W2, L0_gnn_b2, L0_mix_Wq, L0_mix_Wk, L0_mix_Wv, L0_mix_Wo, L0_mix_bo, L0_mix_ln1_g, L0_mix_ln1_b, L0_mix_W1, L0_mix_b1, L0_mix_W2, L0_mix_b2, L0_mix_ln2_g, L0_mix_ln2_b, L0_ffn_sW1, L0_ffn_sb1, L0_ffn_sW2, L0_ffn_sb2, L0_ffn_sW3, L0_ffn_sb3, L0_ffn_eW1, L0_ffn_eb1, L0_ffn_eW2, L0_ffn_eb2, L0_ffn_eW3, L0_ffn_eb3, L0_ffn_gW, L0_ffn_gb, L1_gnn_Wk, L1_gnn_bk, L1_gnn_Wq, L1_gnn_bq, L1_gnn_Wv, L1_gnn_bv, L1_gnn_Wa, L1_gnn_ba, L1_gnn_rel_att, L1_gnn_rel_msg, L1_gnn_rel_pri, L1_gnn_skip, L1_mix_W_qkv, L1_mix_W_out, L1_mix_b_out, L1_ffn_W_fx, L1_ffn_b_fx, L1_ffn_W_x, L1_ffn_b_x, L1_ffn_W_slice, L1_ffn_b_slice, L1_ffn_W_q, L1_ffn_W_k, L1_ffn_W_v, L1_ffn_W_out, L1_ffn_b_out, L1_ffn_temperature):
    import jax
    import jax.numpy as jnp

    def _L0_gnn_ref(x, W1, b1, W2, b2, edge_index):
        import jax, jax.numpy as jnp
        import numpy as np
        N, E, D_IN, D_OUT = (6250, 200000, 256, 256)
        dst = edge_index[0]
        nbr = edge_index[1]
        n = x.shape[0]
        agg = jax.ops.segment_sum(x[nbr], dst, num_segments=n)
        cnt = jax.ops.segment_sum(jnp.ones((nbr.shape[0],), x.dtype), dst, num_segments=n)
        mean = agg / jnp.maximum(cnt, 1.0)[:, None]
        return x @ W1.T + b1 + mean @ W2.T + b2

    def _L0_mix_ref(x, Wq, Wk, Wv, Wo, bo, ln1_g, ln1_b, W1, b1, W2, b2, ln2_g, ln2_b):
        import jax, jax.numpy as jnp
        import numpy as np
        EMB, HEADS, DEPTH, SEQ, BATCH = (256, 8, 4, 1024, 4)
        DH = EMB // HEADS
        FF = 4 * EMB
        EPS = 1e-05

        def _layernorm(x, g, b):
            mu = x.mean(-1, keepdims=True)
            var = ((x - mu) ** 2).mean(-1, keepdims=True)
            return (x - mu) * jax.lax.rsqrt(var + EPS) * g + b

        def _linear_attn(x, Wq, Wk, Wv, Wo, bo):
            b, n, dm = x.shape
            split = lambda t: t.reshape(b, n, HEADS, DH).transpose(0, 2, 1, 3)
            scale = DH ** (-0.25)
            q = jax.nn.softmax(split(x @ Wq) * scale, axis=-1)
            k = jax.nn.softmax(split(x @ Wk) * scale, axis=-2)
            v = split(x @ Wv)
            context = jnp.einsum('bhnd,bhne->bhde', k, v)
            out = jnp.einsum('bhnd,bhde->bhne', q, context)
            out = out.transpose(0, 2, 1, 3).reshape(b, n, dm)
            return out @ Wo + bo

        def _forward(x, Wq, Wk, Wv, Wo, bo, ln1_g, ln1_b, W1, b1, W2, b2, ln2_g, ln2_b):
            for i in range(DEPTH):
                h = _layernorm(x, ln1_g[i], ln1_b[i])
                x = x + _linear_attn(h, Wq[i], Wk[i], Wv[i], Wo[i], bo[i])
                h = _layernorm(x, ln2_g[i], ln2_b[i])
                x = x + (jax.nn.gelu(h @ W1[i] + b1[i], approximate=False) @ W2[i] + b2[i])
            return x
        return _forward(x, Wq, Wk, Wv, Wo, bo, ln1_g, ln1_b, W1, b1, W2, b2, ln2_g, ln2_b)

    def _L0_ffn_ref(x, sW1, sb1, sW2, sb2, sW3, sb3, eW1, eb1, eW2, eb2, eW3, eb3, gW, gb):
        import jax, jax.numpy as jnp
        import numpy as np
        B, A = (512, 8)
        IN, OUT = (256, 256)
        SH1, SH2 = (256, 128)
        EH1, EH2 = (128, 64)
        E, TOPK = (4, 2)

        def _shared_mlp(x, W1, b1, W2, b2, W3, b3):
            h = jax.nn.relu(x @ W1 + b1)
            h = jax.nn.relu(h @ W2 + b2)
            return h @ W3 + b3

        def _experts_mlp(x, eW1, eb1, eW2, eb2, eW3, eb3):
            h = jax.nn.relu(jnp.einsum('baf,efh->ebah', x, eW1) + eb1[:, None, None, :])
            h = jax.nn.relu(jnp.einsum('ebah,ehg->ebag', h, eW2) + eb2[:, None, None, :])
            o = jnp.einsum('ebag,ego->ebao', h, eW3) + eb3[:, None, None, :]
            return jnp.moveaxis(o, 0, -1)
        all_out = _experts_mlp(x, eW1, eb1, eW2, eb2, eW3, eb3)
        shared = _shared_mlp(x, sW1, sb1, sW2, sb2, sW3, sb3)
        gates = jax.nn.softmax(x @ gW + gb, axis=-1)
        topv, topi = jax.lax.top_k(gates, TOPK)
        topw = jax.nn.softmax(topv, axis=-1)
        sel = jnp.take_along_axis(all_out, topi[:, :, None, :], axis=-1)
        gated = jnp.sum(sel * topw[:, :, None, :], axis=-1)
        return shared + gated

    def _L1_gnn_ref(h, src, dst, Wk, bk, Wq, bq, Wv, bv, Wa, ba, rel_att, rel_msg, rel_pri, skip):
        import math
        import jax, jax.numpy as jnp
        import numpy as np
        N = 2500
        E = 40000
        D_IN = 256
        D_OUT = 256
        H = 8
        DK = D_OUT // H
        n = h.shape[0]
        sqrt_dk = math.sqrt(DK)
        k = (h @ Wk.T + bk).reshape(n, H, DK)
        q = (h @ Wq.T + bq).reshape(n, H, DK)
        v = (h @ Wv.T + bv).reshape(n, H, DK)
        k = jnp.einsum('nhd,hde->nhe', k, rel_att)
        v = jnp.einsum('nhd,hde->nhe', v, rel_msg)
        score = jnp.einsum('ehd,ehd->eh', q[dst], k[src]) * rel_pri / sqrt_dk
        m = jax.ops.segment_max(score, dst, num_segments=n)
        ex = jnp.exp(score - m[dst])
        z = jax.ops.segment_sum(ex, dst, num_segments=n)
        attn = ex / z[dst]
        agg = jax.ops.segment_sum(v[src] * attn[:, :, None], dst, num_segments=n)
        t = agg.reshape(n, D_OUT)
        trans = t @ Wa.T + ba
        alpha = jax.nn.sigmoid(skip)
        return trans * alpha + h * (1.0 - alpha)

    def _L1_mix_ref(x, W_qkv, W_out, b_out):
        import jax, jax.numpy as jnp
        import numpy as np
        HEADS = 4
        DIM_HEAD = 32
        B, L, D = x.shape
        scale = DIM_HEAD ** (-0.5)
        qkv = jnp.einsum('bld,df->blf', x, W_qkv)
        qkv = qkv.reshape(B, L, 3, HEADS, DIM_HEAD)
        q = jnp.transpose(qkv[:, :, 0], (0, 2, 1, 3)) * scale
        k = jax.nn.softmax(jnp.transpose(qkv[:, :, 1], (0, 2, 1, 3)), axis=2)
        v = jnp.transpose(qkv[:, :, 2], (0, 2, 1, 3))
        context = jnp.einsum('bhld,bhle->bhde', k, v)
        out = jnp.einsum('bhde,bhld->bhle', context, q)
        out = jnp.transpose(out, (0, 2, 1, 3)).reshape(B, L, HEADS * DIM_HEAD)
        return jnp.einsum('blf,fd->bld', out, W_out) + b_out

    def _L1_ffn_ref(x, W_fx, b_fx, W_x, b_x, W_slice, b_slice, W_q, W_k, W_v, W_out, b_out, temperature):
        import jax, jax.numpy as jnp
        import numpy as np
        DIM = 256
        H = 8
        D = 64
        G = 64
        INNER = H * D
        SCALE = D ** (-0.5)
        B, N, _ = x.shape
        fx_mid = (x @ W_fx + b_fx).reshape(B, N, H, D).transpose(0, 2, 1, 3)
        x_mid = (x @ W_x + b_x).reshape(B, N, H, D).transpose(0, 2, 1, 3)
        temp = jnp.clip(temperature, 0.1, 5.0)
        slice_weights = jax.nn.softmax((x_mid @ W_slice + b_slice) / temp, axis=-1)
        slice_norm = slice_weights.sum(axis=2)
        slice_token = jnp.einsum('bhnc,bhng->bhgc', fx_mid, slice_weights)
        slice_token = slice_token / (slice_norm[..., None] + 1e-05)
        q = slice_token @ W_q
        k = slice_token @ W_k
        v = slice_token @ W_v
        attn = jax.nn.softmax(jnp.einsum('bhgc,bhkc->bhgk', q, k) * SCALE, axis=-1)
        out_slice = jnp.einsum('bhgk,bhkc->bhgc', attn, v)
        out_x = jnp.einsum('bhgc,bhng->bhnc', out_slice, slice_weights)
        out_x = out_x.transpose(0, 2, 1, 3).reshape(B, N, INNER)
        return out_x @ W_out + b_out
    edge_index = jnp.stack([src, dst])
    xn = _layernorm(x, axis=-1)
    x = x + _L0_gnn_ref(xn, L0_gnn_W1, L0_gnn_b1, L0_gnn_W2, L0_gnn_b2, edge_index) + _L0_mix_ref(xn[None], L0_mix_Wq, L0_mix_Wk, L0_mix_Wv, L0_mix_Wo, L0_mix_bo, L0_mix_ln1_g, L0_mix_ln1_b, L0_mix_W1, L0_mix_b1, L0_mix_W2, L0_mix_b2, L0_mix_ln2_g, L0_mix_ln2_b)[0]
    x = x + _L0_ffn_ref(_layernorm(x, axis=-1)[None], L0_ffn_sW1, L0_ffn_sb1, L0_ffn_sW2, L0_ffn_sb2, L0_ffn_sW3, L0_ffn_sb3, L0_ffn_eW1, L0_ffn_eb1, L0_ffn_eW2, L0_ffn_eb2, L0_ffn_eW3, L0_ffn_eb3, L0_ffn_gW, L0_ffn_gb)[0]
    xn = _layernorm(x, axis=-1)
    x = x + _L1_gnn_ref(xn, src, dst, L1_gnn_Wk, L1_gnn_bk, L1_gnn_Wq, L1_gnn_bq, L1_gnn_Wv, L1_gnn_bv, L1_gnn_Wa, L1_gnn_ba, L1_gnn_rel_att, L1_gnn_rel_msg, L1_gnn_rel_pri, L1_gnn_skip) + _L1_mix_ref(xn[None], L1_mix_W_qkv, L1_mix_W_out, L1_mix_b_out)[0]
    x = x + _L1_ffn_ref(_layernorm(x, axis=-1)[None], L1_ffn_W_fx, L1_ffn_b_fx, L1_ffn_W_x, L1_ffn_b_x, L1_ffn_W_slice, L1_ffn_b_slice, L1_ffn_W_q, L1_ffn_W_k, L1_ffn_W_v, L1_ffn_W_out, L1_ffn_b_out, L1_ffn_temperature)[0]
    return x

_drawn_inputs = setup_inputs


def setup_inputs(seed=0):
    import zlib

    import numpy as np

    out = dict(_drawn_inputs(seed))
    spreads = {'L0_mix_bo': (0.0, 0.1),
     'L0_mix_ln1_g': (1.0, 0.6),
     'L0_mix_ln1_b': (0.0, 0.769),
     'L0_mix_b1': (0.0, 0.1),
     'L0_mix_b2': (0.0, 0.1),
     'L0_mix_ln2_g': (1.0, 0.6),
     'L0_mix_ln2_b': (0.0, 0.609),
     'L0_ffn_sb1': (0.0, 0.8),
     'L0_ffn_sb2': (0.0, 0.366),
     'L0_ffn_sb3': (0.0, 0.1),
     'L0_ffn_eb1': (0.0, 0.8),
     'L0_ffn_eb2': (0.0, 0.8),
     'L0_ffn_eb3': (0.0, 0.1),
     'L0_ffn_gb': (0.0, 0.764),
     'L1_gnn_bk': (0.0, 2.0),
     'L1_gnn_bq': (0.0, 0.8),
     'L1_gnn_bv': (0.0, 0.451),
     'L1_gnn_ba': (0.0, 0.1),
     'L1_gnn_rel_pri': (1.0, 0.6),
     'L1_mix_b_out': (0.0, 0.1),
     'L1_ffn_b_fx': (0.0, 0.1),
     'L1_ffn_b_x': (0.0, 0.8),
     'L1_ffn_b_slice': (0.0, 2.0),
     'L1_ffn_b_out': (0.0, 0.1),
     'L1_ffn_temperature': (0.5, 0.6)}
    factors = {'L0_gnn_b1': 3.056,
     'L0_gnn_b2': 2.838,
     'L0_mix_Wq': 23.981,
     'L0_mix_Wk': 23.622,
     'L0_ffn_eW1': 2.772,
     'L1_gnn_Wk': 5.306,
     'L1_gnn_Wq': 5.367,
     'L1_gnn_rel_att': 5.285,
     'L1_ffn_W_x': 8.0,
     'L1_ffn_W_slice': 8.0,
     'L1_ffn_W_q': 8.0,
     'L1_ffn_W_k': 8.0}
    for name, (base, spread) in spreads.items():
        noise = np.random.default_rng([zlib.crc32(name.encode()), seed]).standard_normal(out[name].shape)
        drawn = base * np.exp(spread * noise) if base else spread * noise
        out[name] = jnp.asarray(drawn.astype(out[name].dtype))
    for name, factor in factors.items():
        out[name] = (out[name] * factor).astype(out[name].dtype)
    return out
```

```python
from contextlib import ExitStack, contextmanager

import concourse.bass as bass
from concourse import mybir

ALU = mybir.AluOpType
ACT = mybir.ActivationFunctionType
F32 = mybir.dt.float32
I32 = mybir.dt.int32
X_AXIS = mybir.AxisListType.X

NODES = 6250
EDGES = 100000
D = 256
HALVES = D // 128
TP = 125
NT = NODES // TP
PAIRS = NT // 2
PT = 2 * TP
DEPTH = 4
FF = 4 * D
HEAD = 32
EPS = 1e-5
BIG = 1e30


@contextmanager
def phase(nc, name, sems):
    with ExitStack() as ctx:
        made = {n: ctx.enter_context(nc.semaphore(f"{name}_{n}")) for n in sems}
        for n, credits in sems.items():
            nc.sync.sem_clear(made[n])
            if credits:
                nc.sync.sem_inc(made[n], credits)
        nc.all_engine_barrier(sem_only=True)

        def sb(n, shape, dtype=F32):
            return ctx.enter_context(nc.sbuf_tensor(f"{name}_{n}", shape, dtype))

        def ps(n, banks=1):
            return ctx.enter_context(nc.psum_tensor(f"{name}_{n}_ps", [128, banks, 512], F32))

        block = ctx.enter_context(nc.Block())
        yield block, made, sb, ps


def pairs(eng, main, ahead=None):
    if ahead:
        ahead(0, 0)
    with eng.Fori(0, PAIRS // 2) as j:
        for u in range(2):
            if ahead:
                ahead(2 * j + u + 1, 1 - u)
            main(2 * j + u, u)
    main(PAIRS - 1, 0)


def build(nc, A, out):
    with ExitStack() as ctx:
        def keep(n, shape, dtype=F32):
            return ctx.enter_context(nc.sbuf_tensor(n, shape, dtype))

        def dram(n, shape, dtype=F32):
            return nc.dram_tensor(n, shape, dtype, kind="Internal").ap()

        held = ctx.enter_context(nc.semaphore("held"))

        def hold(eng, sem, value):
            eng.wait_ge(sem, value)
            eng.sem_inc(held, 1)

        G = dict(
            ident=keep("ident", [128, 128]), ones=keep("ones", [128, 128]), zeros=keep("zeros", [128, 132]),
            below=keep("below", [128, 128]),
            spare=keep("spare", [128, 1]), spare_i=keep("spare_i", [128, 1], I32),
            mask32=keep("mask32", [128, 128]), mask64=keep("mask64", [128, 128]),
            X=keep("X", [TP, NT, D]),
            mv=keep("mv", [TP, NT, 2]),
            rstd=keep("rstd", [TP, NT]), shift=keep("shift", [TP, NT]),
            semaphore=lambda n: ctx.enter_context(nc.semaphore(n)),
            hold=hold, keep=keep, dram=dram, A=A, out=out,
        )
        constants(nc, G)
        load_x(nc, G)
        finish_stats(nc, G, "stats0")
        normalise_x(nc, G)
        with ExitStack() as steps:
            def step(n, shape, dtype=F32):
                return steps.enter_context(nc.sbuf_tensor(n, shape, dtype))
            T = dict(src=step("step_src", [EP, STEP_COLS], I32), rel=step("step_rel", [EP, STEP_COLS]),
                     n=step("step_n", [1, STEP_COLS], I32), e=step("step_e", [1, STEP_COLS], I32),
                     nodes=step("nodes", [EP, TP]), nodes_i=step("nodes_i", [EP, TP], I32),
                     gathered=G["semaphore"]("sched_gathered"))
            with nc.sbuf_tensor("src_all", [EP, GTILES], F32) as T["src_all"], \
                    nc.sbuf_tensor("dst_all", [EP, GTILES + GROUP], I32) as T["dst_all"]:
                schedule(nc, G, T)
                edges = EdgeSums(nc, G, T)
                mixer0(nc, G, edges)
            graph0_dense(nc, G, edges)
            finish_stats(nc, G, "x1stats")
            experts(nc, G)
            finish_stats(nc, G, "x2stats")
            layer1(nc, G, T)
        finish_stats(nc, G, "x3stats")
        slice_attention(nc, G)


def tile_of(T, q):
    return T[:, bass.ds(q, 1), :].rearrange("p a b -> p (a b)")


def pair_of(T, p):
    return T[:, bass.ds(2 * p, 2), :]


def constants(nc, G):
    with phase(nc, "const", dict(cleared=0, masks=0, spare=0)) as (block, s, sb, ps):
        @block.gpsimd
        def _(pool):
            pool.memset(G["ident"][:], 0.0).then_inc(s["cleared"], 1)
            pool.wait_ge(s["cleared"], 1)
            pool.affine_select(out=G["ident"][:], in_=G["ident"][:], compare_op=ALU.not_equal, fill=1.0,
                               base=0, pattern=[[-1, 128]], channel_multiplier=1)

            pool.memset(G["below"][:], 1.0).then_inc(s["cleared"], 1)
            pool.wait_ge(s["cleared"], 2)
            pool.affine_select(out=G["below"][:], in_=G["below"][:], compare_op=ALU.is_gt, fill=0.0,
                               base=0, pattern=[[-1, 128]], channel_multiplier=1)
            pool.iota(G["spare_i"][:], [[0, 1]], base=NODES, channel_multiplier=1).then_inc(s["spare"], 1)

        @block.vector
        def _(v):
            v.wait_ge(s["spare"], 1)
            v.tensor_copy(G["spare"][:], G["spare_i"][:])
            v.memset(G["ones"][:], 1.0)
            v.memset(G["zeros"][:], 0.0)
            v.memset(G["mask32"][:], 0.0)
            v.memset(G["mask64"][:], 0.0).then_inc(s["masks"], 1)
            v.wait_ge(s["masks"], 1)
            for m, w in (("mask32", 32), ("mask64", 64)):
                for g in range(128 // w):
                    v.memset(G[m][g * w:(g + 1) * w, g * w:(g + 1) * w], 1.0)


def stats_of_pair(v, G, s, st, X, p):
    G["hold"](v, s["stats_step"], 5 * p + 1)
    for t in range(2):
        v.bn_stats(st[:, t, 0:6], tile_of(X, 2 * p + t)).then_inc(s["stats_step"], 1)
    G["hold"](v, s["stats_step"], 5 * p + 3)
    for t in range(2):
        v.bn_aggr(st[:, t, 6:8], st[:, t, 0:6]).then_inc(s["stats_step"], 1)
    G["hold"](v, s["stats_step"], 5 * p + 5)
    v.tensor_copy(pair_of(G["mv"], p), st[:, :, 6:8]).then_inc(s["stats_step"], 1)


LOADS = 5


def load_x(nc, G):
    x_v = G["A"]["x"].rearrange("(t p) d -> p t d", p=TP)
    step = NT // LOADS
    with phase(nc, "loadx", dict({f"x{n}": 0 for n in range(LOADS)}, stats_step=1)) as (block, s, sb, ps):
        st = sb("st", [TP, 2, 8])

        @block.sync
        def _(sp):
            for n in range(LOADS):
                part = slice(n * step, (n + 1) * step)
                sp.dma_start(G["X"][:, part, :], x_v[:, part, :]).then_inc(s[f"x{n}"], 16)

        @block.vector
        def _(v):
            for n in range(LOADS):
                v.wait_ge(s[f"x{n}"], 16)
                with v.Fori(n * PAIRS // LOADS, (n + 1) * PAIRS // LOADS) as p:
                    stats_of_pair(v, G, s, st, G["X"], p)


def finish_stats(nc, G, name):
    with phase(nc, name, dict(step=0)) as (block, s, sb, ps):
        std = sb("std", [TP, NT])
        mean, var = G["mv"][:, :, 0], G["mv"][:, :, 1]

        @block.vector
        def _(v):
            v.tensor_scalar(std[:], var, EPS, None, ALU.add).then_inc(s["step"], 1)
            v.wait_ge(s["step"], 2)
            v.reciprocal(G["rstd"][:], std[:]).then_inc(s["step"], 1)
            v.wait_ge(s["step"], 3)
            v.scalar_tensor_tensor(out=G["shift"][:], in0=mean, scalar=-1.0, in1=G["rstd"][:],
                                   op0=ALU.mult, op1=ALU.mult).then_inc(s["step"], 1)

        @block.scalar
        def _(act):
            act.wait_ge(s["step"], 1)
            act.activation(std[:], std[:], ACT.Sqrt).then_inc(s["step"], 1)


def normalise_x(nc, G):
    G["xn_d"] = G["dram"]("xn_d", [NODES, D])
    xn_v = G["xn_d"].rearrange("(n t p) d -> n p t d", t=2, p=TP)
    with phase(nc, "normx", dict(done=0, out0=0, out1=0, stats_step=1)) as (block, s, sb, ps):
        st = sb("st", [TP, 2, 8])

        @block.vector
        def _(v):
            def apply(p, b):
                for t in range(2):
                    q = 2 * p + t
                    v.tensor_scalar(tile_of(G["X"], q), tile_of(G["X"], q), G["rstd"][:, bass.ds(q, 1)],
                                    G["shift"][:, bass.ds(q, 1)], ALU.mult, ALU.add).then_inc(s["done"], 1)
                v.wait_ge(s["done"], 2 * p + 2)
                stats_of_pair(v, G, s, st, G["X"], p)
            pairs(v, apply)

        @block.sync
        def _(sp):
            def save(p, b):
                G["hold"](sp, s["done"], 2 * p + 2)
                sp.dma_start(xn_v[bass.ds(p, 1)].rearrange("n p t d -> (n p) t d"),
                             pair_of(G["X"], p)).then_inc(s[f"out{b}"], 16)
            pairs(sp, save)
            sp.wait_ge(s["out0"], 16 * (PAIRS // 2 + 1))
            sp.wait_ge(s["out1"], 16 * (PAIRS // 2))


def hT_sems():
    return dict(h_ready=0, h_turned=2, hT_ready=1)


def normalise_pair(v, G, s, h, p, b):
    for t in range(2):
        q = 2 * p + t
        v.wait_ge(s["h_turned"], p + 1)
        v.tensor_scalar(h[:, b, t, :], tile_of(G["X"], q), G["rstd"][:, bass.ds(q, 1)],
                        G["shift"][:, bass.ds(q, 1)], ALU.mult, ALU.add).then_inc(s["h_ready"], 1)


def turn_pair(pe, G, s, h, psT, p, b):
    pe.wait_ge(s["h_ready"], 2 * p + 2)
    pe.wait_ge(s["hT_ready"], p + 1)
    for c in range(HALVES):
        for t in range(2):
            last = pe.transpose(psT[:, 0, c * 250 + t * TP:c * 250 + (t + 1) * TP],
                                h[:, b, t, c * 128:(c + 1) * 128], G["ident"][0:TP, 0:TP])
    last.then_inc(s["h_turned"], 1)


def affine_evacuate(act, s, psT, hT, gain, bias, p, b, free):
    act.wait_ge(s["h_turned"], p + 3)
    act.wait_ge(*free)
    for c in range(HALVES):
        src = psT[:, 0, c * 250:(c + 1) * 250]
        if gain is None:
            last = act.copy(hT[:, b, c, :], src)
        else:
            last = act.activation(hT[:, b, c, :], src, ACT.Identity, bias=bias[:, c:c + 1], scale=gain[:, c:c + 1])
    last.then_inc(s["hT_ready"], 1)


def mixer0(nc, G, edges):
    A = G["A"]
    q_d = G["dram"]("q_d", [PAIRS, TP, 2 * D])
    with ExitStack() as ctx:
        def keep(n, shape):
            return ctx.enter_context(nc.sbuf_tensor(n, shape, F32))
        Cp = keep("ctx_out", [128, HALVES, D])
        finish_stats(nc, G, "mstats")
        with nc.Fori(0, DEPTH) as l:
            with ExitStack() as kv:
                K = kv.enter_context(nc.sbuf_tensor("K", [TP, NT, D], F32))
                V = kv.enter_context(nc.sbuf_tensor("V", [TP, NT, HALVES, 129], F32))
                kmax = kv.enter_context(nc.sbuf_tensor("kmax", [TP, 2, D], F32))
                Wo = kv.enter_context(nc.sbuf_tensor("Wo", [128, HALVES, D], F32))
                mixer0_qkv(nc, G, l, K, V, kmax, Wo, q_d)
                context(nc, G, "ctx0", HALVES, K, V, kmax, HEAD ** -0.25, Wo, Cp)
            mixer0_attend(nc, G, l, q_d, Cp)
            finish_stats(nc, G, "astats")
            mixer0_ff(nc, G, l, edges)
            finish_stats(nc, G, "fstats")


def layer_rows(W, l):
    return W[bass.ds(l, 1)].rearrange("l (c p) n -> p (l c) n", p=128)


def layer_cols(b, l):
    return b[bass.ds(l, 1)].rearrange("l (c p) -> p (l c)", p=128)


def layer_bcast(b, l):
    return b[bass.ds(l, 1), :].to_broadcast([TP, b.shape[1]])


def mixer0_qkv(nc, G, l, K, V, kmax, Wo, q_d):
    A, hold, X = G["A"], G["hold"], G["X"]
    sems = dict(weights=0, q_ps=0, k_ps=0, v_ps=2, k_copied=2, v_copied=2, q_sub=2, q_exp=0,
                q_div=2, kmax_done=0, soft=0, q_ready=0, qout0=16, qout1=16, biased=0, **hT_sems())
    with phase(nc, "qkv", sems) as (block, s, sb, ps):
        Wqkv = sb("W", [128, HALVES, 3 * D])
        gain, bias = sb("gain", [128, HALVES]), sb("bias", [128, HALVES])
        bo = sb("bo", [TP, D])
        h = sb("h", [TP, 2, 2, D])
        hT = sb("hT", [128, 2, HALVES, PT])
        qs = sb("qs", [TP, 2, D])
        qe = sb("qe", [TP, 2, D])
        q = sb("q", [TP, 2, 2, D])
        qm, qz = sb("qm", [TP, 2, D // HEAD]), sb("qz", [TP, 2, D // HEAD])
        psT, qp, kp, vp = ps("psT"), ps("q", 2), ps("k", 2), ps("v", 2)
        heads = "p t (h e) -> p t h e"

        @block.sync
        def _(sp):
            for n, w in enumerate(("Wk", "Wq", "Wv")):
                sp.dma_start(Wqkv[:, :, n * D:(n + 1) * D], layer_rows(A[f"L0_mix_{w}"], l)).then_inc(s["weights"], 16)
            sp.dma_start(Wo[:], layer_rows(A["L0_mix_Wo"], l)).then_inc(s["weights"], 16)
            sp.dma_start(gain[:], layer_cols(A["L0_mix_ln1_g"], l), allow_slow_non_contiguous=True).then_inc(s["weights"], 16)
            sp.dma_start(bias[:], layer_cols(A["L0_mix_ln1_b"], l), allow_slow_non_contiguous=True).then_inc(s["weights"], 16)
            sp.dma_start(bo[:], layer_bcast(A["L0_mix_bo"], l)).then_inc(s["weights"], 16)

            def save(p, b):
                hold(sp, s["q_div"], p + 3)
                sp.dma_start(q_d[bass.ds(p, 1)].rearrange("n p d -> (n p) d"),
                             q[:, b].rearrange("p t d -> p (t d)")).then_inc(s[f"qout{b}"], 16)
            pairs(sp, save)
            sp.wait_ge(s["qout0"], 16 * 14)
            sp.wait_ge(s["qout1"], 16 * 13)

        @block.vector
        def _(v):
            v.memset(kmax[:], -BIG).then_inc(s["kmax_done"], 1)
            v.memset(V[:, :, :, 128:129], 1.0)

            def soft(p, b):
                qv = qp[0:TP, b].rearrange("p (t h e) -> p t h e", t=2, e=HEAD)
                v.wait_ge(s["q_ps"], p + 1)
                v.tensor_reduce(qm[:], qv, X_AXIS, ALU.max).then_inc(s["soft"], 1)
                v.wait_ge(s["soft"], 3 * p + 1)
                v.tensor_tensor(qs[:].rearrange(heads, e=HEAD), qv,
                                qm[:].unsqueeze(3).to_broadcast([TP, 2, D // HEAD, HEAD]),
                                ALU.subtract).then_inc(s["q_sub"], 1)
                v.wait_ge(s["k_copied"], p + 3)
                v.wait_ge(s["kmax_done"], p + 1)
                v.tensor_tensor(kmax[:], kmax[:], pair_of(K, p), ALU.max).then_inc(s["kmax_done"], 1)
                v.wait_ge(s["q_exp"], p + 1)
                v.tensor_reduce(qz[:], qe[:].rearrange(heads, e=HEAD), X_AXIS, ALU.add).then_inc(s["soft"], 1)
                v.wait_ge(s["soft"], 3 * p + 2)
                v.reciprocal(qz[:], qz[:]).then_inc(s["soft"], 1)
                v.wait_ge(s["q_div"], p + 3)
            pairs(v, soft, lambda p, b: normalise_pair(v, G, s, h, p, b))

        @block.gpsimd
        def _(pool):
            pool.wait_ge(s["weights"], 16 * 7)

            def divide(p, b):
                hold(pool, s["soft"], 3 * p + 3)
                hold(pool, s[f"qout{b}"], 16 * (p // 2) + 16)
                pool.tensor_tensor(q[:, b].rearrange(heads, e=HEAD), qe[:].rearrange(heads, e=HEAD),
                                   qz[:].unsqueeze(3).to_broadcast([TP, 2, D // HEAD, HEAD]),
                                   ALU.mult).then_inc(s["q_div"], 1)
                Xp = pair_of(X, p)
                hold(pool, s["h_ready"], 2 * p + 2)
                pool.tensor_tensor(Xp, Xp, bo[:].unsqueeze(1).to_broadcast([TP, 2, D]), ALU.add).then_inc(s["biased"], 1)
            pairs(pool, divide)

        @block.scalar
        def _(act):
            act.wait_ge(s["weights"], 16 * 7)

            def evacuate(p, b):
                affine_evacuate(act, s, psT, hT, gain, bias, p, b, (s["v_ps"], p + 1))

            def main(p, b):
                act.wait_ge(s["q_sub"], p + 3)
                act.activation(qe[:], qs[:], ACT.Exp, scale=HEAD ** -0.25).then_inc(s["q_exp"], 1)
                hold(act, s["k_ps"], p + 1)
                act.copy(pair_of(K, p), kp[0:TP, b].rearrange("p (t d) -> p t d", t=2)).then_inc(s["k_copied"], 1)
                hold(act, s["v_ps"], p + 3)
                act.copy(V[:, bass.ds(2 * p, 2), :, 0:128],
                         vp[0:TP, b].rearrange("p (t c e) -> p t c e", t=2, e=128)).then_inc(s["v_copied"], 1)
            pairs(act, main, evacuate)

        @block.tensor
        def _(pe):
            pe.wait_ge(s["weights"], 16 * 7)

            def project(p, b):
                pe.wait_ge(s["hT_ready"], p + 2)
                for n, (dst, free, done) in enumerate(((kp, "k_copied", "k_ps"), (qp, "q_sub", "q_ps"),
                                                       (vp, "v_copied", "v_ps"))):
                    pe.wait_ge(s[free], p + 1)
                    for t in range(2):
                        for c in range(HALVES):
                            last = pe.matmul(dst[0:TP, b, t * D:(t + 1) * D], hT[:, b, c, t * TP:(t + 1) * TP],
                                             Wqkv[:, c, n * D:(n + 1) * D], start=(c == 0), stop=(c == HALVES - 1))
                    last.then_inc(s[done], 1)
            pairs(pe, project, lambda p, b: turn_pair(pe, G, s, h, psT, p, b))


def context(nc, G, name, halves, K, V, kmax, scale, Wo, Cp, folded=None):
    hold, w = G["hold"], 128 * halves
    with phase(nc, name, dict(step=0, ks=0, exp=2, used=2, ctx=0)) as (block, s, sb, ps):
        kcol, D_kmax = sb("kcol", [128, halves]), sb("diag", [128, halves, 128])
        krow = sb("krow", [TP, w])
        ks, ek = sb("ks", [TP, 2, 2, w]), sb("ek", [TP, 2, 2, w])
        zinv = sb("zinv", [128, halves])
        C, CT = sb("C", [128, halves, 128]), sb("CT", [128, halves, 128])
        psA, psB, psC = ps("A"), ps("B"), ps("C", 2)

        @block.vector
        def _(v):
            v.tensor_tensor(krow[:], kmax[:, 0, :], kmax[:, 1, :], ALU.max).then_inc(s["step"], 1)
            v.wait_ge(s["step"], 2)
            v.tensor_reduce(kcol[:], psA[:, 0, 0:halves * TP].rearrange("p (c t) -> p c t", c=halves),
                            X_AXIS, ALU.max).then_inc(s["step"], 1)
            v.wait_ge(s["step"], 3)
            for c in range(halves):
                last = v.tensor_scalar(D_kmax[:, c, :], G["ident"][:], kcol[:, c:c + 1], None, ALU.mult)
            last.then_inc(s["step"], 1)
            v.wait_ge(s["step"], 5)
            v.tensor_copy(krow[:], psB[0:TP, 0, 0:w]).then_inc(s["step"], 1)
            v.wait_ge(s["step"], 6)

            def sub(p, b):
                v.wait_ge(s["exp"], p + 1)
                v.tensor_tensor(ks[:, b], pair_of(K, p), krow[:].unsqueeze(1).to_broadcast([TP, 2, w]),
                                ALU.subtract).then_inc(s["ks"], 1)
            pairs(v, sub)
            v.wait_ge(s["ctx"], 1)
            v.reciprocal(zinv[:], psC[:, 0:halves, 128]).then_inc(s["ctx"], 1)
            v.wait_ge(s["ctx"], 2)
            for c in range(halves):
                last = v.scalar_tensor_tensor(out=C[:, c, :], in0=psC[:, c, 0:128], scalar=zinv[:, c:c + 1],
                                              in1=G["mask32"][:], op0=ALU.mult, op1=ALU.mult)
            last.then_inc(s["ctx"], 1)
            v.wait_ge(s["ctx"], 4)
            v.tensor_copy(CT[:], psA[:, 0, 0:w].rearrange("p (c e) -> p c e", c=halves)).then_inc(s["ctx"], 1)
            v.wait_ge(s["ctx"], 6)
            v.tensor_copy(Cp[:], psB[:, 0, 0:halves * D].rearrange("p (c e) -> p c e", c=halves)).then_inc(s["ctx"], 1)
            if folded:
                v.wait_ge(s["ctx"], 8)
                v.tensor_scalar(folded[2][:], psA[:, 0, :].rearrange("p (c e) -> p c e", c=HALVES), folded[1], None,
                                ALU.mult).then_inc(s["ctx"], 1)

        @block.scalar
        def _(act):
            def exp(p, b):
                act.wait_ge(s["ks"], p + 1)
                act.wait_ge(s["used"], p + 1)
                act.activation(ek[:, b], ks[:, b], ACT.Exp, scale=scale).then_inc(s["exp"], 1)
            pairs(act, exp)

        @block.tensor
        def _(pe):
            pe.wait_ge(s["step"], 1)
            for c in range(halves):
                last = pe.transpose(psA[:, 0, c * TP:(c + 1) * TP], krow[:, c * 128:(c + 1) * 128],
                                    G["ident"][0:TP, 0:TP])
            last.then_inc(s["step"], 1)
            pe.wait_ge(s["step"], 4)
            for c in range(halves):
                last = pe.matmul(psB[0:TP, 0, c * 128:(c + 1) * 128], G["ones"][:, 0:TP], D_kmax[:, c, :],
                                 start=True, stop=True)
            last.then_inc(s["step"], 1)
            for c in range(halves):
                pe.matmul(psC[:, c, 0:129], G["zeros"][:, 0:128], G["zeros"][:, 0:129], start=True, stop=False,
                          skip_group_check=True)

            def gather(p, b):
                pe.wait_ge(s["exp"], p + 3)
                for t in range(2):
                    for c in range(halves):
                        end = isinstance(p, int) and t == 1
                        last = pe.matmul(psC[:, c, 0:129], ek[:, b, t, c * 128:(c + 1) * 128],
                                         V[:, bass.ds(2 * p + t, 1), c, :].rearrange("p a e -> p (a e)"),
                                         start=False, stop=end, skip_group_check=True)
                last.then_inc(s["used"], 1)
            pairs(pe, gather)
            pe.wait_ge(s["used"], 2 + PAIRS)
            pe.sem_inc(s["ctx"], 1)
            pe.wait_ge(s["ctx"], 3)
            for c in range(halves):
                last = pe.transpose(psA[:, 0, c * 128:(c + 1) * 128], C[:, c, :], G["ident"][:])
            last.then_inc(s["ctx"], 1)
            pe.wait_ge(s["ctx"], 5)
            for c in range(halves):
                last = pe.matmul(psB[:, 0, c * D:(c + 1) * D], CT[:, c, :], Wo[:, c, :], start=True, stop=True)
            last.then_inc(s["ctx"], 1)
            if folded:
                pe.wait_ge(s["ctx"], 7)
                for c in range(HALVES):
                    last = pe.matmul(psA[:, 0, c * D:(c + 1) * D], folded[0][:, c * 128:(c + 1) * 128], Cp[:, 0, :],
                                     start=True, stop=True)
                last.then_inc(s["ctx"], 1)


def mixer0_attend(nc, G, l, q_d, Cp):
    hold, X = G["hold"], G["X"]
    sems = dict(q0=0, q1=0, q_turned=2, qT=2, o=2, x_done=2, stats_step=1)
    with phase(nc, "attend", sems) as (block, s, sb, ps):
        q, qT = sb("q", [TP, 2, 2 * D]), sb("qT", [128, 2, HALVES, PT])
        st = sb("st", [TP, 2, 8])
        psT, o = ps("psT", 2), ps("o", 2)

        @block.sync
        def _(sp):
            def load(p, b):
                hold(sp, s["q_turned"], p + 1)
                sp.dma_start(q[:, b], q_d[bass.ds(p, 1)].rearrange("n p d -> (n p) d")).then_inc(s[f"q{b}"], 16)
            pairs(sp, load)

        @block.tensor
        def _(pe):
            def turn(p, b):
                pe.wait_ge(s[f"q{b}"], 16 * (p // 2) + 16)
                pe.wait_ge(s["qT"], p + 1)
                for c in range(HALVES):
                    for t in range(2):
                        last = pe.transpose(psT[:, b, c * PT + t * TP:c * PT + (t + 1) * TP],
                                            q[:, b, t * D + c * 128:t * D + (c + 1) * 128], G["ident"][0:TP, 0:TP])
                last.then_inc(s["q_turned"], 1)

            def out(p, b):
                pe.wait_ge(s["qT"], p + 3)
                pe.wait_ge(s["x_done"], p + 1)
                for t in range(2):
                    for c in range(HALVES):
                        last = pe.matmul(o[0:TP, b, t * D:(t + 1) * D], qT[:, b, c, t * TP:(t + 1) * TP], Cp[:, c, :],
                                         start=(c == 0), stop=(c == HALVES - 1))
                last.then_inc(s["o"], 1)
            pairs(pe, out, turn)

        @block.scalar
        def _(act):
            def evacuate(p, b):
                act.wait_ge(s["q_turned"], p + 3)
                act.wait_ge(s["o"], p + 1)
                act.copy(qT[:, b], psT[:, b, 0:2 * PT].rearrange("p (c t) -> p c t", c=HALVES)).then_inc(s["qT"], 1)
            pairs(act, evacuate)

        @block.vector
        def _(v):
            def add(p, b):
                add_and_stats(v, G, s, st, o[0:TP, b].rearrange("p (t d) -> p t d", t=2), p, 2)
            pairs(v, add)


def add_and_stats(v, G, s, st, src, p, credits):
    Xp = pair_of(G["X"], p)
    v.wait_ge(s["o"], p + 3)
    v.tensor_tensor(Xp, Xp, src, ALU.add).then_inc(s["x_done"], 1)
    v.wait_ge(s["x_done"], p + 1 + credits)
    stats_of_pair(v, G, s, st, G["X"], p)


def mixer0_ff(nc, G, l, edges):
    A, hold, X = G["A"], G["hold"], G["X"]
    blocks = FF // 128
    sems = dict(weights=0, hid=0, act_done=4, o=2, x_done=1, biased=0, stats_step=1, **hT_sems(), **edges.SEMS)
    with phase(nc, "ff", sems) as (block, s, sb, ps):
        W1, W2 = sb("W1", [128, HALVES, FF]), sb("W2", [128, blocks, D])
        gain, bias, b1 = sb("gain", [128, HALVES]), sb("bias", [128, HALVES]), sb("b1", [128, blocks])
        b2 = sb("b2", [TP, D])
        h, hT = sb("h", [TP, 2, 2, D]), sb("hT", [128, 2, HALVES, PT])
        act_out = sb("gelu", [128, 2, blocks, PT])
        st = sb("st", [TP, 2, 8])
        psT, hid, o = ps("psT"), ps("hid", 4), ps("o", 2)
        edges.buffers(s, sb, ps)

        @block.sync
        def _(sp):
            for dst, src in ((gain[:], layer_cols(A["L0_mix_ln2_g"], l)), (bias[:], layer_cols(A["L0_mix_ln2_b"], l)),
                             (b1[:], layer_cols(A["L0_mix_b1"], l)), (b2[:], layer_bcast(A["L0_mix_b2"], l)),
                             (W1[:], layer_rows(A["L0_mix_W1"], l)), (W2[:], layer_rows(A["L0_mix_W2"], l))):
                sp.dma_start(dst, src, allow_slow_non_contiguous=True).then_inc(s["weights"], 16)
            pairs(sp, lambda p, b: edges.source_rows(sp, l, p, b))

        @block.vector
        def _(v):
            edges.begin(v, l)

            def ahead(p, b):
                normalise_pair(v, G, s, h, p, b)
                edges.compare(v, l, p, b)

            def add(p, b):
                v.wait_ge(s["biased"], p + 1)
                add_and_stats(v, G, s, st, o[0:TP, :, 0:D], p, 1)
            pairs(v, add, ahead)

        @block.gpsimd
        def _(pool):
            pool.wait_ge(s["weights"], 16 * 6)
            for u in range(GROUP):
                edges.gather(pool, 0, 0, u)
            with pool.Fori(0, PAIRS // 2) as j:
                for b in range(2):
                    edges.move(pool, l, 2 * j + b, b)
                    add_bias(pool, G, s, b2, 2 * j + b)
            for u in range(GROUP):
                edges.scatter(pool, l, PAIRS - 1, 0, u)
            add_bias(pool, G, s, b2, PAIRS - 1)
            for u in range(GROUP):
                hold(pool, edges.stored[u], 16 * PAIRS * l + 16 * PAIRS + 16)

        @block.scalar
        def _(act):
            act.wait_ge(s["weights"], 16 * 6)

            def evacuate(p, b):
                affine_evacuate(act, s, psT, hT, gain, bias, p, b, (s["o"], p + 1))

            def gelu(p, b):
                for n in range(blocks):
                    act.wait_ge(s["hid"], blocks * p + n + 1)
                    act.activation(act_out[:, b, n, :], hid[:, n % 4, 0:PT], ACT.Gelu,
                                   bias=b1[:, n:n + 1]).then_inc(s["act_done"], 1)
                    edges.evacuate(act, l, p, n)
            pairs(act, gelu, evacuate)

        @block.tensor
        def _(pe):
            pe.wait_ge(s["weights"], 16 * 6)

            def products(p, b):
                pe.wait_ge(s["hT_ready"], p + 2)
                for n in range(blocks):
                    pe.wait_ge(s["act_done"], blocks * p + n + 1)
                    for c in range(HALVES):
                        last = pe.matmul(hid[:, n % 4, 0:PT],
                                         W1[:, c, n * 128:(n + 1) * 128], hT[:, b, c, :],
                                         start=(c == 0), stop=(c == HALVES - 1))
                    last.then_inc(s["hid"], 1)
                    edges.product(pe, l, p, b, n)
                pe.wait_ge(s["act_done"], blocks * p + blocks + 4)
                pe.wait_ge(s["x_done"], p + 1)
                for t in range(2):
                    for n in range(blocks):
                        last = pe.matmul(o[0:TP, t, 0:D], act_out[:, b, n, t * TP:(t + 1) * TP], W2[:, n, :],
                                         start=(n == 0), stop=(n == blocks - 1))
                last.then_inc(s["o"], 1)
            pairs(pe, products, lambda p, b: turn_pair(pe, G, s, h, psT, p, b))


def add_bias(pool, G, s, row, p):
    Xp = pair_of(G["X"], p)
    G["hold"](pool, s["h_ready"], 2 * p + 2)
    pool.tensor_tensor(Xp, Xp, row[:].unsqueeze(1).to_broadcast([TP, 2, D]), ALU.add).then_inc(s["biased"], 1)


EP = 128
ETILES = 784
CHUNKS, CHUNK_TILES = 16, 49
ROWS, ROW_TILES = 112, 7
UNROLL = 16
STEPS = 848
STEP_BLOCKS = 7
STEP_COLS = STEP_BLOCKS * 128
RING = 8
PAD_DST = 1000000
GROUP = 8
GROUPS = PAIRS * DEPTH
GTILES = GROUP * GROUPS
REPLICAS = 2
ACC_ROWS = NODES + 150


def schedule(nc, G, T):
    A, ident = G["A"], G["ident"]
    srcp, dstp = G["dram"]("src_tiles", [GTILES, EP], I32), G["dram"]("dst_tiles", [ETILES, EP], I32)
    n_d, e_d = G["dram"]("step_node_d", [STEP_BLOCKS, 128], I32), G["dram"]("step_edge_d", [STEP_BLOCKS, 128], I32)
    G["dst_tiles"], G["src_tiles"] = dstp, srcp
    whole = EDGES // EP
    full = (ROW_TILES - 1) * ROWS * EP
    left = whole - (ROW_TILES - 1) * ROWS
    gathered = T["gathered"]
    with phase(nc, "sched", dict(pad=0, load=0, table=0, v=0, ps=0, iota=0, pool=0, steps=0, turned=0)) as (block, s, sb, ps):
        rows = {n: sb(n, [ROWS, ROW_TILES, EP], I32) for n in ("src", "dst")}
        got = {n: sb("got_" + n, [128, STEP_BLOCKS, EP], I32) for n in ("src", "dst")}
        gotf = {n: sb("gotf_" + n, [128, STEP_BLOCKS, EP]) for n in ("src", "dst")}
        et, st = sb("et", [ROWS, ROW_TILES], I32), sb("st", [128, STEP_BLOCKS], I32)
        etf, stf = sb("etf", [ROWS, ROW_TILES]), sb("stf", [128, STEP_BLOCKS])
        last, quot, over = sb("last", [ROWS, ROW_TILES]), sb("quot", [ROWS, ROW_TILES]), sb("over", [ROWS, ROW_TILES])
        whole_q = sb("whole_q", [ROWS, ROW_TILES], I32)
        diag = sb("diag", [ROWS, ROW_TILES, ROWS])
        ends = sb("ends", [128, ETILES])
        less = sb("less", [128, ETILES])
        es, ns, n125 = sb("es", [128, STEP_BLOCKS]), sb("ns", [128, STEP_BLOCKS]), sb("n125", [128, STEP_BLOCKS])
        esi, nsi = sb("esi", [128, STEP_BLOCKS], I32), sb("nsi", [128, STEP_BLOCKS], I32)
        rowsf = {n: sb("rowsf_" + n, [ROWS, ROW_TILES, EP]) for n in ("src", "dst")}
        tail = sb("tail", [GTILES - ETILES, EP], I32)
        endp, tp, plain = ps("end", 2), ps("tp", 4), ps("plain", 2)

        @block.gpsimd
        def _(pool):
            pool.iota(et[:], [[ROWS, ROW_TILES]], base=0, channel_multiplier=1).then_inc(s["iota"], 1)
            pool.iota(st[:], [[128, STEP_BLOCKS]], base=0, channel_multiplier=1).then_inc(s["iota"], 1)
            pool.iota(T["nodes_i"][:], [[1, TP]], base=0, channel_multiplier=0).then_inc(s["iota"], 1)
            pool.wait_ge(s["table"], 48)
            pool.wait_ge(s["steps"], 1)
            for k in range(STEP_BLOCKS):
                for n, table in (("src", srcp), ("dst", dstp)):
                    pool.indirect_dma_start(got[n][:, k, :], None, table,
                                            bass.IndirectOffsetOnAxis(ap=esi[:, k:k + 1], axis=0)
                                            ).then_inc(gathered, 16)

        @block.sync
        def _(sp):
            sp.wait_ge(s["pad"], 2)
            for n in ("src", "dst"):
                sp.dma_start(rows[n][:, 0:ROW_TILES - 1, :],
                             A[n][0:full].rearrange("(k j e) -> j k e", j=ROWS, e=EP)).then_inc(s["load"], 16)
                sp.dma_start(rows[n][0:left, ROW_TILES - 1, :],
                             A[n][full:whole * EP].rearrange("(j e) -> j e", e=EP)).then_inc(s["load"], 16)
                sp.dma_start(rows[n][left:left + 1, ROW_TILES - 1, 0:EDGES - whole * EP],
                             A[n][whole * EP:EDGES].rearrange("(a e) -> a e", a=1)).then_inc(s["load"], 16)
            sp.wait_ge(s["load"], 96)
            for n, table in (("src", srcp), ("dst", dstp)):
                sp.dma_start(table[0:ETILES].rearrange("(k j) e -> j k e", j=ROWS), rows[n][:]).then_inc(s["table"], 16)
            sp.dma_start(srcp[ETILES:GTILES], tail[:]).then_inc(s["table"], 16)
            sp.wait_ge(s["table"], 48)
            sp.wait_ge(s["steps"], 1)
            for dst, src in ((n_d, nsi), (e_d, esi)):
                sp.dma_start(dst.rearrange("k p -> p k"), src[:], allow_slow_non_contiguous=True).then_inc(s["table"], 16)
            sp.wait_ge(s["table"], 80)
            for dst, src in ((T["n"], n_d), (T["e"], e_d)):
                sp.dma_start(dst[:], src.rearrange("(a k) p -> a (k p)", a=1)).then_inc(s["table"], 16)
            sp.wait_ge(s["table"], 112)

        @block.vector
        def _(v):
            count = [0]

            def link(ins):
                count[0] += 1
                ins.then_inc(s["v"], 1)
                v.wait_ge(s["v"], count[0])

            v.memset(tail[:], NODES)
            v.memset(T["src_all"][:, ETILES:GTILES], float(NODES))
            v.memset(T["dst_all"][:, ETILES:GTILES + GROUP], NODES - 1)
            v.memset(rows["src"][:], NODES).then_inc(s["pad"], 1)
            v.memset(rows["dst"][:], PAD_DST).then_inc(s["pad"], 1)
            v.wait_ge(s["iota"], 3)
            v.tensor_copy(etf[:], et[:])
            v.tensor_copy(stf[:], st[:])
            v.tensor_copy(T["nodes"][:], T["nodes_i"][:])
            v.wait_ge(s["load"], 96)
            v.tensor_copy(rowsf["src"][:], rows["src"][:])
            link(v.tensor_scalar(rowsf["dst"][:], rows["dst"][:], float(NODES - 1), None, ALU.min))
            v.wait_ge(s["ps"], 1)
            link(v.tensor_copy(T["src_all"][:, 0:ETILES].rearrange("p (b c) -> p b c", b=2), plain[:, :, 0:ETILES // 2]))
            v.wait_ge(s["ps"], 2)
            link(v.tensor_copy(T["dst_all"][:, 0:ETILES].rearrange("p (b c) -> p b c", b=2), plain[:, :, 0:ETILES // 2]))
            link(v.tensor_scalar(last[:], rows["dst"][:, :, EP - 1], 0.5, 1.0 / TP, ALU.add, ALU.mult))
            link(v.tensor_copy(whole_q[:], last[:]))
            link(v.tensor_copy(quot[:], whole_q[:]))
            link(v.tensor_tensor(over[:], quot[:], last[:], ALU.is_gt))
            link(v.tensor_tensor(quot[:], quot[:], over[:], ALU.subtract))
            link(v.scalar_tensor_tensor(out=quot[:], in0=quot[:], scalar=float(NT - 1), in1=etf[:],
                                        op0=ALU.min, op1=ALU.add))
            for k in range(ROW_TILES):
                d = v.tensor_scalar(diag[:, k, :], ident[0:ROWS, 0:ROWS], quot[:, k:k + 1], None, ALU.mult)
            link(d)
            v.wait_ge(s["ps"], 3)
            link(v.tensor_copy(ends[:].rearrange("p (b c) -> p b c", b=2), endp[:, :, 0:ETILES // 2]))
            for k in range(STEP_BLOCKS):
                link(v.tensor_scalar(less[:], ends[:], stf[:, k:k + 1], None, ALU.is_lt))
                link(v.tensor_reduce(es[:, k:k + 1], less[:], X_AXIS, ALU.add))
            link(v.tensor_scalar(es[:], es[:], float(ETILES - 1), None, ALU.min))
            link(v.tensor_tensor(ns[:], stf[:], es[:], ALU.subtract))
            link(v.tensor_scalar(n125[:], ns[:], float(TP), None, ALU.mult))
            link(v.tensor_scalar(ns[:], ns[:], float(NT - 1), None, ALU.min))
            link(v.tensor_copy(esi[:], es[:]))
            v.tensor_copy(nsi[:], ns[:]).then_inc(s["steps"], 1)
            v.wait_ge(gathered, 16 * 2 * STEP_BLOCKS)
            for k in range(STEP_BLOCKS):
                v.tensor_copy(gotf["src"][:, k, :], got["src"][:, k, :])
                d = v.tensor_scalar(gotf["dst"][:, k, :], got["dst"][:, k, :], n125[:, k:k + 1], None, ALU.subtract)
            d.then_inc(s["turned"], 1)
            v.wait_ge(s["turned"], 2)
            v.tensor_scalar(T["src"][:, 0:512], tp[:, 0, :], float(NODES - 1), None, ALU.min)
            v.tensor_scalar(T["src"][:, 512:STEP_COLS], tp[:, 1, 0:STEP_COLS - 512], float(NODES - 1), None, ALU.min)
            v.tensor_copy(T["rel"][:, 0:512], tp[:, 2, :])
            v.tensor_copy(T["rel"][:, 512:STEP_COLS], tp[:, 3, 0:STEP_COLS - 512])

        @block.tensor
        def _(pe):
            half = ETILES // 2

            def columns(dst, product):
                for k in range(ROW_TILES):
                    cut = min(max(half, k * ROWS), (k + 1) * ROWS)
                    for lo, hi in ((k * ROWS, cut), (cut, (k + 1) * ROWS)):
                        if hi > lo:
                            mm = product(dst[:, lo // half, lo % half:lo % half + hi - lo], k, lo - k * ROWS, hi - k * ROWS)
                mm.then_inc(s["ps"], 1)

            for n, name in enumerate(("src", "dst")):
                pe.wait_ge(s["v"], 1 + n)
                columns(plain, lambda d, k, lo, hi: pe.matmul(d, rowsf[name][:, k, :], ident[0:ROWS, lo:hi],
                                                              start=True, stop=True))
            pe.wait_ge(s["v"], 10)
            columns(endp, lambda d, k, lo, hi: pe.matmul(d, G["ones"][0:ROWS, :], diag[:, k, lo:hi],
                                                         start=True, stop=True))
            pe.wait_ge(s["turned"], 1)
            for b, n in ((0, "src"), (2, "dst")):
                for k in range(STEP_BLOCKS):
                    mm = pe.transpose(tp[:, b + k // 4, k % 4 * 128:(k % 4 + 1) * 128], gotf[n][:, k, :], ident[:])
            mm.then_inc(s["turned"], 1)


def blocks_of_steps(eng, block):
    block(0)
    with eng.Fori(1, STEPS // UNROLL) as j:
        block(j)


SUM_SLOTS = 8
SUM_LAG = 3
HOT_AHEAD = 4


def edge_sum(nc, G, name, T, ring, table, acc, extra, weights):
    hold, width = G["hold"], D + extra
    sems = dict(idx=0, hot=0, summed=SUM_SLOTS, added=SUM_SLOTS, cleared=0, weighted=RING)
    with phase(nc, name, sems) as (block, s, sb, ps):
        idx = sb("idx", [EP, 2, RING], I32)
        rows = sb("rows", [EP, RING, D])
        hot = sb("hot", [EP, SUM_SLOTS, TP])
        wr = sb("wr", [EP, SUM_SLOTS, width])
        sums = ps("sums", SUM_SLOTS)

        @block.gpsimd
        def _(pool):
            with pool.Fori(0, STEPS // UNROLL) as j:
                for u in range(UNROLL):
                    if u % RING == 0:
                        hold(pool, s["idx"], 2 * j + u // RING + 1)
                    hold(pool, s["weighted"], UNROLL * j + u + 1)
                    pool.indirect_dma_start(rows[:, u % RING, :], None, table,
                                            bass.IndirectOffsetOnAxis(ap=idx[:, u // RING, u % RING:u % RING + 1], axis=0)
                                            ).then_inc(ring[u % RING], 16)

        @block.scalar
        def _(act):
            with act.Fori(0, STEPS // UNROLL) as j:
                for u in range(2):
                    hold(act, s["weighted"], UNROLL * j + RING * u + 1)
                    act.copy(idx[:, u, :], T["src"][:, bass.ds(UNROLL * j + RING * u, RING)]).then_inc(s["idx"], 1)

        @block.tensor
        def _(pe):
            with pe.Fori(0, STEPS // UNROLL) as j:
                for u in range(UNROLL):
                    step, slot = UNROLL * j + u, u % SUM_SLOTS
                    hold(pe, s["weighted"], step + 1 + RING)
                    pe.wait_ge(s["hot"], step + 1)
                    pe.wait_ge(s["added"], step + 1)
                    pe.matmul(sums[0:TP, slot, 0:width], hot[:, slot, :], wr[:, slot, :], start=True, stop=True
                              ).then_inc(s["summed"], 1)

        @block.vector
        def _(v):
            v.memset(acc[:], 0.0).then_inc(s["cleared"], 1)
            v.wait_ge(s["cleared"], 1)

            def one_hot(step, slot):
                v.wait_ge(s["summed"], step + 1)
                v.tensor_scalar(hot[:, slot, :], T["nodes"][:], T["rel"][:, bass.ds(step, 1)], None,
                                ALU.is_equal).then_inc(s["hot"], 1)

            def weigh(step, u, j):
                slot = u % SUM_SLOTS
                e = v.value_load(T["e"][0:1, bass.ds(step, 1)], min_val=0, max_val=ETILES - 1)
                w = weights[:, bass.ds(e, 1), :].rearrange("p a h -> p (a h)")
                v.wait_ge(ring[u % RING], 32 * j + 16 * (u // RING) + 16)
                v.wait_ge(s["summed"], step + 1)
                v.tensor_copy(wr[:, slot, D:width], w)
                v.tensor_tensor(wr[:, slot, 0:D].rearrange("p (h e) -> p h e", h=extra),
                                rows[:, u % RING, :].rearrange("p (h e) -> p h e", h=extra),
                                w.unsqueeze(2).to_broadcast([EP, extra, D // extra]), ALU.mult
                                ).then_inc(s["weighted"], 1)

            def add(step, u):
                n = v.value_load(T["n"][0:1, bass.ds(step, 1)], min_val=0, max_val=NT - 1)
                a = tile_of(acc, n)
                v.wait_ge(s["summed"], step + 1 + SUM_SLOTS)
                v.wait_ge(s["added"], step + SUM_SLOTS)
                v.tensor_tensor(a, a, sums[0:TP, u % SUM_SLOTS, 0:width], ALU.add).then_inc(s["added"], 1)

            def steps(j):
                for u in range(UNROLL):
                    step = UNROLL * j + u
                    one_hot(step + HOT_AHEAD, (u + HOT_AHEAD) % SUM_SLOTS)
                    weigh(step, u, j)
                    if u >= SUM_LAG or not isinstance(j, int):
                        add(step - SUM_LAG, u - SUM_LAG)

            for k in range(HOT_AHEAD):
                one_hot(k, k)
            blocks_of_steps(v, steps)
            for k in range(STEPS - SUM_LAG, STEPS):
                add(k, k)


def fold(nc, G, name, jobs):
    sems = {f"load{n}": 0 for n in range(len(jobs))}
    with phase(nc, name, dict(spread=0, ps=0, out=1, **sems)) as (block, s, sb, ps):
        W = [sb(f"W{n}", [128, HALVES, D]) for n in range(len(jobs))]
        bc = [sb(f"b{n}", [128, HALVES]) for n in range(len(jobs))]
        bb = [sb(f"bb{n}", [128, HALVES, TP]) for n in range(len(jobs))]
        psW, psb = ps("W"), ps("b")

        @block.sync
        def _(sp):
            for n, (Wd, bd, _, _, _) in enumerate(jobs):
                sp.dma_start(W[n][:], Wd.rearrange("(c p) i -> p c i", p=128)).then_inc(s[f"load{n}"], 16)
                sp.dma_start(bc[n][:], bd.rearrange("(c p) -> p c", p=128),
                             allow_slow_non_contiguous=True).then_inc(s[f"load{n}"], 16)

        @block.vector
        def _(v):
            for n, (_, _, _, out, row) in enumerate(jobs):
                v.wait_ge(s[f"load{n}"], 32)
                for c in range(HALVES):
                    last = v.tensor_scalar(bb[n][:, c, :], G["ones"][:, 0:TP], bc[n][:, c:c + 1], None, ALU.mult)
                last.then_inc(s["spread"], 1)
                v.wait_ge(s["ps"], n + 1)
                v.tensor_copy(out, psW[:, 0, :].rearrange("p (m o) -> p m o", m=HALVES))
                v.tensor_copy(row, psb[0:TP, 0, 0:D]).then_inc(s["out"], 1)

        @block.tensor
        def _(pe):
            for n, (_, _, R, _, _) in enumerate(jobs):
                pe.wait_ge(s[f"load{n}"], 32)
                pe.wait_ge(s["spread"], n + 1)
                pe.wait_ge(s["out"], n + 1)
                for c in range(HALVES):
                    r = G["ident"][:] if R is None else R[:, c, :]
                    for m in range(HALVES):
                        pe.matmul(psW[:, 0, m * D + c * 128:m * D + (c + 1) * 128], W[n][:, c, m * 128:(m + 1) * 128],
                                  r, start=True, stop=True)
                    last = pe.matmul(psb[0:TP, 0, c * 128:(c + 1) * 128], bb[n][:, c, :], r, start=True, stop=True)
                last.then_inc(s["ps"], 1)


class EdgeSums:
    SEMS = dict(e_row0=0, e_row1=0, e_same=0, e_dup=0, e_idx=2, e_didx=0, e_mm=GROUP, e_evac=1)

    def __init__(self, nc, G, T):
        self.G, self.T, self.hold = G, T, G["hold"]
        self.landed = [G["semaphore"](f"edge_landed{n}") for n in range(2 * GROUP)]
        self.stored = [G["semaphore"](f"edge_stored{n}") for n in range(GROUP)]
        self.acc = [G["dram"](f"edge_sums{n}", [ACC_ROWS, D + 1]) for n in range(REPLICAS)]
        self.clear(nc)

    def clear(self, nc):
        each = ACC_ROWS * REPLICAS // GROUP
        parts = GROUP // REPLICAS
        with phase(nc, "eclear", dict(zero=0)) as (block, s, sb, ps):
            cols = ACC_ROWS // parts * (D + 1)
            p, n = next((p, cols // p) for p in range(128, 0, -1) if cols % p == 0)
            zero = sb("zero", [p, n])

            @block.vector
            def _(v):
                v.memset(zero[:], 0.0).then_inc(s["zero"], 1)

            @block.gpsimd
            def _(pool):
                pool.wait_ge(s["zero"], 1)
                for k in range(GROUP):
                    a = self.acc[k // parts].rearrange("r c -> (r c)")
                    part = k % parts
                    pool.dma_start(a[part * cols:(part + 1) * cols].rearrange("(p n) -> p n", p=p),
                                   zero[:]).then_inc(self.stored[k], 16)
                for k in range(GROUP):
                    pool.wait_ge(self.stored[k], 16)

    def buffers(self, s, sb, ps):
        self.s = s
        self.srow = sb("e_srow", [EP, 2, GROUP * EP], I32)
        self.didx, self.sidx = sb("e_didx", [EP, 2, GROUP], I32), sb("e_sidx", [EP, 2, GROUP], I32)
        self.same, self.junk = sb("e_same", [EP, GROUP, EP]), sb("e_junk", [EP, GROUP, EP])
        self.dup, self.tmp = sb("e_dup", [EP, GROUP]), sb("e_tmp", [EP, GROUP])
        self.rows = sb("e_rows", [EP, 2, GROUP, D + 1])
        self.comb = sb("e_comb", [EP, GROUP, D + 1])
        self.bank = ps("e_bank")

    def source_rows(self, sp, l, p, b):
        self.hold(sp, self.s["e_idx"], p + 1)
        src = self.G["src_tiles"].rearrange("(g t) e -> g (t e)", t=GROUP)
        sp.dma_start(self.srow[:, b, :], src[bass.ds(PAIRS * l + p, 1), :].to_broadcast([EP, GROUP * EP])
                     ).then_inc(self.s[f"e_row{b}"], 16)

    def gather_indices(self, v, l, p, b):
        if not isinstance(p, int) or p:
            self.hold(v, self.s["e_mm"], GROUP * p)
        v.tensor_copy(self.didx[:, b, :], self.T["dst_all"][:, bass.ds(GROUP * (PAIRS * l + p), GROUP)]
                      ).then_inc(self.s["e_didx"], 1)

    def begin(self, v, l):
        v.memset(self.rows[:, :, :, D:D + 1], 1.0).then_inc(self.s["e_dup"], 1)
        self.gather_indices(v, l, 0, 0)

    def compare(self, v, l, p, b):
        T, s, first = self.T, self.s, GROUP * (PAIRS * l + p)
        v.wait_ge(s[f"e_row{b}"], 16 * (p // 2) + 16)
        for u in range(GROUP):
            v.wait_ge(s["e_mm"], GROUP * p + u + 1)
            v.tensor_scalar(self.same[:, u, :], self.srow[:, b, u * EP:(u + 1) * EP],
                            T["src_all"][:, bass.ds(first + u, 1)], None, ALU.is_equal).then_inc(s["e_same"], 1)
        self.gather_indices(v, l, p + 1, 1 - b)
        v.wait_ge(s["e_dup"], 5 * p + 1)
        for u in range(GROUP):
            v.wait_ge(s["e_same"], GROUP * p + u + 1)
            ins = v.tensor_tensor_reduce(out=self.junk[:, u, :], in0=self.same[:, u, :], in1=self.G["below"][:],
                                         scale=1.0, scalar=0.0, op0=ALU.mult, op1=ALU.add,
                                         accum_out=self.dup[:, u:u + 1])
        ins.then_inc(s["e_dup"], 1)
        v.wait_ge(s["e_dup"], 5 * p + 2)
        sources = T["src_all"][:, bass.ds(first, GROUP)]
        v.tensor_scalar(self.dup[:], self.dup[:], 1.0, None, ALU.min).then_inc(s["e_dup"], 1)
        v.tensor_scalar(self.tmp[:], sources, -1.0, self.G["spare"][:, 0:1], ALU.mult, ALU.add).then_inc(s["e_dup"], 1)
        v.wait_ge(s["e_dup"], 5 * p + 4)
        v.tensor_tensor(self.tmp[:], self.tmp[:], self.dup[:], ALU.mult).then_inc(s["e_dup"], 1)
        v.wait_ge(s["e_dup"], 5 * p + 5)
        v.wait_ge(s["e_evac"], GROUP * p + 1)
        v.tensor_tensor(self.sidx[:, b, :], self.tmp[:], sources, ALU.add).then_inc(s["e_dup"], 1)
        v.wait_ge(s["e_dup"], 5 * p + 6)
        v.sem_inc(s["e_idx"], 1)

    def gather(self, pool, p, b, u):
        if u == 0:
            self.hold(pool, self.s["e_didx"], p + 1)
            pool.wait_ge(self.s["e_dup"], 1)
        self.hold(pool, self.s["e_mm"], GROUP * p + u + 1 - GROUP if not isinstance(p, int) or p else 1)
        pool.indirect_dma_start(self.rows[:, b, u, 0:D], None, self.G["xn_d"],
                                bass.IndirectOffsetOnAxis(ap=self.didx[:, b, u:u + 1], axis=0)).then_inc(self.landed[b * GROUP + u], 16)

    def scatter(self, pool, l, p, b, u):
        g = PAIRS * l + p
        if u == 0:
            self.hold(pool, self.s["e_idx"], p + 3)
        self.hold(pool, self.s["e_evac"], GROUP * p + u + 2)
        if u >= REPLICAS:
            self.hold(pool, self.stored[u - REPLICAS], 16 * g + 32)
        else:
            self.hold(pool, self.stored[u + GROUP - REPLICAS], 16 * g + 16)
        pool.indirect_dma_start(self.acc[u % REPLICAS], bass.IndirectOffsetOnAxis(ap=self.sidx[:, b, u:u + 1], axis=0),
                                self.comb[:, u, :], None, compute_op=ALU.add).then_inc(self.stored[u], 16)

    def move(self, pool, l, p, b):
        for u in range(GROUP):
            self.gather(pool, p + 1, 1 - b, u)
            self.scatter(pool, l, p, b, u)

    def product(self, pe, l, p, b, u):
        pe.wait_ge(self.landed[b * GROUP + u], 16 * ((PAIRS // 2 + 1 - b) * l + p // 2 + 1))
        pe.wait_ge(self.s["e_same"], GROUP * p + u + 1)
        pe.wait_ge(self.s["e_evac"], GROUP * p + u + 1)
        pe.matmul(self.bank[:, 0, 0:D + 1], self.same[:, u, :], self.rows[:, b, u, :], start=True, stop=True
                  ).then_inc(self.s["e_mm"], 1)

    def evacuate(self, act, l, p, u):
        act.wait_ge(self.s["e_mm"], GROUP * p + u + 1 + GROUP)
        act.wait_ge(self.stored[u], 16 * (PAIRS * l + p) + 16)
        act.copy(self.comb[:, u, :], self.bank[:, 0, 0:D + 1]).then_inc(self.s["e_evac"], 1)


def graph0_dense(nc, G, edges):
    A, hold, X = G["A"], G["hold"], G["X"]
    x_v = A["x"].rearrange("(n t p) d -> n p t d", t=2, p=TP)
    xn_v = G["xn_d"].rearrange("(n t p) d -> n p t d", t=2, p=TP)
    sums_v = [a[0:NODES].rearrange("(n t p) d -> n p t d", t=2, p=TP) for a in edges.acc]
    with ExitStack() as ctx:
        def sbuf(n, shape):
            return ctx.enter_context(nc.sbuf_tensor(n, shape, F32))
        W1T, W2T = sbuf("g0_W1T", [128, HALVES, D]), sbuf("g0_W2T", [128, HALVES, D])
        b1, b2 = sbuf("g0_b1", [TP, D]), sbuf("g0_b2", [TP, D])
        fold(nc, G, "g0_fold", [(A["L0_gnn_W1"], A["L0_gnn_b1"], None, W1T[:], b1[:]),
                                (A["L0_gnn_W2"], A["L0_gnn_b2"], None, W2T[:], b2[:])])
        sems = dict(in0=0, in1=0, step=0, turned=2, hT=2, o=2, biased=2, x_done=2, stats_step=1, both=0, mean=1)
        with phase(nc, "g0", sems) as (block, s, sb, ps):
            cinv = sb("cinv", [TP, 2])
            sums = sb("sums", [TP, 2, REPLICAS, 2, D + 1])
            total, mean = sb("total", [TP, 2, D + 1]), sb("mean", [TP, 2, 2, D])
            hT = sb("hT", [128, 2, 2, HALVES, PT])
            xin, xn, bb = sb("xin", [TP, 2, 2, D]), sb("xn", [TP, 2, 2, D]), sb("bb", [TP, D])
            st = sb("st", [TP, 2, 8])
            psT, o = ps("psT", 4), ps("o", 2)

            @block.sync
            def _(sp):
                def load(p, b):
                    hold(sp, s["biased"], p + 1)
                    hold(sp, s["turned"], p + 1)
                    for dst, src in ((xin[:, b], x_v), (xn[:, b], xn_v), (sums[:, b, 0], sums_v[0]),
                                     (sums[:, b, 1], sums_v[1])):
                        sp.dma_start(dst, src[bass.ds(p, 1)].rearrange("n p t d -> (n p) t d")).then_inc(s[f"in{b}"], 16)
                pairs(sp, load)

            @block.gpsimd
            def _(pool):
                pool.tensor_tensor(bb[:], b1[:], b2[:], ALU.add).then_inc(s["both"], 1)
                pool.wait_ge(s["both"], 1)

                def bias(p, b):
                    Xp = pair_of(X, p)
                    hold(pool, s[f"in{b}"], 64 * (p // 2) + 64)
                    pool.tensor_tensor(Xp, Xp, xin[:, b], ALU.add).then_inc(s["both"], 1)
                    hold(pool, s["both"], p + 2)
                    pool.tensor_tensor(Xp, Xp, bb[:].unsqueeze(1).to_broadcast([TP, 2, D]), ALU.add
                                       ).then_inc(s["biased"], 1)
                pairs(pool, bias)

            @block.vector
            def _(v):
                def means(p, b):
                    v.wait_ge(s[f"in{b}"], 64 * (p // 2) + 64)
                    v.wait_ge(s["mean"], p + 1)
                    v.tensor_tensor(total[:], sums[:, b, 0], sums[:, b, 1], ALU.add).then_inc(s["step"], 1)
                    v.wait_ge(s["step"], 3 * p + 1)
                    v.tensor_scalar(cinv[:], total[:, :, D], 1.0, None, ALU.max).then_inc(s["step"], 1)
                    v.wait_ge(s["step"], 3 * p + 2)
                    v.reciprocal(cinv[:], cinv[:]).then_inc(s["step"], 1)
                    v.wait_ge(s["step"], 3 * p + 3)
                    v.wait_ge(s["turned"], p + 1)
                    for t in range(2):
                        last = v.tensor_scalar(mean[:, b, t, :], total[:, t, 0:D], cinv[:, t:t + 1], None, ALU.mult)
                    last.then_inc(s["mean"], 1)

                def add(p, b):
                    v.wait_ge(s["biased"], p + 3)
                    add_and_stats(v, G, s, st, o[0:TP, b].rearrange("p (t d) -> p t d", t=2), p, 2)
                pairs(v, add, means)

            @block.tensor
            def _(pe):
                def turn(p, b):
                    pe.wait_ge(s["mean"], p + 2)
                    pe.wait_ge(s["hT"], p + 1)
                    for k, src in enumerate((xn, mean)):
                        for c in range(HALVES):
                            for t in range(2):
                                last = pe.transpose(psT[:, 2 * b + k, c * PT + t * TP:c * PT + (t + 1) * TP],
                                                    src[:, b, t, c * 128:(c + 1) * 128], G["ident"][0:TP, 0:TP])
                    last.then_inc(s["turned"], 1)

                def products(p, b):
                    pe.wait_ge(s["hT"], p + 3)
                    pe.wait_ge(s["x_done"], p + 1)
                    for t in range(2):
                        for k, w in enumerate((W1T, W2T)):
                            for c in range(HALVES):
                                last = pe.matmul(o[0:TP, b, t * D:(t + 1) * D], hT[:, b, k, c, t * TP:(t + 1) * TP],
                                                 w[:, c, :], start=(k + c == 0), stop=(k + c == 2))
                    last.then_inc(s["o"], 1)
                pairs(pe, products, turn)

            @block.scalar
            def _(act):
                def evacuate(p, b):
                    act.wait_ge(s["turned"], p + 3)
                    act.wait_ge(s["o"], p + 1)
                    for k in range(2):
                        last = act.copy(hT[:, b, k], psT[:, 2 * b + k, 0:2 * PT].rearrange("p (c t) -> p c t", c=HALVES))
                    last.then_inc(s["hT"], 1)
                pairs(act, evacuate)


EXPERTS, TOP = 4, 2


def row_of(b, width):
    return b.rearrange("(a d) -> a d", a=1).to_broadcast([TP, width])


def experts(nc, G):
    A, hold, X = G["A"], G["hold"], G["X"]
    S1, E1, S2, E2, BLOCKS, BANKS = 0, 2, 6, 7, 9, 3
    sems = dict(weights=0, const=0, blk=0, blk_done=BANKS, gate_ps=0, gate=0, gate_exp=0, gate_w=0, w_turned=0, w_sb=1,
                spread=0, scaled=0, o=2, x_done=2, stats_step=1, **hT_sems())
    with phase(nc, "moe", sems) as (block, s, sb, ps):
        sW1, sW2, sW3 = sb("sW1", [128, HALVES, D]), sb("sW2", [128, HALVES, 128]), sb("sW3", [128, D])
        eW1, eW2 = sb("eW1", [128, EXPERTS, HALVES, 128]), sb("eW2", [128, EXPERTS, 64])
        eW3, b3 = sb("eW3", [128, 2, D]), sb("b3", [EXPERTS + 1, D])
        bias = sb("bias", [128, BLOCKS])
        gW, gb = sb("gW", [128, HALVES, EXPERTS]), sb("gb", [TP, EXPERTS])
        sel = sb("sel", [EXPERTS + 1, 2, 2, 64])
        before = sb("before", [TP, EXPERTS, EXPERTS])
        h, hT = sb("h", [TP, 2, 2, D]), sb("hT", [128, 2, HALVES, PT])
        hid, gated = sb("hid", [128, BLOCKS, PT]), sb("gated", [128, 2, PT])
        g, ge, d = sb("g", [TP, 2, EXPERTS]), sb("ge", [TP, 2, EXPERTS]), sb("d", [TP, 2, EXPERTS])
        m, z = sb("m", [TP, 2]), sb("z", [TP, 2])
        gt, eq = sb("gt", [TP, 2, EXPERTS, EXPERTS]), sb("eq", [TP, 2, EXPERTS, EXPERTS])
        w5, w5T = sb("w5", [TP, 2, EXPERTS + 1]), sb("w5T", [EXPERTS + 1, PT])
        st = sb("st", [TP, 2, 8])
        psT, ring, gate_bank, spread, o = ps("psT"), ps("ring", BANKS), ps("gate"), ps("spread"), ps("o", 2)
        logits = gate_bank[0:TP, 0, 0:2 * EXPERTS].rearrange("p (t e) -> p t e", t=2)
        LOADS_N = 5 + EXPERTS + 9

        @block.sync
        def _(sp):
            def col(v, n):
                return v.rearrange("(c p) -> p c", p=128)[:, n:n + 1]
            loads = [(sW1[:], A["L0_ffn_sW1"].rearrange("(c p) h -> p c h", p=128)),
                     (sW2[:], A["L0_ffn_sW2"].rearrange("(c p) h -> p c h", p=128)),
                     (sW3[:], A["L0_ffn_sW3"]),
                     (eW2[:], A["L0_ffn_eW2"].rearrange("e p g -> p e g")),
                     (eW3[:], A["L0_ffn_eW3"].rearrange("(r e) g o -> (e g) r o", e=2))]
            loads += [(eW1[:, e], A["L0_ffn_eW1"][e].rearrange("(c p) h -> p c h", p=128)) for e in range(EXPERTS)]
            loads += [(b3[0:EXPERTS, :], A["L0_ffn_eb3"]),
                      (b3[EXPERTS:EXPERTS + 1, :], A["L0_ffn_sb3"].rearrange("(a d) -> a d", a=1)),
                      (gW[:], A["L0_ffn_gW"].rearrange("(c p) e -> p c e", p=128)),
                      (gb[:], row_of(A["L0_ffn_gb"], EXPERTS)),
                      (bias[:, S1:S1 + 2], A["L0_ffn_sb1"].rearrange("(c p) -> p c", p=128)),
                      (bias[:, E1:E1 + EXPERTS], A["L0_ffn_eb1"].rearrange("e p -> p e")),
                      (bias[:, S2:S2 + 1], A["L0_ffn_sb2"].rearrange("(c p) -> p c", p=128)),
                      (bias[0:64, E2:E2 + 2], A["L0_ffn_eb2"].rearrange("(r e) g -> e g r", e=2)[0]),
                      (bias[64:128, E2:E2 + 2], A["L0_ffn_eb2"].rearrange("(r e) g -> e g r", e=2)[1])]
            assert len(loads) == LOADS_N
            for dst, src in loads:
                sp.dma_start(dst, src, allow_slow_non_contiguous=True).then_inc(s["weights"], 16)

        @block.vector
        def _(v):
            v.memset(w5[:, :, EXPERTS:EXPERTS + 1], 1.0)
            v.memset(before[:], 0.0).then_inc(s["const"], 1)
            for k in range(EXPERTS):
                v.tensor_copy(sel[:, k // 2, k % 2, :], G["ident"][0:EXPERTS + 1, k:k + 1].to_broadcast([EXPERTS + 1, 64]))
            v.wait_ge(s["const"], 1)
            for e in range(1, EXPERTS):
                last = v.memset(before[:, e, 0:e], 1.0)
            last.then_inc(s["const"], 1)
            v.wait_ge(s["const"], 2)
            v.wait_ge(s["weights"], 16 * LOADS_N)

            OPS = 15

            def gates(p, b):
                done = [0]

                def step(ins):
                    done[0] += 1
                    ins.then_inc(s["gate"], 1)
                    v.wait_ge(s["gate"], OPS * p + done[0])

                def over_e(t):
                    return t.unsqueeze(2).to_broadcast([TP, 2, EXPERTS])
                v.wait_ge(s["gate_ps"], p + 1)
                step(v.tensor_tensor(g[:], logits, gb[:].unsqueeze(1).to_broadcast([TP, 2, EXPERTS]), ALU.add))
                step(v.tensor_reduce(m[:], g[:], X_AXIS, ALU.max))
                v.tensor_tensor(d[:], g[:], over_e(m[:]), ALU.subtract).then_inc(s["gate_w"], 1)
                v.wait_ge(s["gate_exp"], 2 * p + 1)
                step(v.tensor_reduce(z[:], ge[:], X_AXIS, ALU.add))
                step(v.reciprocal(z[:], z[:]))
                step(v.tensor_tensor(g[:], ge[:], over_e(z[:]), ALU.mult))
                of_j = g[:].unsqueeze(2).to_broadcast([TP, 2, EXPERTS, EXPERTS])
                of_e = g[:].unsqueeze(3).to_broadcast([TP, 2, EXPERTS, EXPERTS])
                v.tensor_tensor(gt[:], of_j, of_e, ALU.is_gt)
                step(v.tensor_tensor(eq[:], of_j, of_e, ALU.is_equal))
                step(v.tensor_tensor(eq[:], eq[:], before[:].unsqueeze(1).to_broadcast([TP, 2, EXPERTS, EXPERTS]), ALU.mult))
                step(v.tensor_tensor(gt[:], gt[:], eq[:], ALU.add))
                step(v.tensor_reduce(d[:], gt[:], X_AXIS, ALU.add))
                step(v.tensor_scalar(d[:], d[:], float(TOP), None, ALU.is_lt))
                step(v.tensor_reduce(m[:], g[:], X_AXIS, ALU.max))
                v.tensor_tensor(g[:], g[:], over_e(m[:]), ALU.subtract).then_inc(s["gate_w"], 1)
                v.wait_ge(s["gate_exp"], 2 * p + 2)
                step(v.tensor_tensor(d[:], d[:], ge[:], ALU.mult))
                step(v.tensor_reduce(z[:], d[:], X_AXIS, ALU.add))
                step(v.reciprocal(z[:], z[:]))
                step(v.tensor_tensor(w5[:, :, 0:EXPERTS], d[:], over_e(z[:]), ALU.mult))
                assert done[0] == OPS

            def main(p, b):
                gates(p, b)
                v.wait_ge(s["spread"], p + 1)
                v.wait_ge(s["blk_done"], BLOCKS * p + BLOCKS + BANKS)
                v.tensor_tensor(gated[:], hid[:, E2:E2 + 2, :], spread[:, 0, 0:2 * PT].rearrange("p (r t) -> p r t", r=2),
                                ALU.mult).then_inc(s["scaled"], 1)
                add_and_stats(v, G, s, st, o[0:TP, b].rearrange("p (t d) -> p t d", t=2), p, 2)
            pairs(v, main, lambda p, b: normalise_pair(v, G, s, h, p, b))

        @block.scalar
        def _(act):
            act.wait_ge(s["weights"], 16 * LOADS_N)

            def relu(p, n):
                act.wait_ge(s["blk"], BLOCKS * p + n + 1)
                act.activation(hid[:, n, :], ring[:, n % BANKS, 0:PT], ACT.Relu, bias=bias[:, n:n + 1]
                               ).then_inc(s["blk_done"], 1)

            def main(p, b):
                relu(p, 0)
                relu(p, 1)
                act.wait_ge(s["gate_w"], 2 * p + 1)
                act.activation(ge[:], d[:], ACT.Exp).then_inc(s["gate_exp"], 1)
                relu(p, 2)
                relu(p, 3)
                relu(p, 4)
                act.wait_ge(s["gate_w"], 2 * p + 2)
                act.activation(ge[:], g[:], ACT.Exp).then_inc(s["gate_exp"], 1)
                relu(p, 5)
                relu(p, 6)
                act.wait_ge(s["w_turned"], p + 1)
                act.copy(w5T[:], gate_bank[0:EXPERTS + 1, 0, 64:64 + PT]).then_inc(s["w_sb"], 1)
                relu(p, 7)
                relu(p, 8)
            pairs(act, main, lambda p, b: affine_evacuate(act, s, psT, hT, None, None, p, b, (s["o"], p + 1)))

        @block.tensor
        def _(pe):
            pe.wait_ge(s["weights"], 16 * LOADS_N)
            pe.wait_ge(s["const"], 2)

            def main(p, b):
                x = [hT[:, b, c, :] for c in range(HALVES)]

                def blk(n, products):
                    pe.wait_ge(s["blk_done"], BLOCKS * p + n + 1)
                    for lo, hi, k, last_k, w, r in products:
                        mm = pe.matmul(ring[lo:hi, n % BANKS, 0:PT], w, r, start=(k == 0), stop=(k == last_k))
                    mm.then_inc(s["blk"], 1)
                pe.wait_ge(s["hT_ready"], p + 2)
                pe.wait_ge(s["w_sb"], p + 1)
                for t in range(2):
                    for c in range(HALVES):
                        mm = pe.matmul(gate_bank[0:TP, 0, t * EXPERTS:(t + 1) * EXPERTS],
                                       hT[:, b, c, t * TP:(t + 1) * TP], gW[:, c, :], start=(c == 0), stop=(c == 1))
                mm.then_inc(s["gate_ps"], 1)
                for n in range(2):
                    blk(S1 + n, [(0, 128, c, 1, sW1[:, c, n * 128:(n + 1) * 128], x[c]) for c in range(HALVES)])
                for e in range(EXPERTS):
                    blk(E1 + e, [(0, 128, c, 1, eW1[:, e, c, :], x[c]) for c in range(HALVES)])
                pe.wait_ge(s["gate"], 15 * p + 15)
                for t in range(2):
                    mm = pe.transpose(gate_bank[0:EXPERTS + 1, 0, 64 + t * TP:64 + (t + 1) * TP], w5[:, t, :],
                                      G["ident"][0:TP, 0:TP])
                mm.then_inc(s["w_turned"], 1)
                blk(S2, [(0, 128, c, 1, sW2[:, c, :], hid[:, S1 + c, :]) for c in range(HALVES)])
                pe.wait_ge(s["blk_done"], BLOCKS * p + 6 + BANKS)
                for r in range(2):
                    blk(E2 + r, [(64 * k, 64 * k + 64, 0, 0, eW2[:, 2 * r + k, :], hid[:, E1 + 2 * r + k, :]) for k in range(2)])
                pe.wait_ge(s["w_sb"], p + 2)
                for r in range(2):
                    mm = pe.matmul(spread[:, 0, r * PT:(r + 1) * PT], sel[:, r].rearrange("k e g -> k (e g)"), w5T[:],
                                   start=True, stop=True)
                mm.then_inc(s["spread"], 1)
                pe.wait_ge(s["scaled"], p + 1)
                pe.wait_ge(s["x_done"], p + 1)
                for t in range(2):
                    cols = slice(t * TP, (t + 1) * TP)
                    for k, (l, r) in enumerate(((hid[:, S2, cols], sW3[:]), (w5T[:, cols], b3[:]),
                                                (gated[:, 0, cols], eW3[:, 0, :]), (gated[:, 1, cols], eW3[:, 1, :]))):
                        mm = pe.matmul(o[0:TP, b, t * D:(t + 1) * D], l, r, start=(k == 0), stop=(k == 3))
                mm.then_inc(s["o"], 1)
            pairs(pe, main, lambda p, b: turn_pair(pe, G, s, h, psT, p, b))


MW = 128


class Layer1:

    def __init__(self, nc, G, ctx):
        def keep(n, shape):
            return ctx.enter_context(nc.sbuf_tensor("l1_" + n, shape, F32))
        self.WqT, self.WkT, self.WvT = (keep(n, [128, HALVES, D]) for n in ("WqT", "WkT", "WvT"))
        self.WaT = keep("WaT", [128, HALVES, D])
        self.bq, self.bk, self.bv, self.ba = (keep(n, [TP, D]) for n in ("bq", "bk", "bv", "ba"))
        self.keep_h = keep("keep_h", [128, 1])
        self.Wm, self.WqmT = keep("Wm", [128, HALVES, 3 * MW]), keep("WqmT", [128, D])
        self.Wmo, self.Gm = keep("Wmo", [128, 1, D]), keep("Gm", [128, HALVES, D])
        A = G["A"]
        with ExitStack() as tmp:
            def sbuf(n, shape):
                return tmp.enter_context(nc.sbuf_tensor("l1_" + n, shape, F32))
            att, msg, scale, gain = (sbuf(n, [128, HALVES, 128]) for n in ("att", "msg", "scale", "gain"))
            with phase(nc, "l1prep", dict(clear=0, load=0, v=0, act=0, turned=0)) as (block, s, sb, ps):
                pri, alpha, bo = sb("pri", [128, HALVES]), sb("alpha", [128, 1]), sb("bo", [TP, D])
                tp = ps("tp")
                heads = D // HEAD

                @block.sync
                def _(sp):
                    n = 0
                    sp.wait_ge(s["clear"], 2)
                    for k in range(heads):
                        c, r = divmod(k, 128 // HEAD)
                        rows = slice(r * HEAD, (r + 1) * HEAD)
                        sp.dma_start(att[rows, c, rows], A["L1_gnn_rel_att"][k]).then_inc(s["load"], 16)
                        sp.dma_start(msg[rows, c, rows], A["L1_gnn_rel_msg"][k]).then_inc(s["load"], 16)
                        sp.dma_start(pri[rows, c:c + 1], A["L1_gnn_rel_pri"][k:k + 1].rearrange("(a d) -> a d", a=1)
                                     .to_broadcast([HEAD, 1]), allow_slow_non_contiguous=True).then_inc(s["load"], 16)
                    sp.dma_start(alpha[:], A["L1_gnn_skip"].rearrange("(a d) -> a d", a=1).to_broadcast([128, 1]),
                                 allow_slow_non_contiguous=True).then_inc(s["load"], 16)
                    sp.dma_start(self.Wm[:], A["L1_mix_W_qkv"].rearrange("(c p) n -> p c n", p=128)).then_inc(s["load"], 16)
                    sp.dma_start(self.Wmo[:, 0, :], A["L1_mix_W_out"]).then_inc(s["load"], 16)

                @block.vector
                def _(v):
                    v.memset(att[:], 0.0).then_inc(s["clear"], 1)
                    v.memset(msg[:], 0.0).then_inc(s["clear"], 1)
                    v.wait_ge(s["act"], 1)
                    v.tensor_scalar(alpha[:], alpha[:], 1.0, None, ALU.add).then_inc(s["v"], 1)
                    v.wait_ge(s["v"], 1)
                    v.reciprocal(alpha[:], alpha[:]).then_inc(s["v"], 1)
                    v.wait_ge(s["v"], 2)
                    v.tensor_scalar(self.keep_h[:], alpha[:], -1.0, 1.0, ALU.mult, ALU.add)
                    for c in range(HALVES):
                        v.tensor_scalar(gain[:, c, :], G["ident"][:], alpha[:], None, ALU.mult)
                        v.tensor_scalar(scale[:, c, :], G["ident"][:], pri[:, c:c + 1], HEAD ** -0.5, ALU.mult, ALU.mult)
                    v.wait_ge(s["turned"], 1)
                    v.tensor_copy(self.WqmT[:], tp[:, 0, 0:D])

                @block.scalar
                def _(act):
                    act.wait_ge(s["load"], 16 * (3 * heads + 3))
                    act.activation(alpha[:], alpha[:], ACT.Exp, scale=-1.0).then_inc(s["act"], 1)

                @block.tensor
                def _(pe):
                    pe.wait_ge(s["load"], 16 * (3 * heads + 3))
                    for c in range(HALVES):
                        mm = pe.transpose(tp[:, 0, c * 128:(c + 1) * 128], self.Wm[:, c, 0:MW], G["ident"][:])
                    mm.then_inc(s["turned"], 1)
            fold(nc, G, "l1_fold", [
                (A["L1_gnn_Wq"], A["L1_gnn_bq"], scale, self.WqT[:], self.bq[:]),
                (A["L1_gnn_Wk"], A["L1_gnn_bk"], att, self.WkT[:], self.bk[:]),
                (A["L1_gnn_Wv"], A["L1_gnn_bv"], msg, self.WvT[:], self.bv[:]),
                (A["L1_gnn_Wa"], A["L1_gnn_ba"], gain, self.WaT[:], self.ba[:])])


def project1(nc, G, L, Q, k_d, v_d, MK, MV, kmax):
    hold = G["hold"]
    k_v, v_v = (t.rearrange("(n t p) d -> n p t d", t=2, p=TP) for t in (k_d, v_d))
    sems = dict(q_ps=0, k_ps=0, v_ps=0, m_ps=2, q_read=1, k_read=1, v_read=1, m_read=1, kmax=0,
                out0=32, out1=32, **hT_sems())
    with phase(nc, "proj1", sems) as (block, s, sb, ps):
        h, hT = sb("h", [TP, 2, 2, D]), sb("hT", [128, 2, HALVES, PT])
        kv = sb("kv", [TP, 2, 2, 2, D])
        psT, qp, kp, vp, mp = ps("psT"), ps("q"), ps("k"), ps("v"), ps("m")

        def of_pair(bank):
            return bank[0:TP, 0].rearrange("p (t d) -> p t d", t=2)

        @block.sync
        def _(sp):
            def save(p, b):
                for n, (free, dst) in enumerate((("k_read", k_v), ("v_read", v_v))):
                    hold(sp, s[free], p + 2)
                    sp.dma_start(dst[bass.ds(p, 1)].rearrange("n p t d -> (n p) t d"), kv[:, b, n]).then_inc(s[f"out{b}"], 16)
            pairs(sp, save)
            sp.wait_ge(s["out0"], 32 * (PAIRS // 2 + 2))
            sp.wait_ge(s["out1"], 32 * (PAIRS // 2 + 1))

        @block.vector
        def _(v):
            v.memset(MV[:, :, :, MW:MW + 1], 1.0)
            v.memset(kmax[:], -BIG).then_inc(s["kmax"], 1)

            def main(p, b):
                v.wait_ge(s["q_ps"], p + 1)
                v.tensor_tensor(pair_of(Q, p), of_pair(qp), L.bq[:].unsqueeze(1).to_broadcast([TP, 2, D]), ALU.add
                                ).then_inc(s["q_read"], 1)
                v.wait_ge(s[f"out{b}"], 32 * (p // 2) + 32)
                for n, (bank, row, ready, read) in enumerate(((kp, L.bk, "k_ps", "k_read"), (vp, L.bv, "v_ps", "v_read"))):
                    v.wait_ge(s[ready], p + 1)
                    v.tensor_tensor(kv[:, b, n], of_pair(bank), row[:].unsqueeze(1).to_broadcast([TP, 2, D]), ALU.add
                                    ).then_inc(s[read], 1)
                v.wait_ge(s["m_read"], p + 2)
                v.wait_ge(s["kmax"], p + 1)
                v.tensor_tensor(kmax[:], kmax[:], pair_of(MK, p), ALU.max).then_inc(s["kmax"], 1)
            pairs(v, main, lambda p, b: normalise_pair(v, G, s, h, p, b))

        @block.scalar
        def _(act):
            def main(p, b):
                m = of_pair(mp)
                hold(act, s["m_ps"], p + 3)
                act.copy(pair_of(MK, p), m[:, :, 0:MW])
                act.copy(MV[:, bass.ds(2 * p, 2), 0, 0:MW], m[:, :, MW:2 * MW]).then_inc(s["m_read"], 1)
            pairs(act, main, lambda p, b: affine_evacuate(act, s, psT, hT, None, None, p, b, (s["m_ps"], p + 1)))

        @block.tensor
        def _(pe):
            def main(p, b):
                pe.wait_ge(s["hT_ready"], p + 2)
                for bank, w, cols, ready, read in ((qp, L.WqT, slice(0, D), "q_ps", "q_read"), (kp, L.WkT, slice(0, D), "k_ps", "k_read"),
                                                   (vp, L.WvT, slice(0, D), "v_ps", "v_read"),
                                                   (mp, L.Wm, slice(MW, 3 * MW), "m_ps", "m_read")):
                    pe.wait_ge(s[read], p + 1)
                    for t in range(2):
                        for c in range(HALVES):
                            mm = pe.matmul(bank[0:TP, 0, t * D:(t + 1) * D], hT[:, b, c, t * TP:(t + 1) * TP],
                                           w[:, c, cols], start=(c == 0), stop=(c == 1))
                    mm.then_inc(s[ready], 1)
            pairs(pe, main, lambda p, b: turn_pair(pe, G, s, h, psT, p, b))


H1 = D // HEAD
LIST = CHUNK_TILES * EP


def alternating(eng, n, main):
    with eng.Fori(0, n // 2) as j:
        for b in range(2):
            main(2 * j + b, b)
    main(n - 1, 0)


def edge_scores(nc, G, T, ring, Q, k_d, SC):
    hold = G["hold"]
    sems = dict(idx=0, clear=0, hot=0, hot_turned=4, hotT=2, q_ps=2, prod=RING, part=2, sum=2)
    with phase(nc, "scores", sems) as (block, s, sb, ps):
        idx = sb("idx", [EP, 2, RING], I32)
        rows = sb("rows", [EP, RING, D])
        hot, hotT = sb("hot", [EP, 4, TP]), sb("hotT", [TP, 2, EP])
        prod, part = sb("prod", [EP, 2, D]), sb("part", [EP, 2, H1])
        turned, qe = ps("turned", 2), ps("qe", 4)

        @block.gpsimd
        def _(pool):
            with pool.Fori(0, STEPS // UNROLL) as j:
                for u in range(UNROLL):
                    if u % RING == 0:
                        hold(pool, s["idx"], 2 * j + u // RING + 1)
                    hold(pool, s["prod"], UNROLL * j + u + 1)
                    pool.indirect_dma_start(rows[:, u % RING, :], None, k_d,
                                            bass.IndirectOffsetOnAxis(ap=idx[:, u // RING, u % RING:u % RING + 1], axis=0)
                                            ).then_inc(ring[u % RING], 16)

        @block.scalar
        def _(act):
            def evacuate(step, slot):
                act.wait_ge(s["hot_turned"], step + 5)
                act.wait_ge(s["q_ps"], step + 1)
                act.copy(hotT[:, slot, :], turned[0:TP, slot, 0:EP]).then_inc(s["hotT"], 1)

            with act.Fori(0, STEPS // UNROLL) as j:
                for u in range(UNROLL):
                    if u % RING == 0:
                        hold(act, s["prod"], UNROLL * j + u + 1)
                        act.copy(idx[:, u // RING, :], T["src"][:, bass.ds(UNROLL * j + u, RING)]).then_inc(s["idx"], 1)
                    evacuate(UNROLL * j + u, u % 2)

        @block.tensor
        def _(pe):
            def turn(step, u):
                pe.wait_ge(s["hot"], step + 1)
                pe.wait_ge(s["hotT"], step + 1)
                pe.transpose(turned[0:TP, u % 2, 0:EP], hot[:, u % 4, :], G["ident"][:]).then_inc(s["hot_turned"], 1)

            turn(0, 0)
            turn(1, 1)
            with pe.Fori(0, STEPS // UNROLL) as j:
                for u in range(UNROLL):
                    step = UNROLL * j + u
                    turn(step + 2, u + 2)
                    n = pe.value_load(T["n"][0:1, bass.ds(step, 1)], min_val=0, max_val=NT - 1)
                    pe.wait_ge(s["hotT"], step + 3)
                    pe.wait_ge(s["prod"], step + RING - 3)
                    pe.matmul(qe[:, u % 4, 0:D], hotT[:, u % 2, :], tile_of(Q, n), start=True, stop=True
                              ).then_inc(s["q_ps"], 1)

        @block.vector
        def _(v):
            v.memset(SC[:], 0.0).then_inc(s["clear"], 1)
            v.wait_ge(s["clear"], 1)

            def one_hot(step, slot):
                v.wait_ge(s["hot_turned"], step + 1)
                v.tensor_scalar(hot[:, slot, :], T["nodes"][:], T["rel"][:, bass.ds(step, 1)], None,
                                ALU.is_equal).then_inc(s["hot"], 1)

            def product(step, u, j):
                v.wait_ge(ring[u % RING], 32 * j + 16 * (u // RING) + 16)
                v.wait_ge(s["q_ps"], step + 3)
                v.wait_ge(s["part"], step + 1)
                v.tensor_tensor(prod[:, u % 2, :], rows[:, u % RING, :], qe[:, u % 4, 0:D], ALU.mult
                                ).then_inc(s["prod"], 1)

            def reduce_heads(step, b):
                v.wait_ge(s["prod"], step + 1 + RING)
                hold(v, s["sum"], step + 1)
                v.tensor_reduce(part[:, b, :], prod[:, b, :].rearrange("p (h e) -> p h e", e=HEAD),
                                X_AXIS, ALU.add).then_inc(s["part"], 1)

            def add(step, b):
                e = v.value_load(T["e"][0:1, bass.ds(step, 1)], min_val=0, max_val=ETILES - 1)
                score = tile_of(SC, e)
                v.wait_ge(s["part"], step + 3)
                v.wait_ge(s["sum"], step + 2)
                v.tensor_tensor(score, score, part[:, b, :], ALU.add).then_inc(s["sum"], 1)

            def steps(j):
                for u in range(UNROLL):
                    step, later = UNROLL * j + u, not isinstance(j, int)
                    one_hot(step + HOT_AHEAD, (u + HOT_AHEAD) % 4)
                    product(step, u, j)
                    if u >= 1 or later:
                        reduce_heads(step - 1, (u - 1) % 2)
                    if u >= 2 or later:
                        add(step - 2, u % 2)

            for k in range(HOT_AHEAD):
                one_hot(k, k)
            blocks_of_steps(v, steps)
            add(STEPS - 2, 0)
            reduce_heads(STEPS - 1, 1)
            add(STEPS - 1, 1)


def edge_softmax(nc, G, SC):
    hold, ident = G["hold"], G["ident"]
    last = LIST - 1
    SCv = SC[:].rearrange("p (c b) h -> p c b h", c=CHUNKS)
    rows_of = G["dst_tiles"].rearrange("(c r) e -> c (r e)", c=CHUNKS)
    sems = dict(dst=0, pen=0, tile=2, turned=2, put=2, scan=0, row=0, back=2, mturned=2, sub=2, done=0)
    with phase(nc, "segmax", sems) as (block, s, sb, ps):
        dst = sb("dst", [128, LIST], I32)
        pen = sb("pen", [128, LIST + 1])
        ST = sb("ST", [128, LIST])
        sct, mt = sb("sct", [EP, 2, 128]), sb("mt", [128, 2, EP])
        ends = sb("ends", [128, 4])
        er, pr = sb("er", [1, 4, CHUNKS, H1]), sb("pr", [1, 4, H1, CHUNKS])
        same, whole, join = sb("same", [1, H1, CHUNKS]), sb("whole", [1, H1, CHUNKS]), sb("join", [1, H1, CHUNKS])
        pf, pb = sb("pf", [1, H1, CHUNKS]), sb("pb", [1, H1, CHUNKS])
        xf, xb = sb("xf", [1, H1, CHUNKS]), sb("xb", [1, H1, CHUNKS])
        cf, cb = sb("cf", [1, H1, CHUNKS]), sb("cb", [1, H1, CHUNKS])
        carry_row, carry = sb("carry_row", [1, 2, CHUNKS, H1]), sb("carry", [128, 2])
        psS, psM, psR = ps("S", 2), ps("M", 2), ps("R")

        @block.sync
        def _(sp):
            for c in range(CHUNKS):
                sp.dma_start(dst[c * H1:(c + 1) * H1, :], rows_of[c:c + 1, :].to_broadcast([H1, LIST])).then_inc(s["dst"], 16)

        @block.scalar
        def _(act):
            def take(k, b):
                hold(act, s["turned"], k + 1)
                act.copy(sct[:, b, :].rearrange("p (c h) -> p c h", h=H1),
                         SCv[:, :, bass.ds(k, 1), :].rearrange("p c b h -> p c (b h)")).then_inc(s["tile"], 1)
            alternating(act, CHUNK_TILES, take)
            act.wait_ge(s["scan"], 4)

            def back(k, b):
                hold(act, s["mturned"], k + 1)
                act.copy(mt[:, b, :], ST[:, bass.ds(k * EP, EP)]).then_inc(s["back"], 1)
            alternating(act, CHUNK_TILES, back)
            act.wait_ge(s["sub"], 2 + CHUNK_TILES)
            act.activation(SC[:], SC[:], ACT.Exp).then_inc(s["done"], 1)

        @block.tensor
        def _(pe):
            def turn(k, b):
                pe.wait_ge(s["tile"], k + 3)
                pe.wait_ge(s["put"], k + 1)
                pe.transpose(psS[:, b, 0:128], sct[:, b, :], ident[:]).then_inc(s["turned"], 1)
            alternating(pe, CHUNK_TILES, turn)
            pe.wait_ge(s["row"], 1)
            for k in range(4):
                mm = pe.matmul(psR[0:1, 0, k * 128:(k + 1) * 128], ends[:, k:k + 1], ident[:], start=True, stop=True)
            mm.then_inc(s["row"], 1)
            pe.wait_ge(s["row"], 4)
            for k in range(2):
                mm = pe.matmul(psR[:, 0, k:k + 1], carry_row[:, k].rearrange("a c h -> a (c h)"), G["ones"][0:1, 0:1],
                               start=True, stop=True)
            mm.then_inc(s["row"], 1)

            def turn_back(k, b):
                pe.wait_ge(s["back"], k + 3)
                pe.wait_ge(s["sub"], k + 1)
                pe.transpose(psM[:, b, 0:EP], mt[:, b, :], ident[:]).then_inc(s["mturned"], 1)
            alternating(pe, CHUNK_TILES, turn_back)

        @block.vector
        def _(v):
            count = [0]

            def link(ins):
                count[0] += 1
                ins.then_inc(s["pen"], 1)
                v.wait_ge(s["pen"], count[0])

            v.wait_ge(s["dst"], 16 * CHUNKS)
            v.memset(pen[:, 0:1], 0.0)
            v.memset(pen[:, LIST:LIST + 1], 0.0)
            v.tensor_copy(ends[:, 2:3], dst[:, 0:1])
            v.tensor_copy(ends[:, 3:4], dst[:, last:last + 1])
            link(v.tensor_tensor(pen[:, 1:LIST], dst[:, 1:LIST], dst[:, 0:last], ALU.is_equal))
            link(v.tensor_scalar(pen[:, 1:LIST], pen[:, 1:LIST], -1.0, BIG, ALU.add, ALU.mult))

            def put(k, b):
                hold(v, s["turned"], k + 3)
                v.tensor_copy(ST[:, bass.ds(k * EP, EP)], psS[:, b, 0:128]).then_inc(s["put"], 1)
            alternating(v, CHUNK_TILES, put)
            v.wait_ge(s["put"], 2 + CHUNK_TILES)

            def scan(first, second):
                v.tensor_tensor_scan(ST[:], pen[:, 0:LIST], ST[:], first, ALU.add, ALU.max).then_inc(s["scan"], 1)
                v.wait_ge(s["scan"], 1 if isinstance(first, float) else 3)
                v.tensor_tensor_scan(ST[:, ::-1], pen[:, LIST:0:-1], ST[:, ::-1], second, ALU.add, ALU.max
                                     ).then_inc(s["scan"], 1)
                v.wait_ge(s["scan"], 2 if isinstance(first, float) else 4)

            scan(-BIG, -BIG)
            v.tensor_copy(ends[:, 0:1], ST[:, last:last + 1])
            v.tensor_copy(ends[:, 1:2], ST[:, 0:1]).then_inc(s["row"], 1)
            v.wait_ge(s["row"], 2)
            link(v.tensor_copy(er[:].rearrange("a k c h -> a (k c h)"), psR[0:1, 0, :]))
            link(v.tensor_copy(pr[:], er[:].rearrange("a k c h -> a k h c")))
            a, f, d0, d1 = (pr[:, k] for k in range(4))
            C1 = CHUNKS - 1
            v.memset(same[:, :, 0:1], 0.0)
            link(v.tensor_tensor(same[:, :, 1:CHUNKS], d0[:, :, 1:CHUNKS], d1[:, :, 0:C1], ALU.is_equal))
            link(v.tensor_tensor(whole[:], d0, d1, ALU.is_equal))
            link(v.tensor_tensor(pf[:], whole[:], same[:], ALU.mult))
            v.memset(pb[:, :, C1:CHUNKS], 0.0)
            link(v.tensor_tensor(pb[:, :, 0:C1], whole[:, :, 0:C1], same[:, :, 1:CHUNKS], ALU.mult))
            for t in (pf, pb):
                link(v.tensor_scalar(t[:], t[:], -1.0, BIG, ALU.add, ALU.mult))
            link(v.tensor_scalar(join[:], same[:], -1.0, BIG, ALU.add, ALU.mult))

            def flat(t):
                return t[:].rearrange("a h c -> a (h c)")
            link(v.tensor_tensor_scan(flat(xf), flat(pf), a.rearrange("a h c -> a (h c)"), -BIG, ALU.add, ALU.max))
            link(v.tensor_tensor_scan(flat(xb)[:, ::-1], flat(pb)[:, ::-1], f.rearrange("a h c -> a (h c)")[:, ::-1],
                                      -BIG, ALU.add, ALU.max))
            v.memset(cf[:, :, 0:1], -BIG)
            v.memset(cb[:, :, C1:CHUNKS], -BIG)
            link(v.tensor_tensor(cf[:, :, 1:CHUNKS], xf[:, :, 0:C1], join[:, :, 1:CHUNKS], ALU.add))
            link(v.tensor_tensor(cb[:, :, 0:C1], xb[:, :, 1:CHUNKS], join[:, :, 1:CHUNKS], ALU.add))
            v.tensor_copy(carry_row[:, 0], cf[:].rearrange("a h c -> a c h")).then_inc(s["row"], 1)
            v.tensor_copy(carry_row[:, 1], cb[:].rearrange("a h c -> a c h")).then_inc(s["row"], 1)
            v.wait_ge(s["row"], 5)
            link(v.tensor_copy(carry[:], psR[:, 0, 0:2]))
            scan(carry[:, 0:1], carry[:, 1:2])

            def subtract(k, b):
                hold(v, s["mturned"], k + 3)
                part = SCv[:, :, bass.ds(k, 1), :].rearrange("p c b h -> p c (b h)")
                v.tensor_tensor(part, part, psM[:, b, 0:128].rearrange("p (c h) -> p c h", h=H1), ALU.subtract
                                ).then_inc(s["sub"], 1)
            alternating(v, CHUNK_TILES, subtract)


def combine1(nc, G, L, acc):
    A, hold, X = G["A"], G["hold"], G["X"]
    sems = dict(load=0, both=0, z=0, t_ready=0, t_turned=2, tT=2, o=2, x_done=2, biased=2, kept=0, stats_step=1, **hT_sems())
    with phase(nc, "comb1", sems) as (block, s, sb, ps):
        h, hT = sb("h", [TP, 2, 2, D]), sb("hT", [128, 2, HALVES, PT])
        t, tT = sb("t", [TP, 2, 2, D]), sb("tT", [128, 2, HALVES, PT])
        zinv, bb, hk = sb("zinv", [TP, NT, H1]), sb("bb", [TP, D]), sb("hk", [TP, 2, D])
        st = sb("st", [TP, 2, 8])
        psT, psA, o = ps("psT"), ps("psA"), ps("o", 2)

        @block.sync
        def _(sp):
            sp.dma_start(bb[:], row_of(A["L1_mix_b_out"], D)).then_inc(s["load"], 16)

        @block.gpsimd
        def _(pool):
            pool.wait_ge(s["load"], 16)
            pool.tensor_tensor(bb[:], bb[:], L.ba[:], ALU.add).then_inc(s["both"], 1)
            pool.wait_ge(s["both"], 1)

            def keep(p, b):
                Xp = pair_of(X, p)
                hold(pool, s["h_ready"], 2 * p + 2)
                pool.tensor_scalar(hk[:], h[:, b], L.keep_h[0:TP, :], None, ALU.mult).then_inc(s["kept"], 1)
                hold(pool, s["kept"], 2 * p + 1)
                pool.tensor_tensor(Xp, Xp, hk[:], ALU.add).then_inc(s["kept"], 1)
                hold(pool, s["kept"], 2 * p + 2)
                pool.tensor_tensor(Xp, Xp, bb[:].unsqueeze(1).to_broadcast([TP, 2, D]), ALU.add).then_inc(s["biased"], 1)
            pairs(pool, keep)

        @block.vector
        def _(v):
            v.tensor_scalar(zinv[:], acc[:, :, D:D + H1], 0.5, None, ALU.max).then_inc(s["z"], 1)
            v.wait_ge(s["z"], 1)
            v.reciprocal(zinv[:], zinv[:]).then_inc(s["z"], 1)
            v.wait_ge(s["z"], 2)

            def ahead(p, b):
                v.wait_ge(s["biased"], p + 1)
                normalise_pair(v, G, s, h, p, b)
                v.wait_ge(s["t_turned"], p + 1)
                v.tensor_tensor(t[:, b].rearrange("p t (h e) -> p t h e", e=HEAD),
                                acc[:, bass.ds(2 * p, 2), 0:D].rearrange("p t (h e) -> p t h e", e=HEAD),
                                zinv[:, bass.ds(2 * p, 2), :].unsqueeze(3).to_broadcast([TP, 2, H1, HEAD]),
                                ALU.mult).then_inc(s["t_ready"], 1)

            def add(p, b):
                v.wait_ge(s["biased"], p + 3)
                add_and_stats(v, G, s, st, o[0:TP, b].rearrange("p (t d) -> p t d", t=2), p, 2)
            pairs(v, add, ahead)

        @block.scalar
        def _(act):
            def evacuate(p, b):
                affine_evacuate(act, s, psT, hT, None, None, p, b, (s["o"], p + 1))
                act.wait_ge(s["t_turned"], p + 3)
                act.copy(tT[:, b], psA[:, 0, 0:2 * PT].rearrange("p (c t) -> p c t", c=HALVES)).then_inc(s["tT"], 1)
            pairs(act, evacuate)

        @block.tensor
        def _(pe):
            def ahead(p, b):
                turn_pair(pe, G, s, h, psT, p, b)
                pe.wait_ge(s["t_ready"], p + 1)
                pe.wait_ge(s["tT"], p + 2)
                for c in range(HALVES):
                    for k in range(2):
                        mm = pe.transpose(psA[:, 0, c * 250 + k * TP:c * 250 + (k + 1) * TP],
                                          t[:, b, k, c * 128:(c + 1) * 128], G["ident"][0:TP, 0:TP])
                mm.then_inc(s["t_turned"], 1)

            def main(p, b):
                pe.wait_ge(s["hT_ready"], p + 2)
                pe.wait_ge(s["tT"], p + 3)
                pe.wait_ge(s["x_done"], p + 1)
                for k in range(2):
                    for n, (src, w) in enumerate(((hT, L.Gm), (tT, L.WaT))):
                        for c in range(HALVES):
                            mm = pe.matmul(o[0:TP, b, k * D:(k + 1) * D], src[:, b, c, k * TP:(k + 1) * TP], w[:, c, :],
                                           start=(n + c == 0), stop=(n + c == 2))
                mm.then_inc(s["o"], 1)
            pairs(pe, main, ahead)


def layer1(nc, G, T):
    dram = G["dram"]
    k_d, v_d = dram("k1_d", [NODES, D]), dram("v1_d", [NODES, D])
    rings = [[G["semaphore"](f"ring{m}_{n}") for n in range(RING)] for m in range(2)]
    with ExitStack() as ctx:
        L = Layer1(nc, G, ctx)
        buf = ctx.enter_context(nc.sbuf_tensor("MK_SC", [EP, NT * MW], F32))
        MK = buf[0:TP, :].rearrange("p (t d) -> p t d", d=MW)
        SC = buf[:, 0:ETILES * H1].rearrange("p (t h) -> p t h", h=H1)
        with nc.sbuf_tensor("Q", [TP, NT, D], F32) as Q:
            with ExitStack() as kv:
                MV = kv.enter_context(nc.sbuf_tensor("MV", [TP, NT, 1, MW + 1], F32))
                kmax = kv.enter_context(nc.sbuf_tensor("kmax1", [TP, 2, MW], F32))
                Cp = kv.enter_context(nc.sbuf_tensor("Cp1", [128, 1, D], F32))
                project1(nc, G, L, Q, k_d, v_d, MK, MV, kmax)
                context(nc, G, "ctx1", 1, MK, MV, kmax, 1.0, L.Wmo, Cp, (L.WqmT, HEAD ** -0.5, L.Gm))
            edge_scores(nc, G, T, rings[0], Q, k_d, SC)
        edge_softmax(nc, G, SC)
        acc = ctx.enter_context(nc.sbuf_tensor("acc1", [TP, NT, D + H1], F32))
        edge_sum(nc, G, "sum1", T, rings[1], v_d, acc, H1, weights=SC)
        combine1(nc, G, L, acc)


SH, SD, SG = 8, 64, 64
SI = SH * SD
SJ = SI // 128


def slice_attention(nc, G):
    A = G["A"]
    with ExitStack() as ctx:
        def keep(n, shape):
            return ctx.enter_context(nc.sbuf_tensor("sl_" + n, shape, F32))
        W = keep("W", [TP, NT, SI])
        fold_out = keep("fold", [128, SJ, D])
        with ExitStack() as mid:
            def part(n, shape):
                return mid.enter_context(nc.sbuf_tensor("sl_" + n, shape, F32))
            tokens, norms = part("tokens", [128, SJ, 128]), part("norms", [TP, SI])
            with ExitStack() as w:
                Wxs = w.enter_context(nc.sbuf_tensor("sl_Wxs", [128, HALVES, SI], F32))
                bxs = w.enter_context(nc.sbuf_tensor("sl_bxs", [TP, SI], F32))
                slice_weights_prep(nc, G, Wxs, bxs)
                slice_assign(nc, G, Wxs, bxs, W, tokens, norms)
            slice_mix(nc, G, tokens, norms, fold_out)
        slice_out(nc, G, W, fold_out)


def slice_weights_prep(nc, G, Wxs, bxs):
    A, ident = G["A"], G["ident"]
    loads = 6 + SH
    with phase(nc, "slprep", dict(clear=0, load=0, v=0, turned=0, ps=0)) as (block, s, sb, ps):
        Wx, WxT = sb("Wx", [128, HALVES, SI]), sb("WxT", [128, SJ, D])
        WS, R = sb("WS", [128, 128]), sb("R", [128, SJ, 128])
        bx, bs, tinv = sb("bx", [128, SJ]), sb("bs", [128, 1]), sb("tinv", [128, SJ])
        dg = sb("dg", [128, SJ, 128])
        bb, sp_bs = sb("bb", [128, SJ, TP]), sb("sbs", [128, TP])
        tp, wp, bp = ps("tp", 2), ps("wp", 2), ps("bp")

        @block.sync
        def _(sp):
            sp.wait_ge(s["clear"], 1)
            n = 0
            both = [(WS[k * 64:(k + 1) * 64, k * 64:(k + 1) * 64], A["L1_ffn_W_slice"]) for k in range(2)]
            both += [(bs[k * 64:(k + 1) * 64, :], A["L1_ffn_b_slice"].rearrange("(g a) -> g a", a=1)) for k in range(2)]
            both += [(Wx[:], A["L1_ffn_W_x"].rearrange("(c p) n -> p c n", p=128)),
                     (bx[:], A["L1_ffn_b_x"].rearrange("(j p) -> p j", p=128))]
            temp = A["L1_ffn_temperature"].rearrange("a h b c -> a (h b c)")
            both += [(tinv[k % 2 * 64:(k % 2 + 1) * 64, k // 2:k // 2 + 1], temp[0:1, k:k + 1].to_broadcast([64, 1]))
                     for k in range(SH)]
            for dst, src in both:
                sp.dma_start(dst, src, allow_slow_non_contiguous=True).then_inc(s["load"], 16)
                n += 1
            assert n == loads

        @block.vector
        def _(v):
            count = [0]

            def link(ins):
                count[0] += 1
                ins.then_inc(s["v"], 1)
                v.wait_ge(s["v"], count[0])

            v.memset(WS[:], 0.0).then_inc(s["clear"], 1)
            v.wait_ge(s["load"], 16 * (loads))
            link(v.tensor_scalar(tinv[:], tinv[:], 0.1, 5.0, ALU.max, ALU.min))
            link(v.reciprocal(tinv[:], tinv[:]))
            for j in range(SJ):
                v.tensor_scalar(R[:, j, :], WS[:], tinv[:, j:j + 1], None, ALU.mult)
                v.tensor_scalar(dg[:, j, :], ident[:], tinv[:, j:j + 1], None, ALU.mult)
                v.tensor_scalar(bb[:, j, :], G["ones"][:, 0:TP], bx[:, j:j + 1], None, ALU.mult)
            link(v.tensor_scalar(sp_bs[:], G["ones"][:, 0:TP], bs[:], None, ALU.mult))
            v.wait_ge(s["turned"], 1)
            link(v.tensor_copy(WxT[:].rearrange("p (a j) i -> p a (j i)", a=2), tp[:]))
            v.wait_ge(s["ps"], 1)
            v.tensor_copy(Wxs[:], wp[:])
            v.tensor_copy(bxs[:], bp[0:TP, 0, :])

        @block.tensor
        def _(pe):
            pe.wait_ge(s["load"], 16 * (loads))
            for j in range(SJ):
                for c in range(HALVES):
                    at = j % 2 * D + c * 128
                    mm = pe.transpose(tp[:, j // 2, at:at + 128], Wx[:, c, j * 128:(j + 1) * 128], ident[:])
            mm.then_inc(s["turned"], 1)
            pe.wait_ge(s["v"], 4)
            for j in range(SJ):
                cols = slice(j * 128, (j + 1) * 128)
                for c in range(HALVES):
                    pe.matmul(wp[:, c, cols], WxT[:, j, c * 128:(c + 1) * 128], R[:, j, :], start=True, stop=True)
                pe.matmul(bp[0:TP, 0, cols], bb[:, j, :], R[:, j, :], start=True, stop=False)
                mm = pe.matmul(bp[0:TP, 0, cols], sp_bs[:], dg[:, j, :], start=False, stop=True)
            mm.then_inc(s["ps"], 1)


def slice_assign(nc, G, Wxs, bxs, W, tokens, norms):
    A, hold, X = G["A"], G["hold"], G["X"]
    sems = dict(load=0, lg_ps=0, lg_read=2, fx_ps=4, fx_sb=2, small=0, sub=0, exp=0, w=2, norm=1, sliced=2, init=0,
                done=0, **hT_sems())
    with phase(nc, "slassign", sems) as (block, s, sb, ps):
        Wfx = sb("Wfx", [128, HALVES, SI])
        h, hT = sb("h", [TP, 2, 2, D]), sb("hT", [128, 2, HALVES, PT])
        lg = sb("lg", [TP, 2, SI])
        fx = sb("fx", [TP, 2, 2, SI])
        m, z = sb("m", [TP, 2, SH]), sb("z", [TP, 2, SH])
        psT, lp, fp, tk = ps("psT"), ps("lp", 2), ps("fp", 2), ps("tk")

        @block.sync
        def _(sp):
            sp.dma_start(Wfx[:], A["L1_ffn_W_fx"].rearrange("(c p) n -> p c n", p=128)).then_inc(s["load"], 16)

        @block.vector
        def _(v):
            v.memset(norms[:], 0.0).then_inc(s["init"], 1)

            def heads(t):
                return t.rearrange("p (h g) -> p h g", g=SG)

            def main(p, b):
                for t in range(2):
                    q = 2 * p + t
                    v.wait_ge(s["lg_ps"], q + 1)
                    v.wait_ge(s["w"], q + 1)
                    v.tensor_tensor(lg[:, t, :], lp[0:TP, t, :], bxs[:], ALU.add).then_inc(s["lg_read"], 1)
                    v.wait_ge(s["lg_read"], q + 3)
                    v.tensor_reduce(m[:, t, :], heads(lg[:, t, :]), X_AXIS, ALU.max).then_inc(s["small"], 1)
                    v.wait_ge(s["small"], 6 * p + 1 + t)
                    v.tensor_tensor(heads(lg[:, t, :]), heads(lg[:, t, :]), m[:, t, :].unsqueeze(2).to_broadcast([TP, SH, SG]),
                                    ALU.subtract).then_inc(s["sub"], 1)
                for t in range(2):
                    q = 2 * p + t
                    v.wait_ge(s["exp"], q + 1)
                    v.tensor_reduce(z[:, t, :], heads(lg[:, t, :]), X_AXIS, ALU.add).then_inc(s["small"], 1)
                    v.wait_ge(s["small"], 6 * p + 3 + 2 * t)
                    v.reciprocal(z[:, t, :], z[:, t, :]).then_inc(s["small"], 1)
            pairs(v, main, lambda p, b: normalise_pair(v, G, s, h, p, b))
            v.wait_ge(s["done"], 1)
            v.tensor_copy(tokens[:], tk[:, 0, :].rearrange("p (j g) -> p j g", j=SJ))

        @block.gpsimd
        def _(pool):
            pool.wait_ge(s["init"], 1)

            def divide(p, b):
                for t in range(2):
                    q = 2 * p + t
                    hold(pool, s["small"], 6 * p + 4 + 2 * t)
                    wq = tile_of(W, q)
                    pool.tensor_tensor(wq.rearrange("p (h g) -> p h g", g=SG),
                                       lg[:, t, :].rearrange("p (h g) -> p h g", g=SG),
                                       z[:, t, :].unsqueeze(2).to_broadcast([TP, SH, SG]), ALU.mult).then_inc(s["w"], 1)
                    hold(pool, s["w"], q + 3)
                    hold(pool, s["norm"], q + 1)
                    pool.tensor_tensor(norms[:], norms[:], wq, ALU.add).then_inc(s["norm"], 1)
            pairs(pool, divide)

        @block.scalar
        def _(act):
            def main(p, b):
                for t in range(2):
                    q = 2 * p + t
                    act.wait_ge(s["sub"], q + 1)
                    act.activation(lg[:, t, :], lg[:, t, :], ACT.Exp).then_inc(s["exp"], 1)
                    act.wait_ge(s["fx_ps"], q + 5)
                    act.wait_ge(s["sliced"], p + 1)
                    act.copy(fx[:, b, t, :], fp[0:TP, t, :]).then_inc(s["fx_sb"], 1)
            pairs(act, main, lambda p, b: affine_evacuate(act, s, psT, hT, None, None, p, b, (s["fx_ps"], 2 * p + 2)))

        @block.tensor
        def _(pe):
            pe.wait_ge(s["load"], 16)
            pe.matmul(tk[:, 0, :], G["zeros"][:, 0:128], Wxs[:, 0, :], start=True, stop=False, skip_group_check=True)

            def project(p, b):
                pe.wait_ge(s["hT_ready"], p + 2)
                for t in range(2):
                    for bank, w, free, ready in ((lp, Wxs, "lg_read", "lg_ps"), (fp, Wfx, "fx_sb", "fx_ps")):
                        pe.wait_ge(s[free], 2 * p + t + 1)
                        for c in range(HALVES):
                            mm = pe.matmul(bank[0:TP, t, :], hT[:, b, c, t * TP:(t + 1) * TP], w[:, c, :],
                                           start=(c == 0), stop=(c == 1))
                        mm.then_inc(s[ready], 1)

            def ahead(p, b):
                turn_pair(pe, G, s, h, psT, p, b)
                project(p, b)

            def sums(p, b):
                pe.wait_ge(s["w"], 2 * p + 4)
                pe.wait_ge(s["fx_sb"], 2 * p + 4)
                for t in range(2):
                    for j in range(SJ):
                        mm = pe.matmul(tk[:, 0, j * 128:(j + 1) * 128], fx[:, b, t, j * 128:(j + 1) * 128],
                                       W[:, bass.ds(2 * p + t, 1), j * 128:(j + 1) * 128].rearrange("p a g -> p (a g)"),
                                       start=False, stop=(isinstance(p, int) and t == 1), skip_group_check=True)
                mm.then_inc(s["sliced"], 1)
            pairs(pe, sums, ahead)
            pe.wait_ge(s["sliced"], PAIRS + 2)
            pe.sem_inc(s["done"], 1)


def slice_mix(nc, G, tokens, norms, fold_out):
    A, ident = G["A"], G["ident"]
    with phase(nc, "slmix", dict(clear=0, load=0, v=0, a=0, p=0)) as (block, s, sb, ps):
        Wq, Wk, Wv = (sb(n, [128, 128]) for n in ("Wq", "Wk", "Wv"))
        Wo, bfx = sb("Wo", [128, SJ, D]), sb("bfx", [128, SJ])
        n1, n2 = sb("n1", [128, SJ, 128]), sb("n2", [128, SJ, 128])
        tok = sb("tok", [128, SJ, 128])
        qT, kT, vv = sb("qT", [128, SI]), sb("kT", [128, SI]), sb("vv", [128, SJ, 128])
        at, ab = sb("at", [128, SJ, SG]), sb("ab", [128, SJ, 128])
        abT, osT = sb("abT", [128, SJ, 128]), sb("osT", [128, SJ, 128])
        m, z = sb("m", [128, SJ]), sb("z", [128, SJ])
        p0, p1, p2, p3 = ps("p0"), ps("p1"), ps("p2"), ps("p3", 2)

        def blocks(bank):
            return bank[:, 0, :].rearrange("p (j g) -> p j g", j=SJ)

        @block.sync
        def _(sp):
            sp.wait_ge(s["clear"], 1)
            loads = [(w[k * 64:(k + 1) * 64, k * 64:(k + 1) * 64], A[n]) for w, n in
                     ((Wq, "L1_ffn_W_q"), (Wk, "L1_ffn_W_k"), (Wv, "L1_ffn_W_v")) for k in range(2)]
            loads += [(Wo[:], A["L1_ffn_W_out"].rearrange("(j p) d -> p j d", p=128)),
                      (bfx[:], A["L1_ffn_b_fx"].rearrange("(j p) -> p j", p=128))]
            for dst, src in loads:
                sp.dma_start(dst, src, allow_slow_non_contiguous=True).then_inc(s["load"], 16)

        @block.vector
        def _(v):
            count = [0]

            def link(ins):
                count[0] += 1
                ins.then_inc(s["v"], 1)
                v.wait_ge(s["v"], count[0])

            def each(t):
                return t[:].unsqueeze(2).to_broadcast([128, SJ, SG])

            v.memset(ab[:], 0.0)
            v.memset(Wq[:], 0.0)
            v.memset(Wk[:], 0.0)
            v.memset(Wv[:], 0.0).then_inc(s["clear"], 1)
            v.wait_ge(s["clear"], 1)
            v.wait_ge(s["load"], 16 * 8)
            v.wait_ge(s["p"], 1)
            link(v.tensor_copy(n1[:], blocks(p0)))
            link(v.tensor_scalar(n2[:], n1[:], 1e-5, None, ALU.add))
            link(v.reciprocal(n2[:], n2[:]))
            for j in range(SJ):
                d = v.scalar_tensor_tensor(out=tok[:, j, :], in0=n1[:, j, :], scalar=bfx[:, j:j + 1],
                                           in1=tokens[:, j, :], op0=ALU.mult, op1=ALU.add)
            link(d)
            link(v.tensor_tensor(tok[:], tok[:], n2[:], ALU.mult))
            link(v.tensor_tensor(tok[:], tok[:], G["mask64"][:].unsqueeze(1).to_broadcast([128, SJ, 128]), ALU.mult))
            v.wait_ge(s["p"], 2)
            v.tensor_copy(qT[:], p0[:, 0, :])
            v.tensor_copy(kT[:], p1[:, 0, :])
            link(v.tensor_copy(vv[:], blocks(p2)))
            v.wait_ge(s["p"], 3)
            for k in range(2):
                rows = slice(64 * k, 64 * k + 64)
                d = v.tensor_scalar(at[rows], blocks(p0)[rows, :, rows], SD ** -0.5, None, ALU.mult)
            link(d)
            link(v.tensor_reduce(m[:], at[:], X_AXIS, ALU.max))
            link(v.tensor_tensor(at[:], at[:], each(m), ALU.subtract))
            v.wait_ge(s["a"], 1)
            link(v.tensor_reduce(z[:], at[:], X_AXIS, ALU.add))
            link(v.reciprocal(z[:], z[:]))
            for k in range(2):
                rows = slice(64 * k, 64 * k + 64)
                d = v.tensor_tensor(ab[rows, :, rows], at[rows], z[rows].unsqueeze(2).to_broadcast([64, SJ, SG]), ALU.mult)
            link(d)
            v.wait_ge(s["p"], 4)
            link(v.tensor_copy(abT[:], blocks(p1)))
            v.wait_ge(s["p"], 5)
            link(v.tensor_copy(osT[:], blocks(p2)))
            v.wait_ge(s["p"], 6)
            v.tensor_copy(fold_out[:].rearrange("p (a j) d -> p a (j d)", a=2), p3[:])

        @block.scalar
        def _(act):
            act.wait_ge(s["v"], 10)
            act.activation(at[:], at[:], ACT.Exp).then_inc(s["a"], 1)

        @block.tensor
        def _(pe):
            pe.matmul(p0[:, 0, :], G["ones"][0:TP, :], norms[:], start=True, stop=True).then_inc(s["p"], 1)
            pe.wait_ge(s["v"], 6)
            pe.matmul(p0[:, 0, :], Wq[:], tok[:].rearrange("p j g -> p (j g)"), start=True, stop=True)
            pe.matmul(p1[:, 0, :], Wk[:], tok[:].rearrange("p j g -> p (j g)"), start=True, stop=True)
            for j in range(SJ):
                mm = pe.matmul(blocks(p2)[:, j, :], tok[:, j, :], Wv[:], start=True, stop=True)
            mm.then_inc(s["p"], 1)
            pe.wait_ge(s["v"], 7)
            for j in range(SJ):
                cols = slice(j * 128, (j + 1) * 128)
                mm = pe.matmul(blocks(p0)[:, j, :], qT[:, cols], kT[:, cols], start=True, stop=True)
            mm.then_inc(s["p"], 1)
            pe.wait_ge(s["v"], 13)
            for j in range(SJ):
                mm = pe.transpose(blocks(p1)[:, j, :], ab[:, j, :], ident[:])
            mm.then_inc(s["p"], 1)
            pe.wait_ge(s["v"], 14)
            for j in range(SJ):
                mm = pe.matmul(blocks(p2)[:, j, :], vv[:, j, :], abT[:, j, :], start=True, stop=True)
            mm.then_inc(s["p"], 1)
            pe.wait_ge(s["v"], 15)
            for j in range(SJ):
                mm = pe.matmul(p3[:, j // 2, j % 2 * D:(j % 2 + 1) * D], osT[:, j, :], Wo[:, j, :], start=True, stop=True)
            mm.then_inc(s["p"], 1)


def slice_out(nc, G, W, fold_out):
    A, hold, X = G["A"], G["hold"], G["X"]
    out_v = G["out"].rearrange("(n t p) d -> n p t d", t=2, p=TP)
    sems = dict(load=0, wc=0, w_turned=2, wT=2, o=2, biased=0, y=2, out0=16, out1=16)
    with phase(nc, "slout", sems) as (block, s, sb, ps):
        wc, wT = sb("wc", [TP, 2, 2, SI]), sb("wT", [128, 2, 2, SI])
        bo, y = sb("bo", [TP, D]), sb("y", [TP, 2, 2, D])
        psT, o = ps("psT", 4), ps("o", 2)

        @block.sync
        def _(sp):
            sp.dma_start(bo[:], row_of(A["L1_ffn_b_out"], D)).then_inc(s["load"], 16)

            def save(p, b):
                hold(sp, s["y"], p + 3)
                sp.dma_start(out_v[bass.ds(p, 1)].rearrange("n p t d -> (n p) t d"), y[:, b]).then_inc(s[f"out{b}"], 16)
            pairs(sp, save)
            sp.wait_ge(s["out0"], 16 * (PAIRS // 2 + 2))
            sp.wait_ge(s["out1"], 16 * (PAIRS // 2 + 1))

        @block.gpsimd
        def _(pool):
            pool.wait_ge(s["load"], 16)

            def bias(p, b):
                Xp = pair_of(X, p)
                pool.tensor_tensor(Xp, Xp, bo[:].unsqueeze(1).to_broadcast([TP, 2, D]), ALU.add).then_inc(s["biased"], 1)
            pairs(pool, bias)

        @block.vector
        def _(v):
            def copy(p, b):
                hold(v, s["w_turned"], p + 1)
                v.tensor_copy(wc[:, b], pair_of(W, p)).then_inc(s["wc"], 1)

            def add(p, b):
                v.wait_ge(s["o"], p + 3)
                v.wait_ge(s["biased"], p + 1)
                v.wait_ge(s[f"out{b}"], 16 * (p // 2) + 16)
                v.tensor_tensor(y[:, b], pair_of(X, p), o[0:TP, b].rearrange("p (t d) -> p t d", t=2), ALU.add
                                ).then_inc(s["y"], 1)
            pairs(v, add, copy)

        @block.scalar
        def _(act):
            def evacuate(p, b):
                act.wait_ge(s["w_turned"], p + 3)
                act.wait_ge(s["o"], p + 1)
                for t in range(2):
                    last = act.copy(wT[:, b, t, 0:SJ * TP], psT[:, 2 * b + t, 0:SJ * TP])
                last.then_inc(s["wT"], 1)
            pairs(act, evacuate)

        @block.tensor
        def _(pe):
            def turn(p, b):
                pe.wait_ge(s["wc"], p + 1)
                pe.wait_ge(s["wT"], p + 1)
                for t in range(2):
                    for j in range(SJ):
                        mm = pe.transpose(psT[:, 2 * b + t, j * TP:(j + 1) * TP], wc[:, b, t, j * 128:(j + 1) * 128],
                                          G["ident"][0:TP, 0:TP])
                mm.then_inc(s["w_turned"], 1)

            def product(p, b):
                pe.wait_ge(s["wT"], p + 3)
                pe.wait_ge(s["y"], p + 1)
                for t in range(2):
                    for j in range(SJ):
                        mm = pe.matmul(o[0:TP, b, t * D:(t + 1) * D], wT[:, b, t, j * TP:(j + 1) * TP], fold_out[:, j, :],
                                       start=(j == 0), stop=(j == SJ - 1))
                mm.then_inc(s["o"], 1)
            pairs(pe, product, turn)


def kernel(**inputs):
    import numpy as np
    import concourse.bacc as bacc
    from concourse import mybir
    from concourse.bass_utils import run_bass_kernel_spmd

    nc = bacc.Bacc("TRN2", target_bir_lowering=False, num_devices=1)
    arrays, A = {}, {}
    for name, value in inputs.items():
        a = np.ascontiguousarray(value)
        if a.ndim == 0:
            a = a.reshape(1)
        arrays[f"in_{name}_dram"] = a
        A[name] = nc.dram_tensor(f"in_{name}_dram", a.shape, mybir.dt.from_np(a.dtype), kind="ExternalInput").ap()
    out = nc.dram_tensor("out_0_dram", (NODES, D), mybir.dt.float32, kind="ExternalOutput").ap()
    build(nc, A, out)
    r = run_bass_kernel_spmd(nc, [arrays], core_ids=[0])
    return r.results[0]["out_0_dram"]
```

```python
from contextlib import ExitStack, contextmanager

import concourse.bass as bass
from concourse import mybir

ALU = mybir.AluOpType
ACT = mybir.ActivationFunctionType
F32 = mybir.dt.float32
I32 = mybir.dt.int32
X_AXIS = mybir.AxisListType.X

NODES = 6250
EDGES = 100000
D = 256
HALVES = D // 128
TP = 125
NT = NODES // TP
PAIRS = NT // 2
PT = 2 * TP
DEPTH = 4
FF = 4 * D
HEAD = 32
EPS = 1e-5
BIG = 1e30


@contextmanager
def phase(nc, name, sems):
    with ExitStack() as ctx:
        made = {n: ctx.enter_context(nc.semaphore(f"{name}_{n}")) for n in sems}
        for n, credits in sems.items():
            nc.sync.sem_clear(made[n])
            if credits:
                nc.sync.sem_inc(made[n], credits)
        nc.all_engine_barrier(sem_only=True)

        def sb(n, shape, dtype=F32):
            return ctx.enter_context(nc.sbuf_tensor(f"{name}_{n}", shape, dtype))

        def ps(n, banks=1):
            return ctx.enter_context(nc.psum_tensor(f"{name}_{n}_ps", [128, banks, 512], F32))

        block = ctx.enter_context(nc.Block())
        yield block, made, sb, ps


def pairs(eng, main, ahead=None, early=None):
    def turn(p, u):
        if early and not (isinstance(p, int) and p + 2 >= PAIRS):
            early(p + 2, u)
        if ahead and not (isinstance(p, int) and p + 1 >= PAIRS):
            ahead(p + 1, 1 - u)
        main(p, u)

    if early:
        early(0, 0)
        early(1, 1)
    if ahead:
        ahead(0, 0)
    looped = PAIRS - 1 if not early else PAIRS - 3
    with eng.Fori(0, looped // 2) as j:
        for u in range(2):
            turn(2 * j + u, u)
    for p in range(looped, PAIRS):
        turn(p, p % 2)


def build(nc, A, out):
    with ExitStack() as ctx:
        def keep(n, shape, dtype=F32):
            return ctx.enter_context(nc.sbuf_tensor(n, shape, dtype))

        def dram(n, shape, dtype=F32):
            return nc.dram_tensor(n, shape, dtype, kind="Internal").ap()

        held = ctx.enter_context(nc.semaphore("held"))

        def hold(eng, sem, value):
            eng.wait_ge(sem, value)
            eng.sem_inc(held, 1)

        G = dict(
            ident=keep("ident", [128, 128]), ones=keep("ones", [128, 128]), zeros=keep("zeros", [128, 132]),
            below=keep("below", [128, 128]),
            spare=keep("spare", [128, 1]), spare_i=keep("spare_i", [128, 1], I32),
            mask32=keep("mask32", [128, 128]), mask64=keep("mask64", [128, 128]),
            X=keep("X", [TP, NT, D]),
            stats=keep("stats", [TP, NT, 6]),
            rstd=keep("rstd", [TP, NT]), shift=keep("shift", [TP, NT]),
            semaphore=lambda n: ctx.enter_context(nc.semaphore(n)),
            hold=hold, keep=keep, dram=dram, A=A, out=out,
        )
        constants(nc, G)
        load_x(nc, G)
        finish_stats(nc, G, "stats0")
        edges = EdgeSums(nc, G)
        with edges.zeros(nc) as edges.zero:
            normalise_x(nc, G, edges)
        with ExitStack() as steps:
            def step(n, shape, dtype=F32):
                return steps.enter_context(nc.sbuf_tensor(n, shape, dtype))
            T = dict(src=step("step_src", [EP, STEP_COLS], I32), rel=step("step_rel", [EP, STEP_COLS]),
                     n=step("step_n", [1, STEP_COLS], I32), e=step("step_e", [1, STEP_COLS], I32),
                     nodes=step("nodes", [EP, TP]), nodes_i=step("nodes_i", [EP, TP], I32),
                     gathered=G["semaphore"]("sched_gathered"))
            with nc.sbuf_tensor("src_all", [EP, GTILES], F32) as T["src_all"], \
                    nc.sbuf_tensor("dst_all", [EP, GTILES + GROUP], I32) as T["dst_all"]:
                schedule(nc, G, T)
                edges.T = T
                mixer0(nc, G, edges)
            graph0_dense(nc, G, edges)
            finish_stats(nc, G, "x1stats")
            experts(nc, G)
            finish_stats(nc, G, "x2stats")
            layer1(nc, G, T)
        finish_stats(nc, G, "x3stats")
        slice_attention(nc, G)


def tile_of(T, q):
    return T[:, bass.ds(q, 1), :].rearrange("p a b -> p (a b)")


def pair_of(T, p):
    return T[:, bass.ds(2 * p, 2), :]


def constants(nc, G):
    with phase(nc, "const", dict(cleared=0, masks=0, spare=0)) as (block, s, sb, ps):
        @block.gpsimd
        def _(pool):
            pool.memset(G["ident"][:], 0.0).then_inc(s["cleared"], 1)
            pool.wait_ge(s["cleared"], 1)
            pool.affine_select(out=G["ident"][:], in_=G["ident"][:], compare_op=ALU.not_equal, fill=1.0,
                               base=0, pattern=[[-1, 128]], channel_multiplier=1)

            pool.memset(G["below"][:], 1.0).then_inc(s["cleared"], 1)
            pool.wait_ge(s["cleared"], 2)
            pool.affine_select(out=G["below"][:], in_=G["below"][:], compare_op=ALU.is_gt, fill=0.0,
                               base=0, pattern=[[-1, 128]], channel_multiplier=1)
            pool.iota(G["spare_i"][:], [[0, 1]], base=NODES, channel_multiplier=1).then_inc(s["spare"], 1)

        @block.vector
        def _(v):
            v.wait_ge(s["spare"], 1)
            v.tensor_copy(G["spare"][:], G["spare_i"][:])
            v.memset(G["ones"][:], 1.0)
            v.memset(G["zeros"][:], 0.0)
            v.memset(G["mask32"][:], 0.0)
            v.memset(G["mask64"][:], 0.0).then_inc(s["masks"], 1)
            v.wait_ge(s["masks"], 1)
            for m, w in (("mask32", 32), ("mask64", 64)):
                for g in range(128 // w):
                    v.memset(G[m][g * w:(g + 1) * w, g * w:(g + 1) * w], 1.0)


def stats_of_pair(v, G, X, p):
    for t in range(2):
        q = 2 * p + t
        v.bn_stats(tile_of(G["stats"], q), tile_of(X, q))


LOADS = 5


def load_x(nc, G):
    x_v = G["A"]["x"].rearrange("(t p) d -> p t d", p=TP)
    step = NT // LOADS
    with phase(nc, "loadx", {f"x{n}": 0 for n in range(LOADS)}) as (block, s, sb, ps):
        @block.sync
        def _(sp):
            for n in range(LOADS):
                part = slice(n * step, (n + 1) * step)
                sp.dma_start(G["X"][:, part, :], x_v[:, part, :]).then_inc(s[f"x{n}"], 16)

        @block.vector
        def _(v):
            for n in range(LOADS):
                v.wait_ge(s[f"x{n}"], 16)
                with v.Fori(n * PAIRS // LOADS, (n + 1) * PAIRS // LOADS) as p:
                    stats_of_pair(v, G, G["X"], p)


def finish_stats(nc, G, name):
    with phase(nc, name, dict(step=0)) as (block, s, sb, ps):
        std, means, apart, squares = (sb(n, [TP, NT]) for n in ("std", "means", "apart", "squares"))
        m0, s0, m1, s1 = (G["stats"][:, :, k] for k in (1, 2, 4, 5))

        @block.vector
        def _(v):
            v.tensor_tensor(apart[:], m0, m1, ALU.subtract).then_inc(s["step"], 1)
            v.tensor_tensor(squares[:], s0, s1, ALU.add).then_inc(s["step"], 1)
            v.tensor_tensor(means[:], m0, m1, ALU.add).then_inc(s["step"], 1)
            v.wait_ge(s["step"], 3)
            v.tensor_tensor(apart[:], apart[:], apart[:], ALU.mult).then_inc(s["step"], 1)
            v.tensor_scalar(squares[:], squares[:], 1.0 / D, EPS, ALU.mult, ALU.add).then_inc(s["step"], 1)
            v.wait_ge(s["step"], 5)
            v.scalar_tensor_tensor(out=std[:], in0=apart[:], scalar=0.25, in1=squares[:],
                                   op0=ALU.mult, op1=ALU.add).then_inc(s["step"], 1)
            v.wait_ge(s["step"], 7)
            v.reciprocal(G["rstd"][:], std[:]).then_inc(s["step"], 1)
            v.wait_ge(s["step"], 8)
            v.scalar_tensor_tensor(out=G["shift"][:], in0=means[:], scalar=-0.5, in1=G["rstd"][:],
                                   op0=ALU.mult, op1=ALU.mult).then_inc(s["step"], 1)

        @block.scalar
        def _(act):
            act.wait_ge(s["step"], 6)
            act.activation(std[:], std[:], ACT.Sqrt).then_inc(s["step"], 1)


def normalise_x(nc, G, edges):
    G["xn_d"] = G["dram"]("xn_d", [NODES, D])
    xn_v = G["xn_d"].rearrange("(n t p) d -> n p t d", t=2, p=TP)
    with phase(nc, "normx", dict(done=0, out0=0, out1=0)) as (block, s, sb, ps):
        @block.vector
        def _(v):
            def apply(p, b):
                for t in range(2):
                    q = 2 * p + t
                    v.tensor_scalar(tile_of(G["X"], q), tile_of(G["X"], q), G["rstd"][:, bass.ds(q, 1)],
                                    G["shift"][:, bass.ds(q, 1)], ALU.mult, ALU.add).then_inc(s["done"], 1)

            def stats(p, b):
                G["hold"](v, s["done"], 2 * p + 2)
                stats_of_pair(v, G, G["X"], p)
            pairs(v, stats, apply)

        @block.gpsimd
        def _(pool):
            edges.clear(pool)

        @block.sync
        def _(sp):
            def save(p, b):
                G["hold"](sp, s["done"], 2 * p + 2)
                sp.dma_start(xn_v[bass.ds(p, 1)].rearrange("n p t d -> (n p) t d"),
                             pair_of(G["X"], p)).then_inc(s[f"out{b}"], 16)
            pairs(sp, save)
            sp.wait_ge(s["out0"], 16 * (PAIRS // 2 + 1))
            sp.wait_ge(s["out1"], 16 * (PAIRS // 2))


def hT_sems():
    return dict(h_ready=0, h_turned=2, hT_ready=1)


def normalise_pair(v, G, s, h, p, b):
    for t in range(2):
        q = 2 * p + t
        v.wait_ge(s["h_turned"], p + 1)
        v.tensor_scalar(h[:, b, t, :], tile_of(G["X"], q), G["rstd"][:, bass.ds(q, 1)],
                        G["shift"][:, bass.ds(q, 1)], ALU.mult, ALU.add).then_inc(s["h_ready"], 1)


def turn_pair(pe, G, s, h, psT, p, b):
    pe.wait_ge(s["h_ready"], 2 * p + 2)
    pe.wait_ge(s["hT_ready"], p + 1)
    for c in range(HALVES):
        for t in range(2):
            last = pe.transpose(psT[:, 0, c * 250 + t * TP:c * 250 + (t + 1) * TP],
                                h[:, b, t, c * 128:(c + 1) * 128], G["ident"][0:TP, 0:TP])
    last.then_inc(s["h_turned"], 1)


def affine_evacuate(act, s, psT, hT, gain, bias, p, b, free):
    act.wait_ge(s["h_turned"], p + 3)
    act.wait_ge(*free)
    for c in range(HALVES):
        src = psT[:, 0, c * 250:(c + 1) * 250]
        if gain is None:
            last = act.copy(hT[:, b, c, :], src)
        else:
            last = act.activation(hT[:, b, c, :], src, ACT.Identity, bias=bias[:, c:c + 1], scale=gain[:, c:c + 1])
    last.then_inc(s["hT_ready"], 1)


def mixer0(nc, G, edges):
    A = G["A"]
    q_d = G["dram"]("q_d", [PAIRS, TP, 2 * D])
    with ExitStack() as ctx:
        def keep(n, shape):
            return ctx.enter_context(nc.sbuf_tensor(n, shape, F32))
        Cp = keep("ctx_out", [128, HALVES, D])
        finish_stats(nc, G, "mstats")
        with nc.Fori(0, DEPTH) as l:
            with ExitStack() as kv:
                K = kv.enter_context(nc.sbuf_tensor("K", [TP, NT, D], F32))
                V = kv.enter_context(nc.sbuf_tensor("V", [TP, NT, HALVES, 129], F32))
                kmax = kv.enter_context(nc.sbuf_tensor("kmax", [TP, 2, D], F32))
                Wo = kv.enter_context(nc.sbuf_tensor("Wo", [128, HALVES, D], F32))
                mixer0_qkv(nc, G, l, K, V, kmax, Wo, q_d)
                context(nc, G, "ctx0", HALVES, K, V, kmax, HEAD ** -0.25, Wo, Cp)
            mixer0_attend(nc, G, l, q_d, Cp)
            finish_stats(nc, G, "astats")
            mixer0_ff(nc, G, l, edges)
            finish_stats(nc, G, "fstats")


def layer_rows(W, l):
    return W[bass.ds(l, 1)].rearrange("l (c p) n -> p (l c) n", p=128)


def layer_cols(b, l):
    return b[bass.ds(l, 1)].rearrange("l (c p) -> p (l c)", p=128)


def layer_bcast(b, l):
    return b[bass.ds(l, 1), :].to_broadcast([TP, b.shape[1]])


def mixer0_qkv(nc, G, l, K, V, kmax, Wo, q_d):
    A, hold, X = G["A"], G["hold"], G["X"]
    sems = dict(weights=0, q_ps=0, k_ps=0, v_ps=2, k_copied=2, v_copied=2, q_sub=2, q_exp=0,
                q_div=2, kmax_done=0, qm=0, qz=0, qout0=16, qout1=16, biased=0, **hT_sems())
    with phase(nc, "qkv", sems) as (block, s, sb, ps):
        Wqkv = sb("W", [128, HALVES, 3 * D])
        gain, bias = sb("gain", [128, HALVES]), sb("bias", [128, HALVES])
        bo = sb("bo", [TP, D])
        h = sb("h", [TP, 2, 2, D])
        hT = sb("hT", [128, 2, HALVES, PT])
        q = sb("q", [TP, 2, 2, D])
        qm, qz = sb("qm", [TP, 2, D // HEAD]), sb("qz", [TP, 2, 2, D // HEAD])
        psT, qp, kp, vp = ps("psT"), ps("q", 2), ps("k", 2), ps("v", 2)
        heads = "p t (h e) -> p t h e"

        @block.sync
        def _(sp):
            for n, w in enumerate(("Wk", "Wq", "Wv")):
                sp.dma_start(Wqkv[:, :, n * D:(n + 1) * D], layer_rows(A[f"L0_mix_{w}"], l)).then_inc(s["weights"], 16)
            sp.dma_start(Wo[:], layer_rows(A["L0_mix_Wo"], l)).then_inc(s["weights"], 16)
            sp.dma_start(gain[:], layer_cols(A["L0_mix_ln1_g"], l), allow_slow_non_contiguous=True).then_inc(s["weights"], 16)
            sp.dma_start(bias[:], layer_cols(A["L0_mix_ln1_b"], l), allow_slow_non_contiguous=True).then_inc(s["weights"], 16)
            sp.dma_start(bo[:], layer_bcast(A["L0_mix_bo"], l)).then_inc(s["weights"], 16)

            def save(p, b):
                hold(sp, s["q_div"], p + 3)
                sp.dma_start(q_d[bass.ds(p, 1)].rearrange("n p d -> (n p) d"),
                             q[:, b].rearrange("p t d -> p (t d)")).then_inc(s[f"qout{b}"], 16)
            pairs(sp, save)
            sp.wait_ge(s["qout0"], 16 * 14)
            sp.wait_ge(s["qout1"], 16 * 13)

        @block.vector
        def _(v):
            v.memset(kmax[:], -BIG).then_inc(s["kmax_done"], 1)
            v.memset(V[:, :, :, 128:129], 1.0)

            def soft(p, b):
                qv = qp[0:TP, b].rearrange("p (t h e) -> p t h e", t=2, e=HEAD)
                v.wait_ge(s["q_ps"], p + 1)
                v.wait_ge(s["q_sub"], p + 1)
                v.tensor_reduce(qm[:], qv, X_AXIS, ALU.max).then_inc(s["qm"], 1)
                v.wait_ge(s["qm"], p + 1)
                v.wait_ge(s[f"qout{b}"], 16 * (p // 2) + 16)
                v.tensor_tensor(q[:, b].rearrange(heads, e=HEAD), qv,
                                qm[:].unsqueeze(3).to_broadcast([TP, 2, D // HEAD, HEAD]),
                                ALU.subtract).then_inc(s["q_sub"], 1)
                v.wait_ge(s["k_copied"], p + 3)
                v.wait_ge(s["kmax_done"], p + 1)
                v.tensor_tensor(kmax[:], kmax[:], pair_of(K, p), ALU.max).then_inc(s["kmax_done"], 1)
                v.wait_ge(s["q_exp"], p + 1)
                v.wait_ge(s["q_div"], p + 1)
                v.tensor_reduce(qz[:, b], q[:, b].rearrange(heads, e=HEAD), X_AXIS, ALU.add).then_inc(s["qz"], 1)
                v.wait_ge(s["qz"], 2 * p + 1)
                v.reciprocal(qz[:, b], qz[:, b]).then_inc(s["qz"], 1)
            pairs(v, soft, early=lambda p, b: normalise_pair(v, G, s, h, p, b))

        @block.gpsimd
        def _(pool):
            pool.wait_ge(s["weights"], 16 * 7)

            def divide(p, b):
                hold(pool, s["qz"], 2 * p + 2)
                pool.tensor_tensor(q[:, b].rearrange(heads, e=HEAD), q[:, b].rearrange(heads, e=HEAD),
                                   qz[:, b].unsqueeze(3).to_broadcast([TP, 2, D // HEAD, HEAD]),
                                   ALU.mult).then_inc(s["q_div"], 1)
                Xp = pair_of(X, p)
                hold(pool, s["h_ready"], 2 * p + 2)
                pool.tensor_tensor(Xp, Xp, bo[:].unsqueeze(1).to_broadcast([TP, 2, D]), ALU.add).then_inc(s["biased"], 1)
            pairs(pool, divide)

        @block.scalar
        def _(act):
            act.wait_ge(s["weights"], 16 * 7)

            def evacuate(p, b):
                affine_evacuate(act, s, psT, hT, gain, bias, p, b, (s["v_ps"], p + 1))

            def main(p, b):
                act.wait_ge(s["q_sub"], p + 3)
                act.activation(q[:, b], q[:, b], ACT.Exp, scale=HEAD ** -0.25).then_inc(s["q_exp"], 1)
                hold(act, s["k_ps"], p + 1)
                act.copy(pair_of(K, p), kp[0:TP, b].rearrange("p (t d) -> p t d", t=2)).then_inc(s["k_copied"], 1)
                hold(act, s["v_ps"], p + 3)
                act.copy(V[:, bass.ds(2 * p, 2), :, 0:128],
                         vp[0:TP, b].rearrange("p (t c e) -> p t c e", t=2, e=128)).then_inc(s["v_copied"], 1)
            pairs(act, main, evacuate)

        @block.tensor
        def _(pe):
            pe.wait_ge(s["weights"], 16 * 7)

            def project(p, b):
                pe.wait_ge(s["hT_ready"], p + 2)
                for n, (dst, free, done) in enumerate(((kp, "k_copied", "k_ps"), (qp, "q_sub", "q_ps"),
                                                       (vp, "v_copied", "v_ps"))):
                    pe.wait_ge(s[free], p + 1)
                    for t in range(2):
                        for c in range(HALVES):
                            last = pe.matmul(dst[0:TP, b, t * D:(t + 1) * D], hT[:, b, c, t * TP:(t + 1) * TP],
                                             Wqkv[:, c, n * D:(n + 1) * D], start=(c == 0), stop=(c == HALVES - 1))
                    last.then_inc(s[done], 1)
            pairs(pe, project, lambda p, b: turn_pair(pe, G, s, h, psT, p, b))


def context(nc, G, name, halves, K, V, kmax, scale, Wo, Cp, folded=None):
    hold, w = G["hold"], 128 * halves
    with phase(nc, name, dict(step=0, ks=0, exp=2, used=2, ctx=0)) as (block, s, sb, ps):
        kcol, D_kmax = sb("kcol", [128, halves]), sb("diag", [128, halves, 128])
        krow = sb("krow", [TP, w])
        ks, ek = sb("ks", [TP, 2, 2, w]), sb("ek", [TP, 2, 2, w])
        zinv = sb("zinv", [128, halves])
        C, CT = sb("C", [128, halves, 128]), sb("CT", [128, halves, 128])
        psA, psB, psC = ps("A"), ps("B"), ps("C", 2)

        @block.vector
        def _(v):
            v.tensor_tensor(krow[:], kmax[:, 0, :], kmax[:, 1, :], ALU.max).then_inc(s["step"], 1)
            v.wait_ge(s["step"], 2)
            v.tensor_reduce(kcol[:], psA[:, 0, 0:halves * TP].rearrange("p (c t) -> p c t", c=halves),
                            X_AXIS, ALU.max).then_inc(s["step"], 1)
            v.wait_ge(s["step"], 3)
            for c in range(halves):
                last = v.tensor_scalar(D_kmax[:, c, :], G["ident"][:], kcol[:, c:c + 1], None, ALU.mult)
            last.then_inc(s["step"], 1)
            v.wait_ge(s["step"], 5)
            v.tensor_copy(krow[:], psB[0:TP, 0, 0:w]).then_inc(s["step"], 1)
            v.wait_ge(s["step"], 6)

            def sub(p, b):
                v.wait_ge(s["exp"], p + 1)
                v.tensor_tensor(ks[:, b], pair_of(K, p), krow[:].unsqueeze(1).to_broadcast([TP, 2, w]),
                                ALU.subtract).then_inc(s["ks"], 1)
            pairs(v, sub)
            v.wait_ge(s["ctx"], 1)
            v.reciprocal(zinv[:], psC[:, 0:halves, 128]).then_inc(s["ctx"], 1)
            v.wait_ge(s["ctx"], 2)
            for c in range(halves):
                last = v.scalar_tensor_tensor(out=C[:, c, :], in0=psC[:, c, 0:128], scalar=zinv[:, c:c + 1],
                                              in1=G["mask32"][:], op0=ALU.mult, op1=ALU.mult)
            last.then_inc(s["ctx"], 1)
            v.wait_ge(s["ctx"], 4)
            v.tensor_copy(CT[:], psA[:, 0, 0:w].rearrange("p (c e) -> p c e", c=halves)).then_inc(s["ctx"], 1)
            v.wait_ge(s["ctx"], 6)
            v.tensor_copy(Cp[:], psB[:, 0, 0:halves * D].rearrange("p (c e) -> p c e", c=halves)).then_inc(s["ctx"], 1)
            if folded:
                v.wait_ge(s["ctx"], 8)
                v.tensor_scalar(folded[2][:], psA[:, 0, :].rearrange("p (c e) -> p c e", c=HALVES), folded[1], None,
                                ALU.mult).then_inc(s["ctx"], 1)

        @block.scalar
        def _(act):
            def exp(p, b):
                act.wait_ge(s["ks"], p + 1)
                act.wait_ge(s["used"], p + 1)
                act.activation(ek[:, b], ks[:, b], ACT.Exp, scale=scale).then_inc(s["exp"], 1)
            pairs(act, exp)

        @block.tensor
        def _(pe):
            pe.wait_ge(s["step"], 1)
            for c in range(halves):
                last = pe.transpose(psA[:, 0, c * TP:(c + 1) * TP], krow[:, c * 128:(c + 1) * 128],
                                    G["ident"][0:TP, 0:TP])
            last.then_inc(s["step"], 1)
            pe.wait_ge(s["step"], 4)
            for c in range(halves):
                last = pe.matmul(psB[0:TP, 0, c * 128:(c + 1) * 128], G["ones"][:, 0:TP], D_kmax[:, c, :],
                                 start=True, stop=True)
            last.then_inc(s["step"], 1)
            for c in range(halves):
                pe.matmul(psC[:, c, 0:129], G["zeros"][:, 0:128], G["zeros"][:, 0:129], start=True, stop=False,
                          skip_group_check=True)

            def gather(p, b):
                pe.wait_ge(s["exp"], p + 3)
                for t in range(2):
                    for c in range(halves):
                        end = isinstance(p, int) and t == 1
                        last = pe.matmul(psC[:, c, 0:129], ek[:, b, t, c * 128:(c + 1) * 128],
                                         V[:, bass.ds(2 * p + t, 1), c, :].rearrange("p a e -> p (a e)"),
                                         start=False, stop=end, skip_group_check=True)
                last.then_inc(s["used"], 1)
            pairs(pe, gather)
            pe.wait_ge(s["used"], 2 + PAIRS)
            pe.sem_inc(s["ctx"], 1)
            pe.wait_ge(s["ctx"], 3)
            for c in range(halves):
                last = pe.transpose(psA[:, 0, c * 128:(c + 1) * 128], C[:, c, :], G["ident"][:])
            last.then_inc(s["ctx"], 1)
            pe.wait_ge(s["ctx"], 5)
            for c in range(halves):
                last = pe.matmul(psB[:, 0, c * D:(c + 1) * D], CT[:, c, :], Wo[:, c, :], start=True, stop=True)
            last.then_inc(s["ctx"], 1)
            if folded:
                pe.wait_ge(s["ctx"], 7)
                for c in range(HALVES):
                    last = pe.matmul(psA[:, 0, c * D:(c + 1) * D], folded[0][:, c * 128:(c + 1) * 128], Cp[:, 0, :],
                                     start=True, stop=True)
                last.then_inc(s["ctx"], 1)


def mixer0_attend(nc, G, l, q_d, Cp):
    hold, X = G["hold"], G["X"]
    sems = dict(q0=0, q1=0, q_turned=2, qT=2, o=2, x_done=2)
    with phase(nc, "attend", sems) as (block, s, sb, ps):
        q, qT = sb("q", [TP, 2, 2 * D]), sb("qT", [128, 2, HALVES, PT])
        psT, o = ps("psT", 2), ps("o", 2)

        @block.sync
        def _(sp):
            def load(p, b):
                hold(sp, s["q_turned"], p + 1)
                sp.dma_start(q[:, b], q_d[bass.ds(p, 1)].rearrange("n p d -> (n p) d")).then_inc(s[f"q{b}"], 16)
            pairs(sp, load)

        @block.tensor
        def _(pe):
            def turn(p, b):
                pe.wait_ge(s[f"q{b}"], 16 * (p // 2) + 16)
                pe.wait_ge(s["qT"], p + 1)
                for c in range(HALVES):
                    for t in range(2):
                        last = pe.transpose(psT[:, b, c * PT + t * TP:c * PT + (t + 1) * TP],
                                            q[:, b, t * D + c * 128:t * D + (c + 1) * 128], G["ident"][0:TP, 0:TP])
                last.then_inc(s["q_turned"], 1)

            def out(p, b):
                pe.wait_ge(s["qT"], p + 3)
                pe.wait_ge(s["x_done"], p + 1)
                for t in range(2):
                    for c in range(HALVES):
                        last = pe.matmul(o[0:TP, b, t * D:(t + 1) * D], qT[:, b, c, t * TP:(t + 1) * TP], Cp[:, c, :],
                                         start=(c == 0), stop=(c == HALVES - 1))
                last.then_inc(s["o"], 1)
            pairs(pe, out, turn)

        @block.scalar
        def _(act):
            def evacuate(p, b):
                act.wait_ge(s["q_turned"], p + 3)
                act.wait_ge(s["o"], p + 1)
                act.copy(qT[:, b], psT[:, b, 0:2 * PT].rearrange("p (c t) -> p c t", c=HALVES)).then_inc(s["qT"], 1)
            pairs(act, evacuate)

        @block.vector
        def _(v):
            def add(p, b):
                add_and_stats(v, G, s, o[0:TP, b].rearrange("p (t d) -> p t d", t=2), p, 2)
            pairs(v, add)


def add_and_stats(v, G, s, src, p, credits):
    Xp = pair_of(G["X"], p)
    v.wait_ge(s["o"], p + 3)
    v.tensor_tensor(Xp, Xp, src, ALU.add).then_inc(s["x_done"], 1)
    G["hold"](v, s["x_done"], p + 1 + credits)
    stats_of_pair(v, G, G["X"], p)


def mixer0_ff(nc, G, l, edges):
    A, hold, X = G["A"], G["hold"], G["X"]
    blocks = FF // 128
    sems = dict(weights=0, hid=0, act_done=4, o=2, x_done=1, biased=0, **hT_sems(), **edges.SEMS)
    with phase(nc, "ff", sems) as (block, s, sb, ps):
        W1, W2 = sb("W1", [128, HALVES, FF]), sb("W2", [128, blocks, D])
        gain, bias, b1 = sb("gain", [128, HALVES]), sb("bias", [128, HALVES]), sb("b1", [128, blocks])
        b2 = sb("b2", [TP, D])
        h, hT = sb("h", [TP, 2, 2, D]), sb("hT", [128, 2, HALVES, PT])
        act_out = sb("gelu", [128, 2, blocks, PT])
        psT, hid, o = ps("psT"), ps("hid", 4), ps("o", 2)
        edges.buffers(s, sb, ps)

        @block.sync
        def _(sp):
            for dst, src in ((gain[:], layer_cols(A["L0_mix_ln2_g"], l)), (bias[:], layer_cols(A["L0_mix_ln2_b"], l)),
                             (b1[:], layer_cols(A["L0_mix_b1"], l)), (b2[:], layer_bcast(A["L0_mix_b2"], l)),
                             (W1[:], layer_rows(A["L0_mix_W1"], l)), (W2[:], layer_rows(A["L0_mix_W2"], l))):
                sp.dma_start(dst, src, allow_slow_non_contiguous=True).then_inc(s["weights"], 16)
            pairs(sp, lambda p, b: edges.source_rows(sp, l, p, b))

        @block.vector
        def _(v):
            edges.begin(v, l)
            v.wait_ge(s["weights"], 16 * 6)

            def early(p, b):
                normalise_pair(v, G, s, h, p, b)
                Xp = pair_of(X, p)
                v.wait_ge(s["h_ready"], 2 * p + 2)
                v.tensor_tensor(Xp, Xp, b2[:].unsqueeze(1).to_broadcast([TP, 2, D]), ALU.add).then_inc(s["biased"], 1)

            def add(p, b):
                v.wait_ge(s["biased"], p + 1)
                add_and_stats(v, G, s, o[0:TP, :, 0:D], p, 1)
            pairs(v, add, lambda p, b: edges.compare(v, l, p, b), early)

        @block.gpsimd
        def _(pool):
            pool.wait_ge(s["weights"], 16 * 6)
            for u in range(GROUP):
                edges.gather(pool, 0, 0, u)
            with pool.Fori(0, PAIRS // 2) as j:
                for b in range(2):
                    edges.move(pool, l, 2 * j + b, b)
            for u in range(GROUP):
                edges.scatter(pool, l, PAIRS - 1, 0, u)
            for u in range(GROUP):
                hold(pool, edges.stored[u], 16 * PAIRS * l + 16 * PAIRS + 16)

        @block.scalar
        def _(act):
            act.wait_ge(s["weights"], 16 * 6)

            def evacuate(p, b):
                affine_evacuate(act, s, psT, hT, gain, bias, p, b, (s["o"], p + 1))

            def gelu(p, b):
                for n in range(blocks):
                    act.wait_ge(s["hid"], blocks * p + n + 1)
                    act.activation(act_out[:, b, n, :], hid[:, n % 4, 0:PT], ACT.Gelu,
                                   bias=b1[:, n:n + 1]).then_inc(s["act_done"], 1)
                    if n % 2:
                        edges.evacuate(act, l, p, n // 2)
                for u in range(GROUP // 2, GROUP):
                    edges.evacuate(act, l, p, u)
            pairs(act, gelu, evacuate)

        @block.tensor
        def _(pe):
            pe.wait_ge(s["weights"], 16 * 6)

            def products(p, b):
                pe.wait_ge(s["hT_ready"], p + 2)
                for n in range(blocks):
                    pe.wait_ge(s["act_done"], blocks * p + n + 1)
                    for c in range(HALVES):
                        last = pe.matmul(hid[:, n % 4, 0:PT],
                                         W1[:, c, n * 128:(n + 1) * 128], hT[:, b, c, :],
                                         start=(c == 0), stop=(c == HALVES - 1))
                    last.then_inc(s["hid"], 1)
                    if n % 2:
                        edges.product(pe, l, p, b, n // 2)
                pe.wait_ge(s["act_done"], blocks * p + blocks + 4)
                pe.wait_ge(s["x_done"], p + 1)
                for t in range(2):
                    for n in range(blocks):
                        last = pe.matmul(o[0:TP, t, 0:D], act_out[:, b, n, t * TP:(t + 1) * TP], W2[:, n, :],
                                         start=(n == 0), stop=(n == blocks - 1))
                        if n % 4 == 3:
                            if n == blocks - 1 and t == 1:
                                last.then_inc(s["o"], 1)
                            edges.product(pe, l, p, b, GROUP // 2 + 2 * t + n // 4)
            pairs(pe, products, lambda p, b: turn_pair(pe, G, s, h, psT, p, b))



EP = 128
ETILES = 784
CHUNKS, CHUNK_TILES = 16, 49
ROWS, ROW_TILES = 112, 7
UNROLL = 16
STEPS = 848
STEP_BLOCKS = 7
STEP_COLS = STEP_BLOCKS * 128
RING = 8
PAD_DST = 1000000
GROUP = 8
GROUPS = PAIRS * DEPTH
GTILES = GROUP * GROUPS
REPLICAS = 2
ACC_ROWS = NODES + 150


def schedule(nc, G, T):
    A, ident = G["A"], G["ident"]
    srcp, dstp = G["dram"]("src_tiles", [GTILES, EP], I32), G["dram"]("dst_tiles", [ETILES, EP], I32)
    n_d, e_d = G["dram"]("step_node_d", [STEP_BLOCKS, 128], I32), G["dram"]("step_edge_d", [STEP_BLOCKS, 128], I32)
    G["dst_tiles"], G["src_tiles"] = dstp, srcp
    whole = EDGES // EP
    full = (ROW_TILES - 1) * ROWS * EP
    left = whole - (ROW_TILES - 1) * ROWS
    gathered = T["gathered"]
    with phase(nc, "sched", dict(pad=0, load=0, table=0, v=0, ps=0, iota=0, pool=0, steps=0, turned=0)) as (block, s, sb, ps):
        rows = {n: sb(n, [ROWS, ROW_TILES, EP], I32) for n in ("src", "dst")}
        got = {n: sb("got_" + n, [128, STEP_BLOCKS, EP], I32) for n in ("src", "dst")}
        gotf = {n: sb("gotf_" + n, [128, STEP_BLOCKS, EP]) for n in ("src", "dst")}
        et, st = sb("et", [ROWS, ROW_TILES], I32), sb("st", [128, STEP_BLOCKS], I32)
        etf, stf = sb("etf", [ROWS, ROW_TILES]), sb("stf", [128, STEP_BLOCKS])
        last, quot, over = sb("last", [ROWS, ROW_TILES]), sb("quot", [ROWS, ROW_TILES]), sb("over", [ROWS, ROW_TILES])
        whole_q = sb("whole_q", [ROWS, ROW_TILES], I32)
        diag = sb("diag", [ROWS, ROW_TILES, ROWS])
        ends = sb("ends", [128, ETILES])
        less = sb("less", [128, ETILES])
        es, ns, n125 = sb("es", [128, STEP_BLOCKS]), sb("ns", [128, STEP_BLOCKS]), sb("n125", [128, STEP_BLOCKS])
        esi, nsi = sb("esi", [128, STEP_BLOCKS], I32), sb("nsi", [128, STEP_BLOCKS], I32)
        rowsf = {n: sb("rowsf_" + n, [ROWS, ROW_TILES, EP]) for n in ("src", "dst")}
        tail = sb("tail", [GTILES - ETILES, EP], I32)
        endp, tp, plain = ps("end", 2), ps("tp", 4), ps("plain", 2)

        @block.gpsimd
        def _(pool):
            pool.iota(et[:], [[ROWS, ROW_TILES]], base=0, channel_multiplier=1).then_inc(s["iota"], 1)
            pool.iota(st[:], [[128, STEP_BLOCKS]], base=0, channel_multiplier=1).then_inc(s["iota"], 1)
            pool.iota(T["nodes_i"][:], [[1, TP]], base=0, channel_multiplier=0).then_inc(s["iota"], 1)
            pool.wait_ge(s["table"], 48)
            pool.wait_ge(s["steps"], 1)
            for k in range(STEP_BLOCKS):
                for n, table in (("src", srcp), ("dst", dstp)):
                    pool.indirect_dma_start(got[n][:, k, :], None, table,
                                            bass.IndirectOffsetOnAxis(ap=esi[:, k:k + 1], axis=0)
                                            ).then_inc(gathered, 16)

        @block.sync
        def _(sp):
            sp.wait_ge(s["pad"], 2)
            for n in ("src", "dst"):
                sp.dma_start(rows[n][:, 0:ROW_TILES - 1, :],
                             A[n][0:full].rearrange("(k j e) -> j k e", j=ROWS, e=EP)).then_inc(s["load"], 16)
                sp.dma_start(rows[n][0:left, ROW_TILES - 1, :],
                             A[n][full:whole * EP].rearrange("(j e) -> j e", e=EP)).then_inc(s["load"], 16)
                sp.dma_start(rows[n][left:left + 1, ROW_TILES - 1, 0:EDGES - whole * EP],
                             A[n][whole * EP:EDGES].rearrange("(a e) -> a e", a=1)).then_inc(s["load"], 16)
            sp.wait_ge(s["load"], 96)
            for n, table in (("src", srcp), ("dst", dstp)):
                sp.dma_start(table[0:ETILES].rearrange("(k j) e -> j k e", j=ROWS), rows[n][:]).then_inc(s["table"], 16)
            sp.dma_start(srcp[ETILES:GTILES], tail[:]).then_inc(s["table"], 16)
            sp.wait_ge(s["table"], 48)
            sp.wait_ge(s["steps"], 1)
            for dst, src in ((n_d, nsi), (e_d, esi)):
                sp.dma_start(dst.rearrange("k p -> p k"), src[:], allow_slow_non_contiguous=True).then_inc(s["table"], 16)
            sp.wait_ge(s["table"], 80)
            for dst, src in ((T["n"], n_d), (T["e"], e_d)):
                sp.dma_start(dst[:], src.rearrange("(a k) p -> a (k p)", a=1)).then_inc(s["table"], 16)
            sp.wait_ge(s["table"], 112)

        @block.vector
        def _(v):
            count = [0]

            def link(ins):
                count[0] += 1
                ins.then_inc(s["v"], 1)
                v.wait_ge(s["v"], count[0])

            v.memset(tail[:], NODES)
            v.memset(T["src_all"][:, ETILES:GTILES], float(NODES))
            v.memset(T["dst_all"][:, ETILES:GTILES + GROUP], NODES - 1)
            v.memset(rows["src"][:], NODES).then_inc(s["pad"], 1)
            v.memset(rows["dst"][:], PAD_DST).then_inc(s["pad"], 1)
            v.wait_ge(s["iota"], 3)
            v.tensor_copy(etf[:], et[:])
            v.tensor_copy(stf[:], st[:])
            v.tensor_copy(T["nodes"][:], T["nodes_i"][:])
            v.wait_ge(s["load"], 96)
            v.tensor_copy(rowsf["src"][:], rows["src"][:])
            link(v.tensor_scalar(rowsf["dst"][:], rows["dst"][:], float(NODES - 1), None, ALU.min))
            v.wait_ge(s["ps"], 1)
            link(v.tensor_copy(T["src_all"][:, 0:ETILES].rearrange("p (b c) -> p b c", b=2), plain[:, :, 0:ETILES // 2]))
            v.wait_ge(s["ps"], 2)
            link(v.tensor_copy(T["dst_all"][:, 0:ETILES].rearrange("p (b c) -> p b c", b=2), plain[:, :, 0:ETILES // 2]))
            link(v.tensor_scalar(last[:], rows["dst"][:, :, EP - 1], 0.5, 1.0 / TP, ALU.add, ALU.mult))
            link(v.tensor_copy(whole_q[:], last[:]))
            link(v.tensor_copy(quot[:], whole_q[:]))
            link(v.tensor_tensor(over[:], quot[:], last[:], ALU.is_gt))
            link(v.tensor_tensor(quot[:], quot[:], over[:], ALU.subtract))
            link(v.scalar_tensor_tensor(out=quot[:], in0=quot[:], scalar=float(NT - 1), in1=etf[:],
                                        op0=ALU.min, op1=ALU.add))
            for k in range(ROW_TILES):
                d = v.tensor_scalar(diag[:, k, :], ident[0:ROWS, 0:ROWS], quot[:, k:k + 1], None, ALU.mult)
            link(d)
            v.wait_ge(s["ps"], 3)
            link(v.tensor_copy(ends[:].rearrange("p (b c) -> p b c", b=2), endp[:, :, 0:ETILES // 2]))
            for k in range(STEP_BLOCKS):
                link(v.tensor_scalar(less[:], ends[:], stf[:, k:k + 1], None, ALU.is_lt))
                link(v.tensor_reduce(es[:, k:k + 1], less[:], X_AXIS, ALU.add))
            link(v.tensor_scalar(es[:], es[:], float(ETILES - 1), None, ALU.min))
            link(v.tensor_tensor(ns[:], stf[:], es[:], ALU.subtract))
            link(v.tensor_scalar(n125[:], ns[:], float(TP), None, ALU.mult))
            link(v.tensor_scalar(ns[:], ns[:], float(NT - 1), None, ALU.min))
            link(v.tensor_copy(esi[:], es[:]))
            v.tensor_copy(nsi[:], ns[:]).then_inc(s["steps"], 1)
            v.wait_ge(gathered, 16 * 2 * STEP_BLOCKS)
            for k in range(STEP_BLOCKS):
                v.tensor_copy(gotf["src"][:, k, :], got["src"][:, k, :])
                d = v.tensor_scalar(gotf["dst"][:, k, :], got["dst"][:, k, :], n125[:, k:k + 1], None, ALU.subtract)
            d.then_inc(s["turned"], 1)
            v.wait_ge(s["turned"], 2)
            v.tensor_scalar(T["src"][:, 0:512], tp[:, 0, :], float(NODES - 1), None, ALU.min)
            v.tensor_scalar(T["src"][:, 512:STEP_COLS], tp[:, 1, 0:STEP_COLS - 512], float(NODES - 1), None, ALU.min)
            v.tensor_copy(T["rel"][:, 0:512], tp[:, 2, :])
            v.tensor_copy(T["rel"][:, 512:STEP_COLS], tp[:, 3, 0:STEP_COLS - 512])

        @block.tensor
        def _(pe):
            half = ETILES // 2

            def columns(dst, product):
                for k in range(ROW_TILES):
                    cut = min(max(half, k * ROWS), (k + 1) * ROWS)
                    for lo, hi in ((k * ROWS, cut), (cut, (k + 1) * ROWS)):
                        if hi > lo:
                            mm = product(dst[:, lo // half, lo % half:lo % half + hi - lo], k, lo - k * ROWS, hi - k * ROWS)
                mm.then_inc(s["ps"], 1)

            for n, name in enumerate(("src", "dst")):
                pe.wait_ge(s["v"], 1 + n)
                columns(plain, lambda d, k, lo, hi: pe.matmul(d, rowsf[name][:, k, :], ident[0:ROWS, lo:hi],
                                                              start=True, stop=True))
            pe.wait_ge(s["v"], 10)
            columns(endp, lambda d, k, lo, hi: pe.matmul(d, G["ones"][0:ROWS, :], diag[:, k, lo:hi],
                                                         start=True, stop=True))
            pe.wait_ge(s["turned"], 1)
            for b, n in ((0, "src"), (2, "dst")):
                for k in range(STEP_BLOCKS):
                    mm = pe.transpose(tp[:, b + k // 4, k % 4 * 128:(k % 4 + 1) * 128], gotf[n][:, k, :], ident[:])
            mm.then_inc(s["turned"], 1)


def blocks_of_steps(eng, block):
    block(0)
    with eng.Fori(1, STEPS // UNROLL) as j:
        block(j)


def load_four(nc, eng, regs, row, step, top):
    eng.load(regs, row[0:1, bass.ds(step, 4)])
    return [nc.s_assert_within(eng.snap(r), 0, top, skip_runtime_bounds_check_because="schedule() clamps the rows")
            for r in regs]


SUM_SLOTS = 8
SUM_LAG = 4
HOT_AHEAD = 8


def one_hot_of_four(v, T, hot, step, u):
    slot = u % UNROLL
    return v.tensor_tensor(hot[:, slot:slot + 4, :], T["nodes"][:].unsqueeze(1).to_broadcast([EP, 4, TP]),
                           T["rel"][:, bass.ds(step, 4)].unsqueeze(2).to_broadcast([EP, 4, TP]), ALU.is_equal)


def copy_indices(act, T, idx, s, step, u):
    slot = u // 4 % 4
    act.copy(idx[:, slot, :], T["src"][:, bass.ds(step, 4)]).then_inc(s["idx"], 1)


def edge_sum(nc, G, name, T, ring, table, acc, extra, weights):
    hold, width = G["hold"], D + extra
    sems = dict(idx=0, hot=0, summed=SUM_SLOTS, added=SUM_SLOTS, cleared=0, weighted=RING)
    with phase(nc, name, sems) as (block, s, sb, ps):
        idx = sb("idx", [EP, 4, 4], I32)
        rows = sb("rows", [EP, RING, D])
        hot = sb("hot", [EP, UNROLL, TP])
        wr = sb("wr", [EP, SUM_SLOTS, width])
        sums = ps("sums", SUM_SLOTS)

        @block.gpsimd
        def _(pool):
            with pool.Fori(0, STEPS // UNROLL) as j:
                for u in range(UNROLL):
                    if u % 4 == 0:
                        hold(pool, s["idx"], 4 * j + u // 4 + 1)
                    hold(pool, s["weighted"], UNROLL * j + u + 1)
                    pool.indirect_dma_start(rows[:, u % RING, :], None, table,
                                            bass.IndirectOffsetOnAxis(ap=idx[:, u // 4, u % 4:u % 4 + 1], axis=0)
                                            ).then_inc(ring[u % RING], 16)

        @block.scalar
        def _(act):
            def indices(j):
                for u in range(0, UNROLL, 4):
                    step = UNROLL * j + u
                    if u >= 8 or not isinstance(j, int):
                        hold(act, s["weighted"], step - 12 + RING)
                    copy_indices(act, T, idx, s, step, u)
            blocks_of_steps(act, indices)

        @block.tensor
        def _(pe):
            with pe.Fori(0, STEPS // UNROLL) as j:
                for u in range(UNROLL):
                    step, slot = UNROLL * j + u, u % SUM_SLOTS
                    hold(pe, s["weighted"], step + 1 + RING)
                    if u % 4 == 0:
                        pe.wait_ge(s["hot"], 4 * j + u // 4 + 1)
                    pe.wait_ge(s["added"], step + 1)
                    pe.matmul(sums[0:TP, slot, 0:width], hot[:, u, :], wr[:, slot, :], start=True, stop=True
                              ).then_inc(s["summed"], 1)

        @block.vector
        def _(v):
            e_regs, n_regs = ([v.alloc_register(f"{k}{i}") for i in range(4)] for k in ("sum_e", "sum_n"))
            v.memset(acc[:], 0.0).then_inc(s["cleared"], 1)
            v.wait_ge(s["cleared"], 1)

            def weigh(step, u, j, e):
                slot = u % SUM_SLOTS
                w = weights[:, bass.ds(e, 1), :].rearrange("p a h -> p (a h)")
                v.wait_ge(ring[u % RING], 32 * j + 16 * (u // RING) + 16)
                v.wait_ge(s["summed"], step + 1)
                v.tensor_copy(wr[:, slot, D:width], w)
                v.tensor_tensor(wr[:, slot, 0:D].rearrange("p (h e) -> p h e", h=extra),
                                rows[:, u % RING, :].rearrange("p (h e) -> p h e", h=extra),
                                w.unsqueeze(2).to_broadcast([EP, extra, D // extra]), ALU.mult
                                ).then_inc(s["weighted"], 1)

            def add(step, u, n):
                a = tile_of(acc, n)
                v.wait_ge(s["summed"], step + 1 + SUM_SLOTS)
                v.wait_ge(s["added"], step + SUM_SLOTS)
                v.tensor_tensor(a, a, sums[0:TP, u % SUM_SLOTS, 0:width], ALU.add).then_inc(s["added"], 1)

            def steps(j):
                for u in range(UNROLL):
                    step, adds = UNROLL * j + u, u >= SUM_LAG or not isinstance(j, int)
                    if u % 4 == 0:
                        v.wait_ge(s["summed"], step + HOT_AHEAD - 12 + SUM_SLOTS)
                        one_hot_of_four(v, T, hot, step + HOT_AHEAD, u + HOT_AHEAD).then_inc(s["hot"], 1)
                        e = load_four(nc, v, e_regs, T["e"], step, ETILES - 1)
                    weigh(step, u, j, e[u % 4])
                    if adds:
                        if u % 4 == 0:
                            n = load_four(nc, v, n_regs, T["n"], step - SUM_LAG, NT - 1)
                        add(step - SUM_LAG, u - SUM_LAG, n[u % 4])

            for k in range(0, HOT_AHEAD, 4):
                one_hot_of_four(v, T, hot, k, k).then_inc(s["hot"], 1)
            blocks_of_steps(v, steps)
            n = load_four(nc, v, n_regs, T["n"], STEPS - SUM_LAG, NT - 1)
            for k in range(SUM_LAG):
                add(STEPS - SUM_LAG + k, k - SUM_LAG, n[k])


def fold(nc, G, name, jobs):
    sems = {f"load{n}": 0 for n in range(len(jobs))}
    with phase(nc, name, dict(spread=0, ps=0, out=1, **sems)) as (block, s, sb, ps):
        W = [sb(f"W{n}", [128, HALVES, D]) for n in range(len(jobs))]
        bc = [sb(f"b{n}", [128, HALVES]) for n in range(len(jobs))]
        bb = [sb(f"bb{n}", [128, HALVES, TP]) for n in range(len(jobs))]
        psW, psb = ps("W"), ps("b")

        @block.sync
        def _(sp):
            for n, (Wd, bd, _, _, _) in enumerate(jobs):
                sp.dma_start(W[n][:], Wd.rearrange("(c p) i -> p c i", p=128)).then_inc(s[f"load{n}"], 16)
                sp.dma_start(bc[n][:], bd.rearrange("(c p) -> p c", p=128),
                             allow_slow_non_contiguous=True).then_inc(s[f"load{n}"], 16)

        @block.vector
        def _(v):
            for n, (_, _, _, out, row) in enumerate(jobs):
                v.wait_ge(s[f"load{n}"], 32)
                for c in range(HALVES):
                    last = v.tensor_scalar(bb[n][:, c, :], G["ones"][:, 0:TP], bc[n][:, c:c + 1], None, ALU.mult)
                last.then_inc(s["spread"], 1)
                v.wait_ge(s["ps"], n + 1)
                v.tensor_copy(out, psW[:, 0, :].rearrange("p (m o) -> p m o", m=HALVES))
                v.tensor_copy(row, psb[0:TP, 0, 0:D]).then_inc(s["out"], 1)

        @block.tensor
        def _(pe):
            for n, (_, _, R, _, _) in enumerate(jobs):
                pe.wait_ge(s[f"load{n}"], 32)
                pe.wait_ge(s["spread"], n + 1)
                pe.wait_ge(s["out"], n + 1)
                for c in range(HALVES):
                    r = G["ident"][:] if R is None else R[:, c, :]
                    for m in range(HALVES):
                        pe.matmul(psW[:, 0, m * D + c * 128:m * D + (c + 1) * 128], W[n][:, c, m * 128:(m + 1) * 128],
                                  r, start=True, stop=True)
                    last = pe.matmul(psb[0:TP, 0, c * 128:(c + 1) * 128], bb[n][:, c, :], r, start=True, stop=True)
                last.then_inc(s["ps"], 1)


class EdgeSums:
    SEMS = dict(e_row0=0, e_row1=0, e_same=0, e_dup=0, e_idx=2, e_didx=0, e_mm=GROUP, e_evac=1)

    def __init__(self, nc, G):
        self.G, self.T, self.hold = G, None, G["hold"]
        self.landed = [G["semaphore"](f"edge_landed{n}") for n in range(2 * GROUP)]
        self.stored = [G["semaphore"](f"edge_stored{n}") for n in range(GROUP)]
        self.acc = [G["dram"](f"edge_sums{n}", [ACC_ROWS, D + 1]) for n in range(REPLICAS)]

    def zeros(self, nc):
        self.clear_parts = GROUP // REPLICAS
        self.clear_cols = ACC_ROWS // self.clear_parts * (D + 1)
        self.clear_rows = next(p for p in range(128, 0, -1) if self.clear_cols % p == 0)
        self.zeroed = self.G["semaphore"]("edge_zeroed")
        return nc.sbuf_tensor("e_zero", [self.clear_rows, self.clear_cols // self.clear_rows], F32)

    def clear(self, pool):
        zero, cols, parts = self.zero, self.clear_cols, self.clear_parts
        pool.memset(zero[:], 0.0).then_inc(self.zeroed, 1)
        pool.wait_ge(self.zeroed, 1)
        for k in range(GROUP):
            a = self.acc[k // parts].rearrange("r c -> (r c)")
            part = k % parts
            pool.dma_start(a[part * cols:(part + 1) * cols].rearrange("(p n) -> p n", p=self.clear_rows),
                           zero[:]).then_inc(self.stored[k], 16)
        for k in range(GROUP):
            pool.wait_ge(self.stored[k], 16)

    def buffers(self, s, sb, ps):
        self.s = s
        self.srow = sb("e_srow", [EP, 2, GROUP * EP], I32)
        self.didx, self.sidx = sb("e_didx", [EP, 2, GROUP], I32), sb("e_sidx", [EP, 2, GROUP], I32)
        self.same, self.junk = sb("e_same", [EP, GROUP, EP]), sb("e_junk", [EP, GROUP, EP])
        self.dup, self.tmp = sb("e_dup", [EP, GROUP]), sb("e_tmp", [EP, GROUP])
        self.rows = sb("e_rows", [EP, 2, GROUP, D + 1])
        self.comb = sb("e_comb", [EP, GROUP, D + 1])
        self.bank = ps("e_bank")

    def source_rows(self, sp, l, p, b):
        self.hold(sp, self.s["e_idx"], p + 1)
        src = self.G["src_tiles"].rearrange("(g t) e -> g (t e)", t=GROUP)
        sp.dma_start(self.srow[:, b, :], src[bass.ds(PAIRS * l + p, 1), :].to_broadcast([EP, GROUP * EP])
                     ).then_inc(self.s[f"e_row{b}"], 16)

    def gather_indices(self, v, l, p, b):
        if not isinstance(p, int) or p:
            self.hold(v, self.s["e_mm"], GROUP * p)
        v.tensor_copy(self.didx[:, b, :], self.T["dst_all"][:, bass.ds(GROUP * (PAIRS * l + p), GROUP)]
                      ).then_inc(self.s["e_didx"], 1)

    def begin(self, v, l):
        v.memset(self.rows[:, :, :, D:D + 1], 1.0).then_inc(self.s["e_dup"], 1)
        self.gather_indices(v, l, 0, 0)

    def compare(self, v, l, p, b):
        T, s, first = self.T, self.s, GROUP * (PAIRS * l + p)
        v.wait_ge(s[f"e_row{b}"], 16 * (p // 2) + 16)
        for u in range(GROUP):
            v.wait_ge(s["e_mm"], GROUP * p + u + 1)
            v.tensor_scalar(self.same[:, u, :], self.srow[:, b, u * EP:(u + 1) * EP],
                            T["src_all"][:, bass.ds(first + u, 1)], None, ALU.is_equal).then_inc(s["e_same"], 1)
        self.gather_indices(v, l, p + 1, 1 - b)
        v.wait_ge(s["e_dup"], 5 * p + 1)
        for u in range(GROUP):
            v.wait_ge(s["e_same"], GROUP * p + u + 1)
            ins = v.tensor_tensor_reduce(out=self.junk[:, u, :], in0=self.same[:, u, :], in1=self.G["below"][:],
                                         scale=1.0, scalar=0.0, op0=ALU.mult, op1=ALU.add,
                                         accum_out=self.dup[:, u:u + 1])
        ins.then_inc(s["e_dup"], 1)
        v.wait_ge(s["e_dup"], 5 * p + 2)
        sources = T["src_all"][:, bass.ds(first, GROUP)]
        v.tensor_scalar(self.dup[:], self.dup[:], 1.0, None, ALU.min).then_inc(s["e_dup"], 1)
        v.tensor_scalar(self.tmp[:], sources, -1.0, self.G["spare"][:, 0:1], ALU.mult, ALU.add).then_inc(s["e_dup"], 1)
        v.wait_ge(s["e_dup"], 5 * p + 4)
        v.tensor_tensor(self.tmp[:], self.tmp[:], self.dup[:], ALU.mult).then_inc(s["e_dup"], 1)
        v.wait_ge(s["e_dup"], 5 * p + 5)
        v.wait_ge(s["e_evac"], GROUP * p + 1)
        v.tensor_tensor(self.sidx[:, b, :], self.tmp[:], sources, ALU.add).then_inc(s["e_dup"], 1)
        v.wait_ge(s["e_dup"], 5 * p + 6)
        v.sem_inc(s["e_idx"], 1)

    def gather(self, pool, p, b, u):
        if u == 0:
            self.hold(pool, self.s["e_didx"], p + 1)
            pool.wait_ge(self.s["e_dup"], 1)
        self.hold(pool, self.s["e_mm"], GROUP * p + u + 1 - GROUP if not isinstance(p, int) or p else 1)
        pool.indirect_dma_start(self.rows[:, b, u, 0:D], None, self.G["xn_d"],
                                bass.IndirectOffsetOnAxis(ap=self.didx[:, b, u:u + 1], axis=0)).then_inc(self.landed[b * GROUP + u], 16)

    def scatter(self, pool, l, p, b, u):
        g = PAIRS * l + p
        if u == 0:
            self.hold(pool, self.s["e_idx"], p + 3)
        self.hold(pool, self.s["e_evac"], GROUP * p + u + 2)
        if u >= REPLICAS:
            self.hold(pool, self.stored[u - REPLICAS], 16 * g + 32)
        else:
            self.hold(pool, self.stored[u + GROUP - REPLICAS], 16 * g + 16)
        pool.indirect_dma_start(self.acc[u % REPLICAS], bass.IndirectOffsetOnAxis(ap=self.sidx[:, b, u:u + 1], axis=0),
                                self.comb[:, u, :], None, compute_op=ALU.add).then_inc(self.stored[u], 16)

    def move(self, pool, l, p, b):
        for u in range(GROUP):
            self.gather(pool, p + 1, 1 - b, u)
            self.scatter(pool, l, p, b, u)

    def product(self, pe, l, p, b, u):
        pe.wait_ge(self.landed[b * GROUP + u], 16 * ((PAIRS // 2 + 1 - b) * l + p // 2 + 1))
        pe.wait_ge(self.s["e_same"], GROUP * p + u + 1)
        pe.wait_ge(self.s["e_evac"], GROUP * p + u + 1)
        pe.matmul(self.bank[:, 0, 0:D + 1], self.same[:, u, :], self.rows[:, b, u, :], start=True, stop=True
                  ).then_inc(self.s["e_mm"], 1)

    def evacuate(self, act, l, p, u):
        act.wait_ge(self.s["e_mm"], GROUP * p + u + 1 + GROUP)
        act.wait_ge(self.stored[u], 16 * (PAIRS * l + p) + 16)
        act.copy(self.comb[:, u, :], self.bank[:, 0, 0:D + 1]).then_inc(self.s["e_evac"], 1)


def graph0_dense(nc, G, edges):
    A, hold, X = G["A"], G["hold"], G["X"]
    x_v = A["x"].rearrange("(n t p) d -> n p t d", t=2, p=TP)
    xn_v = G["xn_d"].rearrange("(n t p) d -> n p t d", t=2, p=TP)
    sums_v = [a[0:NODES].rearrange("(n t p) d -> n p t d", t=2, p=TP) for a in edges.acc]
    with ExitStack() as ctx:
        def sbuf(n, shape):
            return ctx.enter_context(nc.sbuf_tensor(n, shape, F32))
        W1T, W2T = sbuf("g0_W1T", [128, HALVES, D]), sbuf("g0_W2T", [128, HALVES, D])
        b1, b2 = sbuf("g0_b1", [TP, D]), sbuf("g0_b2", [TP, D])
        fold(nc, G, "g0_fold", [(A["L0_gnn_W1"], A["L0_gnn_b1"], None, W1T[:], b1[:]),
                                (A["L0_gnn_W2"], A["L0_gnn_b2"], None, W2T[:], b2[:])])
        sems = dict(in0=0, in1=0, step=0, turned=2, hT=2, o=2, biased=2, x_done=2, both=0, mean=1)
        with phase(nc, "g0", sems) as (block, s, sb, ps):
            cinv = sb("cinv", [TP, 2])
            sums = sb("sums", [TP, 2, REPLICAS, 2, D + 1])
            total, mean = sb("total", [TP, 2, D + 1]), sb("mean", [TP, 2, 2, D])
            hT = sb("hT", [128, 2, 2, HALVES, PT])
            xin, xn, bb = sb("xin", [TP, 2, 2, D]), sb("xn", [TP, 2, 2, D]), sb("bb", [TP, D])
            psT, o = ps("psT", 4), ps("o", 2)

            @block.sync
            def _(sp):
                def load(p, b):
                    hold(sp, s["biased"], p + 1)
                    hold(sp, s["turned"], p + 1)
                    for dst, src in ((xin[:, b], x_v), (xn[:, b], xn_v), (sums[:, b, 0], sums_v[0]),
                                     (sums[:, b, 1], sums_v[1])):
                        sp.dma_start(dst, src[bass.ds(p, 1)].rearrange("n p t d -> (n p) t d")).then_inc(s[f"in{b}"], 16)
                pairs(sp, load)

            @block.gpsimd
            def _(pool):
                pool.tensor_tensor(bb[:], b1[:], b2[:], ALU.add).then_inc(s["both"], 1)
                pool.wait_ge(s["both"], 1)

                def bias(p, b):
                    Xp = pair_of(X, p)
                    hold(pool, s[f"in{b}"], 64 * (p // 2) + 64)
                    pool.tensor_tensor(Xp, Xp, xin[:, b], ALU.add).then_inc(s["both"], 1)
                    hold(pool, s["both"], p + 2)
                    pool.tensor_tensor(Xp, Xp, bb[:].unsqueeze(1).to_broadcast([TP, 2, D]), ALU.add
                                       ).then_inc(s["biased"], 1)
                pairs(pool, bias)

            @block.vector
            def _(v):
                def means(p, b):
                    v.wait_ge(s[f"in{b}"], 64 * (p // 2) + 64)
                    v.wait_ge(s["mean"], p + 1)
                    v.tensor_tensor(total[:], sums[:, b, 0], sums[:, b, 1], ALU.add).then_inc(s["step"], 1)
                    v.wait_ge(s["step"], 3 * p + 1)
                    v.tensor_scalar(cinv[:], total[:, :, D], 1.0, None, ALU.max).then_inc(s["step"], 1)
                    v.wait_ge(s["step"], 3 * p + 2)
                    v.reciprocal(cinv[:], cinv[:]).then_inc(s["step"], 1)
                    v.wait_ge(s["step"], 3 * p + 3)
                    v.wait_ge(s["turned"], p + 1)
                    for t in range(2):
                        last = v.tensor_scalar(mean[:, b, t, :], total[:, t, 0:D], cinv[:, t:t + 1], None, ALU.mult)
                    last.then_inc(s["mean"], 1)

                def add(p, b):
                    v.wait_ge(s["biased"], p + 3)
                    add_and_stats(v, G, s, o[0:TP, b].rearrange("p (t d) -> p t d", t=2), p, 2)
                pairs(v, add, early=means)

            @block.tensor
            def _(pe):
                def turn(p, b):
                    pe.wait_ge(s["mean"], p + 2)
                    pe.wait_ge(s["hT"], p + 1)
                    for k, src in enumerate((xn, mean)):
                        for c in range(HALVES):
                            for t in range(2):
                                last = pe.transpose(psT[:, 2 * b + k, c * PT + t * TP:c * PT + (t + 1) * TP],
                                                    src[:, b, t, c * 128:(c + 1) * 128], G["ident"][0:TP, 0:TP])
                    last.then_inc(s["turned"], 1)

                def products(p, b):
                    pe.wait_ge(s["hT"], p + 3)
                    pe.wait_ge(s["x_done"], p + 1)
                    for t in range(2):
                        for k, w in enumerate((W1T, W2T)):
                            for c in range(HALVES):
                                last = pe.matmul(o[0:TP, b, t * D:(t + 1) * D], hT[:, b, k, c, t * TP:(t + 1) * TP],
                                                 w[:, c, :], start=(k + c == 0), stop=(k + c == 2))
                    last.then_inc(s["o"], 1)
                pairs(pe, products, turn)

            @block.scalar
            def _(act):
                def evacuate(p, b):
                    act.wait_ge(s["turned"], p + 3)
                    act.wait_ge(s["o"], p + 1)
                    for k in range(2):
                        last = act.copy(hT[:, b, k], psT[:, 2 * b + k, 0:2 * PT].rearrange("p (c t) -> p c t", c=HALVES))
                    last.then_inc(s["hT"], 1)
                pairs(act, evacuate)


EXPERTS, TOP = 4, 2


def row_of(b, width):
    return b.rearrange("(a d) -> a d", a=1).to_broadcast([TP, width])


def experts(nc, G):
    A, hold, X = G["A"], G["hold"], G["X"]
    S1, E1, S2, E2, BLOCKS, BANKS = 0, 2, 6, 7, 9, 3
    sems = dict(weights=0, const=0, gate_read=1, blk=0, blk_done=BANKS, gate_ps=0, gate=0, gate_exp=0, gate_w=0, w_turned=2, w_sb=1,
                spread=0, scaled=0, o=2, x_done=2, **hT_sems())
    with phase(nc, "moe", sems) as (block, s, sb, ps):
        sW1, sW2, sW3 = sb("sW1", [128, HALVES, D]), sb("sW2", [128, HALVES, 128]), sb("sW3", [128, D])
        eW1, eW2 = sb("eW1", [128, EXPERTS, HALVES, 128]), sb("eW2", [128, EXPERTS, 64])
        eW3, b3 = sb("eW3", [128, 2, D]), sb("b3", [EXPERTS + 1, D])
        bias = sb("bias", [128, BLOCKS])
        gW, gb = sb("gW", [128, HALVES, EXPERTS]), sb("gb", [TP, EXPERTS])
        sel = sb("sel", [EXPERTS + 1, 2, 2, 64])
        before = sb("before", [TP, EXPERTS, EXPERTS])
        h, hT = sb("h", [TP, 2, 2, D]), sb("hT", [128, 2, HALVES, PT])
        hid, gated = sb("hid", [128, BLOCKS, PT]), sb("gated", [128, 2, PT])
        g, ge, d = sb("g", [TP, 2, EXPERTS]), sb("ge", [TP, 2, EXPERTS]), sb("d", [TP, 2, EXPERTS])
        m, z = sb("m", [TP, 2]), sb("z", [TP, 2])
        gt, eq = sb("gt", [TP, 2, EXPERTS, EXPERTS]), sb("eq", [TP, 2, EXPERTS, EXPERTS])
        w5, w5T = sb("w5", [TP, 2, 2, EXPERTS + 1]), sb("w5T", [EXPERTS + 1, PT])
        psT, ring, gate_bank, spread, o = ps("psT"), ps("ring", BANKS), ps("gate"), ps("spread"), ps("o", 2)
        logits = gate_bank[0:TP, 0, 0:2 * EXPERTS].rearrange("p (t e) -> p t e", t=2)
        LOADS_N = 5 + EXPERTS + 9

        @block.sync
        def _(sp):
            def col(v, n):
                return v.rearrange("(c p) -> p c", p=128)[:, n:n + 1]
            loads = [(sW1[:], A["L0_ffn_sW1"].rearrange("(c p) h -> p c h", p=128)),
                     (sW2[:], A["L0_ffn_sW2"].rearrange("(c p) h -> p c h", p=128)),
                     (sW3[:], A["L0_ffn_sW3"]),
                     (eW2[:], A["L0_ffn_eW2"].rearrange("e p g -> p e g")),
                     (eW3[:], A["L0_ffn_eW3"].rearrange("(r e) g o -> (e g) r o", e=2))]
            loads += [(eW1[:, e], A["L0_ffn_eW1"][e].rearrange("(c p) h -> p c h", p=128)) for e in range(EXPERTS)]
            loads += [(b3[0:EXPERTS, :], A["L0_ffn_eb3"]),
                      (b3[EXPERTS:EXPERTS + 1, :], A["L0_ffn_sb3"].rearrange("(a d) -> a d", a=1)),
                      (gW[:], A["L0_ffn_gW"].rearrange("(c p) e -> p c e", p=128)),
                      (gb[:], row_of(A["L0_ffn_gb"], EXPERTS)),
                      (bias[:, S1:S1 + 2], A["L0_ffn_sb1"].rearrange("(c p) -> p c", p=128)),
                      (bias[:, E1:E1 + EXPERTS], A["L0_ffn_eb1"].rearrange("e p -> p e")),
                      (bias[:, S2:S2 + 1], A["L0_ffn_sb2"].rearrange("(c p) -> p c", p=128)),
                      (bias[0:64, E2:E2 + 2], A["L0_ffn_eb2"].rearrange("(r e) g -> e g r", e=2)[0]),
                      (bias[64:128, E2:E2 + 2], A["L0_ffn_eb2"].rearrange("(r e) g -> e g r", e=2)[1])]
            assert len(loads) == LOADS_N
            for dst, src in loads:
                sp.dma_start(dst, src, allow_slow_non_contiguous=True).then_inc(s["weights"], 16)

        @block.vector
        def _(v):
            v.memset(w5[:, :, :, EXPERTS:EXPERTS + 1], 1.0)
            v.memset(before[:], 0.0).then_inc(s["const"], 1)
            for k in range(EXPERTS):
                v.tensor_copy(sel[:, k // 2, k % 2, :], G["ident"][0:EXPERTS + 1, k:k + 1].to_broadcast([EXPERTS + 1, 64]))
            v.wait_ge(s["const"], 1)
            for e in range(1, EXPERTS):
                last = v.memset(before[:, e, 0:e], 1.0)
            last.then_inc(s["const"], 1)
            v.wait_ge(s["const"], 2)
            v.wait_ge(s["weights"], 16 * LOADS_N)

            OPS = 15

            def gates(p, b):
                done = [0]

                def step(ins):
                    done[0] += 1
                    ins.then_inc(s["gate"], 1)
                    v.wait_ge(s["gate"], OPS * p + done[0])

                def over_e(t):
                    return t.unsqueeze(2).to_broadcast([TP, 2, EXPERTS])
                v.wait_ge(s["gate_ps"], p + 1)
                step(v.tensor_tensor(g[:], logits, gb[:].unsqueeze(1).to_broadcast([TP, 2, EXPERTS]), ALU.add))
                v.sem_inc(s["gate_read"], 1)
                step(v.tensor_reduce(m[:], g[:], X_AXIS, ALU.max))
                v.tensor_tensor(d[:], g[:], over_e(m[:]), ALU.subtract).then_inc(s["gate_w"], 1)
                v.wait_ge(s["gate_exp"], 2 * p + 1)
                step(v.tensor_reduce(z[:], ge[:], X_AXIS, ALU.add))
                step(v.reciprocal(z[:], z[:]))
                step(v.tensor_tensor(g[:], ge[:], over_e(z[:]), ALU.mult))
                of_j = g[:].unsqueeze(2).to_broadcast([TP, 2, EXPERTS, EXPERTS])
                of_e = g[:].unsqueeze(3).to_broadcast([TP, 2, EXPERTS, EXPERTS])
                v.tensor_tensor(gt[:], of_j, of_e, ALU.is_gt)
                step(v.tensor_tensor(eq[:], of_j, of_e, ALU.is_equal))
                step(v.tensor_tensor(eq[:], eq[:], before[:].unsqueeze(1).to_broadcast([TP, 2, EXPERTS, EXPERTS]), ALU.mult))
                step(v.tensor_tensor(gt[:], gt[:], eq[:], ALU.add))
                step(v.tensor_reduce(d[:], gt[:], X_AXIS, ALU.add))
                step(v.tensor_scalar(d[:], d[:], float(TOP), None, ALU.is_lt))
                step(v.tensor_reduce(m[:], g[:], X_AXIS, ALU.max))
                v.tensor_tensor(g[:], g[:], over_e(m[:]), ALU.subtract).then_inc(s["gate_w"], 1)
                v.wait_ge(s["gate_exp"], 2 * p + 2)
                step(v.tensor_tensor(d[:], d[:], ge[:], ALU.mult))
                step(v.tensor_reduce(z[:], d[:], X_AXIS, ALU.add))
                step(v.reciprocal(z[:], z[:]))
                v.wait_ge(s["w_turned"], p + 1)
                step(v.tensor_tensor(w5[:, b, :, 0:EXPERTS], d[:], over_e(z[:]), ALU.mult))
                assert done[0] == OPS

            def main(p, b):
                v.wait_ge(s["spread"], p + 1)
                v.wait_ge(s["blk_done"], BLOCKS * p + BLOCKS + BANKS)
                v.tensor_tensor(gated[:], hid[:, E2:E2 + 2, :], spread[:, 0, 0:2 * PT].rearrange("p (r t) -> p r t", r=2),
                                ALU.mult).then_inc(s["scaled"], 1)
                if not isinstance(p, int) or p + 1 < PAIRS:
                    gates(p + 1, 1 - b)
                add_and_stats(v, G, s, o[0:TP, b].rearrange("p (t d) -> p t d", t=2), p, 2)
            def early(p, b):
                normalise_pair(v, G, s, h, p, b)
                if isinstance(p, int) and p == 1:
                    gates(0, 0)
            pairs(v, main, early=early)

        @block.scalar
        def _(act):
            act.wait_ge(s["weights"], 16 * LOADS_N)

            def relu(p, n):
                act.wait_ge(s["blk"], BLOCKS * p + n + 1)
                act.activation(hid[:, n, :], ring[:, n % BANKS, 0:PT], ACT.Relu, bias=bias[:, n:n + 1]
                               ).then_inc(s["blk_done"], 1)

            def main(p, b):
                for n in range(E1 + EXPERTS):
                    relu(p, n)
                act.wait_ge(s["w_turned"], p + 3)
                act.copy(w5T[:], o[0:EXPERTS + 1, b, 0:PT]).then_inc(s["w_sb"], 1)
                for n in range(S2, BLOCKS):
                    relu(p, n)
                if not isinstance(p, int) or p + 1 < PAIRS:
                    exponentials(p + 1)

            def exponentials(p):
                act.wait_ge(s["gate_w"], 2 * p + 1)
                act.activation(ge[:], d[:], ACT.Exp).then_inc(s["gate_exp"], 1)
                act.wait_ge(s["gate_w"], 2 * p + 2)
                act.activation(ge[:], g[:], ACT.Exp).then_inc(s["gate_exp"], 1)

            def ahead(p, b):
                affine_evacuate(act, s, psT, hT, None, None, p, b, (s["o"], p + 1))
                if isinstance(p, int) and p == 0:
                    exponentials(0)
            pairs(act, main, ahead)

        @block.tensor
        def _(pe):
            pe.wait_ge(s["weights"], 16 * LOADS_N)
            pe.wait_ge(s["const"], 2)

            def logits_of(p, b):
                pe.wait_ge(s["hT_ready"], p + 2)
                pe.wait_ge(s["gate_read"], p + 1)
                for t in range(2):
                    for c in range(HALVES):
                        mm = pe.matmul(gate_bank[0:TP, 0, t * EXPERTS:(t + 1) * EXPERTS],
                                       hT[:, b, c, t * TP:(t + 1) * TP], gW[:, c, :], start=(c == 0), stop=(c == 1))
                mm.then_inc(s["gate_ps"], 1)

            def main(p, b):
                x = [hT[:, b, c, :] for c in range(HALVES)]

                def blk(n, products):
                    pe.wait_ge(s["blk_done"], BLOCKS * p + n + 1)
                    for lo, hi, k, last_k, w, r in products:
                        mm = pe.matmul(ring[lo:hi, n % BANKS, 0:PT], w, r, start=(k == 0), stop=(k == last_k))
                    mm.then_inc(s["blk"], 1)
                for n in range(2):
                    blk(S1 + n, [(0, 128, c, 1, sW1[:, c, n * 128:(n + 1) * 128], x[c]) for c in range(HALVES)])
                for e in range(EXPERTS):
                    blk(E1 + e, [(0, 128, c, 1, eW1[:, e, c, :], x[c]) for c in range(HALVES)])
                if not isinstance(p, int) or p + 1 < PAIRS:
                    logits_of(p + 1, 1 - b)
                pe.wait_ge(s["gate"], 15 * p + 15)
                pe.wait_ge(s["x_done"], p + 1)
                pe.wait_ge(s["w_sb"], p + 1)
                for t in range(2):
                    mm = pe.transpose(o[0:EXPERTS + 1, b, t * TP:(t + 1) * TP], w5[:, b, t, :],
                                      G["ident"][0:TP, 0:TP])
                mm.then_inc(s["w_turned"], 1)
                blk(S2, [(0, 128, c, 1, sW2[:, c, :], hid[:, S1 + c, :]) for c in range(HALVES)])
                pe.wait_ge(s["blk_done"], BLOCKS * p + 6 + BANKS)
                for r in range(2):
                    blk(E2 + r, [(64 * k, 64 * k + 64, 0, 0, eW2[:, 2 * r + k, :], hid[:, E1 + 2 * r + k, :]) for k in range(2)])
                pe.wait_ge(s["w_sb"], p + 2)
                for r in range(2):
                    mm = pe.matmul(spread[:, 0, r * PT:(r + 1) * PT], sel[:, r].rearrange("k e g -> k (e g)"), w5T[:],
                                   start=True, stop=True)
                mm.then_inc(s["spread"], 1)
                pe.wait_ge(s["scaled"], p + 1)
                for t in range(2):
                    cols = slice(t * TP, (t + 1) * TP)
                    for k, (l, r) in enumerate(((hid[:, S2, cols], sW3[:]), (w5T[:, cols], b3[:]),
                                                (gated[:, 0, cols], eW3[:, 0, :]), (gated[:, 1, cols], eW3[:, 1, :]))):
                        mm = pe.matmul(o[0:TP, b, t * D:(t + 1) * D], l, r, start=(k == 0), stop=(k == 3))
                mm.then_inc(s["o"], 1)
            def ahead(p, b):
                turn_pair(pe, G, s, h, psT, p, b)
                if isinstance(p, int) and p == 0:
                    logits_of(0, 0)
            pairs(pe, main, ahead)


MW = 128


class Layer1:

    def __init__(self, nc, G, ctx):
        def keep(n, shape):
            return ctx.enter_context(nc.sbuf_tensor("l1_" + n, shape, F32))
        self.WqT, self.WkT, self.WvT = (keep(n, [128, HALVES, D]) for n in ("WqT", "WkT", "WvT"))
        self.WaT = keep("WaT", [128, HALVES, D])
        self.bq, self.bk, self.bv, self.ba = (keep(n, [TP, D]) for n in ("bq", "bk", "bv", "ba"))
        self.keep_h = keep("keep_h", [128, 1])
        self.Wm, self.WqmT = keep("Wm", [128, HALVES, 3 * MW]), keep("WqmT", [128, D])
        self.Wmo, self.Gm = keep("Wmo", [128, 1, D]), keep("Gm", [128, HALVES, D])
        A = G["A"]
        with ExitStack() as tmp:
            def sbuf(n, shape):
                return tmp.enter_context(nc.sbuf_tensor("l1_" + n, shape, F32))
            att, msg, scale, gain = (sbuf(n, [128, HALVES, 128]) for n in ("att", "msg", "scale", "gain"))
            with phase(nc, "l1prep", dict(clear=0, load=0, v=0, act=0, turned=0)) as (block, s, sb, ps):
                pri, alpha, bo = sb("pri", [128, HALVES]), sb("alpha", [128, 1]), sb("bo", [TP, D])
                tp = ps("tp")
                heads = D // HEAD

                @block.sync
                def _(sp):
                    sp.wait_ge(s["clear"], 2)
                    for k in range(heads):
                        c, r = divmod(k, 128 // HEAD)
                        rows = slice(r * HEAD, (r + 1) * HEAD)
                        sp.dma_start(att[rows, c, rows], A["L1_gnn_rel_att"][k]).then_inc(s["load"], 16)
                        sp.dma_start(msg[rows, c, rows], A["L1_gnn_rel_msg"][k]).then_inc(s["load"], 16)
                        sp.dma_start(pri[rows, c:c + 1], A["L1_gnn_rel_pri"][k:k + 1].rearrange("(a d) -> a d", a=1)
                                     .to_broadcast([HEAD, 1]), allow_slow_non_contiguous=True).then_inc(s["load"], 16)
                    sp.dma_start(alpha[:], A["L1_gnn_skip"].rearrange("(a d) -> a d", a=1).to_broadcast([128, 1]),
                                 allow_slow_non_contiguous=True).then_inc(s["load"], 16)
                    sp.dma_start(self.Wm[:], A["L1_mix_W_qkv"].rearrange("(c p) n -> p c n", p=128)).then_inc(s["load"], 16)
                    sp.dma_start(self.Wmo[:, 0, :], A["L1_mix_W_out"]).then_inc(s["load"], 16)

                @block.vector
                def _(v):
                    v.memset(att[:], 0.0).then_inc(s["clear"], 1)
                    v.memset(msg[:], 0.0).then_inc(s["clear"], 1)
                    v.wait_ge(s["act"], 1)
                    v.tensor_scalar(alpha[:], alpha[:], 1.0, None, ALU.add).then_inc(s["v"], 1)
                    v.wait_ge(s["v"], 1)
                    v.reciprocal(alpha[:], alpha[:]).then_inc(s["v"], 1)
                    v.wait_ge(s["v"], 2)
                    v.tensor_scalar(self.keep_h[:], alpha[:], -1.0, 1.0, ALU.mult, ALU.add)
                    for c in range(HALVES):
                        v.tensor_scalar(gain[:, c, :], G["ident"][:], alpha[:], None, ALU.mult)
                        v.tensor_scalar(scale[:, c, :], G["ident"][:], pri[:, c:c + 1], HEAD ** -0.5, ALU.mult, ALU.mult)
                    v.wait_ge(s["turned"], 1)
                    v.tensor_copy(self.WqmT[:], tp[:, 0, 0:D])

                @block.scalar
                def _(act):
                    act.wait_ge(s["load"], 16 * (3 * heads + 3))
                    act.activation(alpha[:], alpha[:], ACT.Exp, scale=-1.0).then_inc(s["act"], 1)

                @block.tensor
                def _(pe):
                    pe.wait_ge(s["load"], 16 * (3 * heads + 3))
                    for c in range(HALVES):
                        mm = pe.transpose(tp[:, 0, c * 128:(c + 1) * 128], self.Wm[:, c, 0:MW], G["ident"][:])
                    mm.then_inc(s["turned"], 1)
            fold(nc, G, "l1_fold", [
                (A["L1_gnn_Wq"], A["L1_gnn_bq"], scale, self.WqT[:], self.bq[:]),
                (A["L1_gnn_Wk"], A["L1_gnn_bk"], att, self.WkT[:], self.bk[:]),
                (A["L1_gnn_Wv"], A["L1_gnn_bv"], msg, self.WvT[:], self.bv[:]),
                (A["L1_gnn_Wa"], A["L1_gnn_ba"], gain, self.WaT[:], self.ba[:])])


def project1(nc, G, L, Q, k_d, v_d, MK, MV, kmax):
    hold = G["hold"]
    k_v, v_v = (t.rearrange("(n t p) d -> n p t d", t=2, p=TP) for t in (k_d, v_d))
    sems = dict(q_ps=0, k_ps=0, v_ps=0, m_ps=2, q_read=1, k_read=1, v_read=1, m_read=1, kmax=0,
                out0=32, out1=32, **hT_sems())
    with phase(nc, "proj1", sems) as (block, s, sb, ps):
        h, hT = sb("h", [TP, 2, 2, D]), sb("hT", [128, 2, HALVES, PT])
        kv = sb("kv", [TP, 2, 2, 2, D])
        psT, qp, kp, vp, mp = ps("psT"), ps("q"), ps("k"), ps("v"), ps("m")

        def of_pair(bank):
            return bank[0:TP, 0].rearrange("p (t d) -> p t d", t=2)

        @block.sync
        def _(sp):
            def save(p, b):
                for n, (free, dst) in enumerate((("k_read", k_v), ("v_read", v_v))):
                    hold(sp, s[free], p + 2)
                    sp.dma_start(dst[bass.ds(p, 1)].rearrange("n p t d -> (n p) t d"), kv[:, b, n]).then_inc(s[f"out{b}"], 16)
            pairs(sp, save)
            sp.wait_ge(s["out0"], 32 * (PAIRS // 2 + 2))
            sp.wait_ge(s["out1"], 32 * (PAIRS // 2 + 1))

        @block.vector
        def _(v):
            v.memset(MV[:, :, :, MW:MW + 1], 1.0)
            v.memset(kmax[:], -BIG).then_inc(s["kmax"], 1)

            def main(p, b):
                v.wait_ge(s["q_ps"], p + 1)
                v.tensor_tensor(pair_of(Q, p), of_pair(qp), L.bq[:].unsqueeze(1).to_broadcast([TP, 2, D]), ALU.add
                                ).then_inc(s["q_read"], 1)
                v.wait_ge(s[f"out{b}"], 32 * (p // 2) + 32)
                for n, (bank, row, ready, read) in enumerate(((kp, L.bk, "k_ps", "k_read"), (vp, L.bv, "v_ps", "v_read"))):
                    v.wait_ge(s[ready], p + 1)
                    v.tensor_tensor(kv[:, b, n], of_pair(bank), row[:].unsqueeze(1).to_broadcast([TP, 2, D]), ALU.add
                                    ).then_inc(s[read], 1)
                v.wait_ge(s["m_read"], p + 2)
                v.wait_ge(s["kmax"], p + 1)
                v.tensor_tensor(kmax[:], kmax[:], pair_of(MK, p), ALU.max).then_inc(s["kmax"], 1)
            pairs(v, main, early=lambda p, b: normalise_pair(v, G, s, h, p, b))

        @block.scalar
        def _(act):
            def main(p, b):
                m = of_pair(mp)
                hold(act, s["m_ps"], p + 3)
                act.copy(pair_of(MK, p), m[:, :, 0:MW])
                act.copy(MV[:, bass.ds(2 * p, 2), 0, 0:MW], m[:, :, MW:2 * MW]).then_inc(s["m_read"], 1)
            pairs(act, main, lambda p, b: affine_evacuate(act, s, psT, hT, None, None, p, b, (s["m_ps"], p + 1)))

        @block.tensor
        def _(pe):
            def main(p, b):
                pe.wait_ge(s["hT_ready"], p + 2)
                for bank, w, cols, ready, read in ((qp, L.WqT, slice(0, D), "q_ps", "q_read"), (kp, L.WkT, slice(0, D), "k_ps", "k_read"),
                                                   (vp, L.WvT, slice(0, D), "v_ps", "v_read"),
                                                   (mp, L.Wm, slice(MW, 3 * MW), "m_ps", "m_read")):
                    pe.wait_ge(s[read], p + 1)
                    for t in range(2):
                        for c in range(HALVES):
                            mm = pe.matmul(bank[0:TP, 0, t * D:(t + 1) * D], hT[:, b, c, t * TP:(t + 1) * TP],
                                           w[:, c, cols], start=(c == 0), stop=(c == 1))
                    mm.then_inc(s[ready], 1)
            pairs(pe, main, lambda p, b: turn_pair(pe, G, s, h, psT, p, b))


H1 = D // HEAD
LIST = CHUNK_TILES * EP


def alternating(eng, n, main):
    with eng.Fori(0, n // 2) as j:
        for b in range(2):
            main(2 * j + b, b)
    main(n - 1, 0)


SCORE_LAG = 4


def edge_scores(nc, G, T, ring, Q, k_d, SC):
    hold = G["hold"]
    sems = dict(idx=0, clear=0, hot=0, hot_turned=8, hotT=2, q_ps=2, prod=RING, part=2, sum=4)
    with phase(nc, "scores", sems) as (block, s, sb, ps):
        idx = sb("idx", [EP, 4, 4], I32)
        rows = sb("rows", [EP, RING, D])
        hot, hotT = sb("hot", [EP, UNROLL, TP]), sb("hotT", [TP, 2, EP])
        prod, part = sb("prod", [EP, 2, D]), sb("part", [EP, 4, H1])
        turned, qe = ps("turned", 2), ps("qe", 4)

        @block.gpsimd
        def _(pool):
            with pool.Fori(0, STEPS // UNROLL) as j:
                for u in range(UNROLL):
                    if u % 4 == 0:
                        hold(pool, s["idx"], 4 * j + u // 4 + 1)
                    hold(pool, s["prod"], UNROLL * j + u + 1)
                    pool.indirect_dma_start(rows[:, u % RING, :], None, k_d,
                                            bass.IndirectOffsetOnAxis(ap=idx[:, u // 4, u % 4:u % 4 + 1], axis=0)
                                            ).then_inc(ring[u % RING], 16)

        @block.scalar
        def _(act):
            def evacuate(step, slot):
                act.wait_ge(s["hot_turned"], step + 9)
                act.wait_ge(s["q_ps"], step + 1)
                act.copy(hotT[:, slot, :], turned[0:TP, slot, 0:EP]).then_inc(s["hotT"], 1)

            copy_indices(act, T, idx, s, 0, 0)
            copy_indices(act, T, idx, s, 4, 4)
            with act.Fori(0, STEPS // UNROLL) as j:
                for u in range(UNROLL):
                    if u % 4 == 0:
                        hold(act, s["prod"], UNROLL * j + u + 8 - 12 + RING)
                        copy_indices(act, T, idx, s, UNROLL * j + u + 8, u + 8)
                    evacuate(UNROLL * j + u, u % 2)

        @block.tensor
        def _(pe):
            def turn(step, u, j=0):
                if u % 4 == 0:
                    pe.wait_ge(s["hot"], 4 * j + u // 4 + 1)
                pe.wait_ge(s["hotT"], step + 1)
                pe.transpose(turned[0:TP, u % 2, 0:EP], hot[:, u % UNROLL, :], G["ident"][:]).then_inc(s["hot_turned"], 1)

            n_regs = [pe.alloc_register(f"score_n{i}") for i in range(4)]
            turn(0, 0)
            turn(1, 1)
            with pe.Fori(0, STEPS // UNROLL) as j:
                for u in range(UNROLL):
                    step = UNROLL * j + u
                    turn(step + 2, u + 2, j)
                    if u % 4 == 0:
                        n = load_four(nc, pe, n_regs, T["n"], step, NT - 1)
                    pe.wait_ge(s["hotT"], step + 3)
                    pe.wait_ge(s["prod"], step + RING - 3)
                    pe.matmul(qe[:, u % 4, 0:D], hotT[:, u % 2, :], tile_of(Q, n[u % 4]), start=True, stop=True
                              ).then_inc(s["q_ps"], 1)

        @block.vector
        def _(v):
            e_regs = [v.alloc_register(f"score_e{i}") for i in range(4)]
            v.memset(SC[:], 0.0).then_inc(s["clear"], 1)
            v.wait_ge(s["clear"], 1)

            def product(step, u, j):
                v.wait_ge(ring[u % RING], 32 * j + 16 * (u // RING) + 16)
                v.wait_ge(s["q_ps"], step + 3)
                v.wait_ge(s["part"], step + 1)
                v.tensor_tensor(prod[:, u % 2, :], rows[:, u % RING, :], qe[:, u % 4, 0:D], ALU.mult
                                ).then_inc(s["prod"], 1)

            def reduce_heads(step, u):
                v.wait_ge(s["prod"], step + 1 + RING)
                hold(v, s["sum"], step + 1)
                v.tensor_reduce(part[:, u % 4, :], prod[:, u % 2, :].rearrange("p (h e) -> p h e", e=HEAD),
                                X_AXIS, ALU.add).then_inc(s["part"], 1)

            def add(step, b, e):
                score = tile_of(SC, e)
                v.wait_ge(s["part"], step + 3)
                v.wait_ge(s["sum"], step + 4)
                v.tensor_tensor(score, score, part[:, b, :], ALU.add).then_inc(s["sum"], 1)

            def steps(j):
                for u in range(UNROLL):
                    step, later = UNROLL * j + u, not isinstance(j, int)
                    if u % 4 == 0:
                        v.wait_ge(s["hot_turned"], step + HOT_AHEAD - 12 + 8)
                        one_hot_of_four(v, T, hot, step + HOT_AHEAD, u + HOT_AHEAD).then_inc(s["hot"], 1)
                    product(step, u, j)
                    if u >= 1 or later:
                        reduce_heads(step - 1, u - 1)
                    if u >= SCORE_LAG or later:
                        if u % 4 == 0:
                            e = load_four(nc, v, e_regs, T["e"], step - SCORE_LAG, ETILES - 1)
                        add(step - SCORE_LAG, u % 4, e[u % 4])

            for k in range(0, HOT_AHEAD, 4):
                one_hot_of_four(v, T, hot, k, k).then_inc(s["hot"], 1)
            blocks_of_steps(v, steps)
            reduce_heads(STEPS - 1, STEPS - 1)
            e = load_four(nc, v, e_regs, T["e"], STEPS - SCORE_LAG, ETILES - 1)
            for k in range(SCORE_LAG):
                add(STEPS - SCORE_LAG + k, k, e[k])


def edge_softmax(nc, G, SC):
    hold, ident = G["hold"], G["ident"]
    last = LIST - 1
    SCv = SC[:].rearrange("p (c b) h -> p c b h", c=CHUNKS)
    rows_of = G["dst_tiles"].rearrange("(c r) e -> c (r e)", c=CHUNKS)
    sems = dict(dst=0, pen=0, tile=2, turned=2, put=2, scan=0, row=0, back=2, mturned=2, sub=2, done=0)
    with phase(nc, "segmax", sems) as (block, s, sb, ps):
        dst = sb("dst", [128, LIST], I32)
        pen = sb("pen", [128, LIST + 1])
        ST = sb("ST", [128, LIST])
        sct, mt = sb("sct", [EP, 2, 128]), sb("mt", [128, 2, EP])
        ends = sb("ends", [128, 4])
        er, pr = sb("er", [1, 4, CHUNKS, H1]), sb("pr", [1, 4, H1, CHUNKS])
        same, whole, join = sb("same", [1, H1, CHUNKS]), sb("whole", [1, H1, CHUNKS]), sb("join", [1, H1, CHUNKS])
        pf, pb = sb("pf", [1, H1, CHUNKS]), sb("pb", [1, H1, CHUNKS])
        xf, xb = sb("xf", [1, H1, CHUNKS]), sb("xb", [1, H1, CHUNKS])
        cf, cb = sb("cf", [1, H1, CHUNKS]), sb("cb", [1, H1, CHUNKS])
        carry_row, carry = sb("carry_row", [1, 2, CHUNKS, H1]), sb("carry", [128, 2])
        psS, psM, psR = ps("S", 2), ps("M", 2), ps("R")

        @block.sync
        def _(sp):
            for c in range(CHUNKS):
                sp.dma_start(dst[c * H1:(c + 1) * H1, :], rows_of[c:c + 1, :].to_broadcast([H1, LIST])).then_inc(s["dst"], 16)

        @block.scalar
        def _(act):
            def take(k, b):
                hold(act, s["turned"], k + 1)
                act.copy(sct[:, b, :].rearrange("p (c h) -> p c h", h=H1),
                         SCv[:, :, bass.ds(k, 1), :].rearrange("p c b h -> p c (b h)")).then_inc(s["tile"], 1)
            alternating(act, CHUNK_TILES, take)
            act.wait_ge(s["scan"], 4)

            def back(k, b):
                hold(act, s["mturned"], k + 1)
                act.copy(mt[:, b, :], ST[:, bass.ds(k * EP, EP)]).then_inc(s["back"], 1)
            alternating(act, CHUNK_TILES, back)
            act.wait_ge(s["sub"], 2 + CHUNK_TILES)
            act.activation(SC[:], SC[:], ACT.Exp).then_inc(s["done"], 1)

        @block.tensor
        def _(pe):
            def turn(k, b):
                pe.wait_ge(s["tile"], k + 3)
                pe.wait_ge(s["put"], k + 1)
                pe.transpose(psS[:, b, 0:128], sct[:, b, :], ident[:]).then_inc(s["turned"], 1)
            alternating(pe, CHUNK_TILES, turn)
            pe.wait_ge(s["row"], 1)
            for k in range(4):
                mm = pe.matmul(psR[0:1, 0, k * 128:(k + 1) * 128], ends[:, k:k + 1], ident[:], start=True, stop=True)
            mm.then_inc(s["row"], 1)
            pe.wait_ge(s["row"], 4)
            for k in range(2):
                mm = pe.matmul(psR[:, 0, k:k + 1], carry_row[:, k].rearrange("a c h -> a (c h)"), G["ones"][0:1, 0:1],
                               start=True, stop=True)
            mm.then_inc(s["row"], 1)

            def turn_back(k, b):
                pe.wait_ge(s["back"], k + 3)
                pe.wait_ge(s["sub"], k + 1)
                pe.transpose(psM[:, b, 0:EP], mt[:, b, :], ident[:]).then_inc(s["mturned"], 1)
            alternating(pe, CHUNK_TILES, turn_back)

        @block.vector
        def _(v):
            count = [0]

            def link(ins):
                count[0] += 1
                ins.then_inc(s["pen"], 1)
                v.wait_ge(s["pen"], count[0])

            v.wait_ge(s["dst"], 16 * CHUNKS)
            v.memset(pen[:, 0:1], 0.0)
            v.memset(pen[:, LIST:LIST + 1], 0.0)
            v.tensor_copy(ends[:, 2:3], dst[:, 0:1])
            v.tensor_copy(ends[:, 3:4], dst[:, last:last + 1])
            link(v.tensor_tensor(pen[:, 1:LIST], dst[:, 1:LIST], dst[:, 0:last], ALU.is_equal))
            link(v.tensor_scalar(pen[:, 1:LIST], pen[:, 1:LIST], -1.0, BIG, ALU.add, ALU.mult))

            def put(k, b):
                hold(v, s["turned"], k + 3)
                v.tensor_copy(ST[:, bass.ds(k * EP, EP)], psS[:, b, 0:128]).then_inc(s["put"], 1)
            alternating(v, CHUNK_TILES, put)
            v.wait_ge(s["put"], 2 + CHUNK_TILES)

            def scan(first, second):
                v.tensor_tensor_scan(ST[:], pen[:, 0:LIST], ST[:], first, ALU.add, ALU.max).then_inc(s["scan"], 1)
                v.wait_ge(s["scan"], 1 if isinstance(first, float) else 3)
                v.tensor_tensor_scan(ST[:, ::-1], pen[:, LIST:0:-1], ST[:, ::-1], second, ALU.add, ALU.max
                                     ).then_inc(s["scan"], 1)
                v.wait_ge(s["scan"], 2 if isinstance(first, float) else 4)

            scan(-BIG, -BIG)
            v.tensor_copy(ends[:, 0:1], ST[:, last:last + 1])
            v.tensor_copy(ends[:, 1:2], ST[:, 0:1]).then_inc(s["row"], 1)
            v.wait_ge(s["row"], 2)
            link(v.tensor_copy(er[:].rearrange("a k c h -> a (k c h)"), psR[0:1, 0, :]))
            link(v.tensor_copy(pr[:], er[:].rearrange("a k c h -> a k h c")))
            a, f, d0, d1 = (pr[:, k] for k in range(4))
            C1 = CHUNKS - 1
            v.memset(same[:, :, 0:1], 0.0)
            link(v.tensor_tensor(same[:, :, 1:CHUNKS], d0[:, :, 1:CHUNKS], d1[:, :, 0:C1], ALU.is_equal))
            link(v.tensor_tensor(whole[:], d0, d1, ALU.is_equal))
            link(v.tensor_tensor(pf[:], whole[:], same[:], ALU.mult))
            v.memset(pb[:, :, C1:CHUNKS], 0.0)
            link(v.tensor_tensor(pb[:, :, 0:C1], whole[:, :, 0:C1], same[:, :, 1:CHUNKS], ALU.mult))
            for t in (pf, pb):
                link(v.tensor_scalar(t[:], t[:], -1.0, BIG, ALU.add, ALU.mult))
            link(v.tensor_scalar(join[:], same[:], -1.0, BIG, ALU.add, ALU.mult))

            def flat(t):
                return t[:].rearrange("a h c -> a (h c)")
            link(v.tensor_tensor_scan(flat(xf), flat(pf), a.rearrange("a h c -> a (h c)"), -BIG, ALU.add, ALU.max))
            link(v.tensor_tensor_scan(flat(xb)[:, ::-1], flat(pb)[:, ::-1], f.rearrange("a h c -> a (h c)")[:, ::-1],
                                      -BIG, ALU.add, ALU.max))
            v.memset(cf[:, :, 0:1], -BIG)
            v.memset(cb[:, :, C1:CHUNKS], -BIG)
            link(v.tensor_tensor(cf[:, :, 1:CHUNKS], xf[:, :, 0:C1], join[:, :, 1:CHUNKS], ALU.add))
            link(v.tensor_tensor(cb[:, :, 0:C1], xb[:, :, 1:CHUNKS], join[:, :, 1:CHUNKS], ALU.add))
            v.tensor_copy(carry_row[:, 0], cf[:].rearrange("a h c -> a c h")).then_inc(s["row"], 1)
            v.tensor_copy(carry_row[:, 1], cb[:].rearrange("a h c -> a c h")).then_inc(s["row"], 1)
            v.wait_ge(s["row"], 5)
            link(v.tensor_copy(carry[:], psR[:, 0, 0:2]))
            scan(carry[:, 0:1], carry[:, 1:2])

            def subtract(k, b):
                hold(v, s["mturned"], k + 3)
                part = SCv[:, :, bass.ds(k, 1), :].rearrange("p c b h -> p c (b h)")
                v.tensor_tensor(part, part, psM[:, b, 0:128].rearrange("p (c h) -> p c h", h=H1), ALU.subtract
                                ).then_inc(s["sub"], 1)
            alternating(v, CHUNK_TILES, subtract)


def combine1(nc, G, L, acc):
    A, hold, X = G["A"], G["hold"], G["X"]
    sems = dict(load=0, both=0, z=0, t_ready=0, t_turned=2, tT=2, o=2, x_done=2, biased=2, kept=0, **hT_sems())
    with phase(nc, "comb1", sems) as (block, s, sb, ps):
        h, hT = sb("h", [TP, 2, 2, D]), sb("hT", [128, 2, HALVES, PT])
        t, tT = sb("t", [TP, 2, 2, D]), sb("tT", [128, 2, HALVES, PT])
        zinv, bb, hk = sb("zinv", [TP, NT, H1]), sb("bb", [TP, D]), sb("hk", [TP, 2, D])
        psT, psA, o = ps("psT"), ps("psA"), ps("o", 2)

        @block.sync
        def _(sp):
            sp.dma_start(bb[:], row_of(A["L1_mix_b_out"], D)).then_inc(s["load"], 16)

        @block.gpsimd
        def _(pool):
            pool.wait_ge(s["load"], 16)
            pool.tensor_tensor(bb[:], bb[:], L.ba[:], ALU.add).then_inc(s["both"], 1)
            pool.wait_ge(s["both"], 1)

            def keep(p, b):
                Xp = pair_of(X, p)
                hold(pool, s["h_ready"], 2 * p + 2)
                pool.tensor_scalar(hk[:], h[:, b], L.keep_h[0:TP, :], None, ALU.mult).then_inc(s["kept"], 1)
                hold(pool, s["kept"], 2 * p + 1)
                pool.tensor_tensor(Xp, Xp, hk[:], ALU.add).then_inc(s["kept"], 1)
                hold(pool, s["kept"], 2 * p + 2)
                pool.tensor_tensor(Xp, Xp, bb[:].unsqueeze(1).to_broadcast([TP, 2, D]), ALU.add).then_inc(s["biased"], 1)
            pairs(pool, keep)

        @block.vector
        def _(v):
            v.tensor_scalar(zinv[:], acc[:, :, D:D + H1], 0.5, None, ALU.max).then_inc(s["z"], 1)
            v.wait_ge(s["z"], 1)
            v.reciprocal(zinv[:], zinv[:]).then_inc(s["z"], 1)
            v.wait_ge(s["z"], 2)

            def ahead(p, b):
                v.wait_ge(s["biased"], p + 1)
                normalise_pair(v, G, s, h, p, b)
                v.wait_ge(s["t_turned"], p + 1)
                v.tensor_tensor(t[:, b].rearrange("p t (h e) -> p t h e", e=HEAD),
                                acc[:, bass.ds(2 * p, 2), 0:D].rearrange("p t (h e) -> p t h e", e=HEAD),
                                zinv[:, bass.ds(2 * p, 2), :].unsqueeze(3).to_broadcast([TP, 2, H1, HEAD]),
                                ALU.mult).then_inc(s["t_ready"], 1)

            def add(p, b):
                v.wait_ge(s["biased"], p + 3)
                add_and_stats(v, G, s, o[0:TP, b].rearrange("p (t d) -> p t d", t=2), p, 2)
            pairs(v, add, early=ahead)

        @block.scalar
        def _(act):
            def evacuate(p, b):
                affine_evacuate(act, s, psT, hT, None, None, p, b, (s["o"], p + 1))
                act.wait_ge(s["t_turned"], p + 3)
                act.copy(tT[:, b], psA[:, 0, 0:2 * PT].rearrange("p (c t) -> p c t", c=HALVES)).then_inc(s["tT"], 1)
            pairs(act, evacuate)

        @block.tensor
        def _(pe):
            def ahead(p, b):
                turn_pair(pe, G, s, h, psT, p, b)
                pe.wait_ge(s["t_ready"], p + 1)
                pe.wait_ge(s["tT"], p + 2)
                for c in range(HALVES):
                    for k in range(2):
                        mm = pe.transpose(psA[:, 0, c * 250 + k * TP:c * 250 + (k + 1) * TP],
                                          t[:, b, k, c * 128:(c + 1) * 128], G["ident"][0:TP, 0:TP])
                mm.then_inc(s["t_turned"], 1)

            def main(p, b):
                pe.wait_ge(s["hT_ready"], p + 2)
                pe.wait_ge(s["tT"], p + 3)
                pe.wait_ge(s["x_done"], p + 1)
                for k in range(2):
                    for n, (src, w) in enumerate(((hT, L.Gm), (tT, L.WaT))):
                        for c in range(HALVES):
                            mm = pe.matmul(o[0:TP, b, k * D:(k + 1) * D], src[:, b, c, k * TP:(k + 1) * TP], w[:, c, :],
                                           start=(n + c == 0), stop=(n + c == 2))
                mm.then_inc(s["o"], 1)
            pairs(pe, main, ahead)


def layer1(nc, G, T):
    dram = G["dram"]
    k_d, v_d = dram("k1_d", [NODES, D]), dram("v1_d", [NODES, D])
    rings = [[G["semaphore"](f"ring{m}_{n}") for n in range(RING)] for m in range(2)]
    with ExitStack() as ctx:
        L = Layer1(nc, G, ctx)
        buf = ctx.enter_context(nc.sbuf_tensor("MK_SC", [EP, NT * MW], F32))
        MK = buf[0:TP, :].rearrange("p (t d) -> p t d", d=MW)
        SC = buf[:, 0:ETILES * H1].rearrange("p (t h) -> p t h", h=H1)
        with nc.sbuf_tensor("Q", [TP, NT, D], F32) as Q:
            with ExitStack() as kv:
                MV = kv.enter_context(nc.sbuf_tensor("MV", [TP, NT, 1, MW + 1], F32))
                kmax = kv.enter_context(nc.sbuf_tensor("kmax1", [TP, 2, MW], F32))
                Cp = kv.enter_context(nc.sbuf_tensor("Cp1", [128, 1, D], F32))
                project1(nc, G, L, Q, k_d, v_d, MK, MV, kmax)
                context(nc, G, "ctx1", 1, MK, MV, kmax, 1.0, L.Wmo, Cp, (L.WqmT, HEAD ** -0.5, L.Gm))
            edge_scores(nc, G, T, rings[0], Q, k_d, SC)
        edge_softmax(nc, G, SC)
        acc = ctx.enter_context(nc.sbuf_tensor("acc1", [TP, NT, D + H1], F32))
        edge_sum(nc, G, "sum1", T, rings[1], v_d, acc, H1, weights=SC)
        combine1(nc, G, L, acc)


SH, SD, SG = 8, 64, 64
SI = SH * SD
SJ = SI // 128


def slice_attention(nc, G):
    A = G["A"]
    with ExitStack() as ctx:
        def keep(n, shape):
            return ctx.enter_context(nc.sbuf_tensor("sl_" + n, shape, F32))
        W = keep("W", [TP, NT, SI])
        fold_out = keep("fold", [128, SJ, D])
        with ExitStack() as mid:
            def part(n, shape):
                return mid.enter_context(nc.sbuf_tensor("sl_" + n, shape, F32))
            tokens, norms = part("tokens", [128, SJ, 128]), part("norms", [TP, SI])
            with ExitStack() as w:
                Wxs = w.enter_context(nc.sbuf_tensor("sl_Wxs", [128, HALVES, SI], F32))
                bxs = w.enter_context(nc.sbuf_tensor("sl_bxs", [TP, SI], F32))
                slice_weights_prep(nc, G, Wxs, bxs)
                slice_assign(nc, G, Wxs, bxs, W, tokens, norms)
            slice_mix(nc, G, tokens, norms, fold_out)
        slice_out(nc, G, W, fold_out)


def slice_weights_prep(nc, G, Wxs, bxs):
    A, ident = G["A"], G["ident"]
    loads = 6 + SH
    with phase(nc, "slprep", dict(clear=0, load=0, v=0, turned=0, ps=0)) as (block, s, sb, ps):
        Wx, WxT = sb("Wx", [128, HALVES, SI]), sb("WxT", [128, SJ, D])
        WS, R = sb("WS", [128, 128]), sb("R", [128, SJ, 128])
        bx, bs, tinv = sb("bx", [128, SJ]), sb("bs", [128, 1]), sb("tinv", [128, SJ])
        dg = sb("dg", [128, SJ, 128])
        bb, sp_bs = sb("bb", [128, SJ, TP]), sb("sbs", [128, TP])
        tp, wp, bp = ps("tp", 2), ps("wp", 2), ps("bp")

        @block.sync
        def _(sp):
            sp.wait_ge(s["clear"], 1)
            both = [(WS[k * 64:(k + 1) * 64, k * 64:(k + 1) * 64], A["L1_ffn_W_slice"]) for k in range(2)]
            both += [(bs[k * 64:(k + 1) * 64, :], A["L1_ffn_b_slice"].rearrange("(g a) -> g a", a=1)) for k in range(2)]
            both += [(Wx[:], A["L1_ffn_W_x"].rearrange("(c p) n -> p c n", p=128)),
                     (bx[:], A["L1_ffn_b_x"].rearrange("(j p) -> p j", p=128))]
            temp = A["L1_ffn_temperature"].rearrange("a h b c -> a (h b c)")
            both += [(tinv[k % 2 * 64:(k % 2 + 1) * 64, k // 2:k // 2 + 1], temp[0:1, k:k + 1].to_broadcast([64, 1]))
                     for k in range(SH)]
            for dst, src in both:
                sp.dma_start(dst, src, allow_slow_non_contiguous=True).then_inc(s["load"], 16)
            assert len(both) == loads

        @block.vector
        def _(v):
            count = [0]

            def link(ins):
                count[0] += 1
                ins.then_inc(s["v"], 1)
                v.wait_ge(s["v"], count[0])

            v.memset(WS[:], 0.0).then_inc(s["clear"], 1)
            v.wait_ge(s["load"], 16 * (loads))
            link(v.tensor_scalar(tinv[:], tinv[:], 0.1, 5.0, ALU.max, ALU.min))
            link(v.reciprocal(tinv[:], tinv[:]))
            for j in range(SJ):
                v.tensor_scalar(R[:, j, :], WS[:], tinv[:, j:j + 1], None, ALU.mult)
                v.tensor_scalar(dg[:, j, :], ident[:], tinv[:, j:j + 1], None, ALU.mult)
                v.tensor_scalar(bb[:, j, :], G["ones"][:, 0:TP], bx[:, j:j + 1], None, ALU.mult)
            link(v.tensor_scalar(sp_bs[:], G["ones"][:, 0:TP], bs[:], None, ALU.mult))
            v.wait_ge(s["turned"], 1)
            link(v.tensor_copy(WxT[:].rearrange("p (a j) i -> p a (j i)", a=2), tp[:]))
            v.wait_ge(s["ps"], 1)
            v.tensor_copy(Wxs[:], wp[:])
            v.tensor_copy(bxs[:], bp[0:TP, 0, :])

        @block.tensor
        def _(pe):
            pe.wait_ge(s["load"], 16 * (loads))
            for j in range(SJ):
                for c in range(HALVES):
                    at = j % 2 * D + c * 128
                    mm = pe.transpose(tp[:, j // 2, at:at + 128], Wx[:, c, j * 128:(j + 1) * 128], ident[:])
            mm.then_inc(s["turned"], 1)
            pe.wait_ge(s["v"], 4)
            for j in range(SJ):
                cols = slice(j * 128, (j + 1) * 128)
                for c in range(HALVES):
                    pe.matmul(wp[:, c, cols], WxT[:, j, c * 128:(c + 1) * 128], R[:, j, :], start=True, stop=True)
                pe.matmul(bp[0:TP, 0, cols], bb[:, j, :], R[:, j, :], start=True, stop=False)
                mm = pe.matmul(bp[0:TP, 0, cols], sp_bs[:], dg[:, j, :], start=False, stop=True)
            mm.then_inc(s["ps"], 1)


def slice_assign(nc, G, Wxs, bxs, W, tokens, norms):
    A, hold, X = G["A"], G["hold"], G["X"]
    sems = dict(load=0, lg_ps=0, lg_read=2, fx_ps=4, fx_sb=2, m=0, z=0, sub=0, exp=0, w=4, norm=1, sliced=2, init=0,
                done=0, **hT_sems())
    with phase(nc, "slassign", sems) as (block, s, sb, ps):
        Wfx = sb("Wfx", [128, HALVES, SI])
        h, hT = sb("h", [TP, 2, 2, D]), sb("hT", [128, 2, HALVES, PT])
        lg = sb("lg", [TP, 2, 2, SI])
        fx = sb("fx", [TP, 2, 2, SI])
        m, z = sb("m", [TP, 2, 2, SH]), sb("z", [TP, 2, 2, SH])
        psT, lp, fp, tk = ps("psT"), ps("lp", 2), ps("fp", 2), ps("tk")

        @block.sync
        def _(sp):
            sp.dma_start(Wfx[:], A["L1_ffn_W_fx"].rearrange("(c p) n -> p c n", p=128)).then_inc(s["load"], 16)

        @block.vector
        def _(v):
            v.memset(norms[:], 0.0).then_inc(s["init"], 1)

            def heads(t):
                return t.rearrange("p (h g) -> p h g", g=SG)

            def logits(p, b):
                for t in range(2):
                    q, x = 2 * p + t, lg[:, b, t, :]
                    v.wait_ge(s["lg_ps"], q + 1)
                    v.wait_ge(s["w"], q + 1)
                    v.tensor_tensor(x, lp[0:TP, t, :], bxs[:], ALU.add).then_inc(s["lg_read"], 1)
                    v.wait_ge(s["lg_read"], q + 3)
                    v.tensor_reduce(m[:, b, t, :], heads(x), X_AXIS, ALU.max).then_inc(s["m"], 1)
                    v.wait_ge(s["m"], q + 1)
                    v.tensor_tensor(heads(x), heads(x), m[:, b, t, :].unsqueeze(2).to_broadcast([TP, SH, SG]),
                                    ALU.subtract).then_inc(s["sub"], 1)

            def early(p, b):
                normalise_pair(v, G, s, h, p, b)
                if isinstance(p, int) and p == 1:
                    logits(0, 0)

            def main(p, b):
                for t in range(2):
                    v.wait_ge(s["exp"], 2 * p + t + 1)
                    v.wait_ge(s["w"], 2 * p + t + 1)
                    v.tensor_reduce(z[:, b, t, :], heads(lg[:, b, t, :]), X_AXIS, ALU.add).then_inc(s["z"], 1)
                    v.wait_ge(s["z"], 4 * p + 1 + 2 * t)
                    v.reciprocal(z[:, b, t, :], z[:, b, t, :]).then_inc(s["z"], 1)
                if not isinstance(p, int) or p + 1 < PAIRS:
                    logits(p + 1, 1 - b)
            pairs(v, main, early=early)
            v.wait_ge(s["done"], 1)
            v.tensor_copy(tokens[:], tk[:, 0, :].rearrange("p (j g) -> p j g", j=SJ))

        @block.gpsimd
        def _(pool):
            pool.wait_ge(s["init"], 1)

            def divide(p, b):
                for t in range(2):
                    q = 2 * p + t
                    hold(pool, s["z"], 4 * p + 2 + 2 * t)
                    wq = tile_of(W, q)
                    pool.tensor_tensor(wq.rearrange("p (h g) -> p h g", g=SG),
                                       lg[:, b, t, :].rearrange("p (h g) -> p h g", g=SG),
                                       z[:, b, t, :].unsqueeze(2).to_broadcast([TP, SH, SG]), ALU.mult).then_inc(s["w"], 1)
                    hold(pool, s["w"], q + 5)
                    hold(pool, s["norm"], q + 1)
                    pool.tensor_tensor(norms[:], norms[:], wq, ALU.add).then_inc(s["norm"], 1)
            pairs(pool, divide)

        @block.scalar
        def _(act):
            def exponentials(p, b):
                for t in range(2):
                    act.wait_ge(s["sub"], 2 * p + t + 1)
                    act.activation(lg[:, b, t, :], lg[:, b, t, :], ACT.Exp).then_inc(s["exp"], 1)

            def main(p, b):
                for t in range(2):
                    act.wait_ge(s["fx_ps"], 2 * p + t + 5)
                    act.wait_ge(s["sliced"], p + 1)
                    act.copy(fx[:, b, t, :], fp[0:TP, t, :]).then_inc(s["fx_sb"], 1)
                if not isinstance(p, int) or p + 1 < PAIRS:
                    exponentials(p + 1, 1 - b)

            def ahead(p, b):
                affine_evacuate(act, s, psT, hT, None, None, p, b, (s["fx_ps"], 2 * p + 2))
                if isinstance(p, int) and p == 0:
                    exponentials(0, 0)
            pairs(act, main, ahead)

        @block.tensor
        def _(pe):
            pe.wait_ge(s["load"], 16)
            pe.matmul(tk[:, 0, :], G["zeros"][:, 0:128], Wxs[:, 0, :], start=True, stop=False, skip_group_check=True)

            def project(p, b):
                pe.wait_ge(s["hT_ready"], p + 2)
                for bank, w, free, ready in ((lp, Wxs, "lg_read", "lg_ps"), (fp, Wfx, "fx_sb", "fx_ps")):
                    for t in range(2):
                        pe.wait_ge(s[free], 2 * p + t + 1)
                        for c in range(HALVES):
                            mm = pe.matmul(bank[0:TP, t, :], hT[:, b, c, t * TP:(t + 1) * TP], w[:, c, :],
                                           start=(c == 0), stop=(c == 1))
                        mm.then_inc(s[ready], 1)

            def ahead(p, b):
                turn_pair(pe, G, s, h, psT, p, b)
                project(p, b)

            def sums(p, b):
                pe.wait_ge(s["w"], 2 * p + 6)
                pe.wait_ge(s["fx_sb"], 2 * p + 4)
                for t in range(2):
                    for j in range(SJ):
                        mm = pe.matmul(tk[:, 0, j * 128:(j + 1) * 128], fx[:, b, t, j * 128:(j + 1) * 128],
                                       W[:, bass.ds(2 * p + t, 1), j * 128:(j + 1) * 128].rearrange("p a g -> p (a g)"),
                                       start=False, stop=(isinstance(p, int) and t == 1), skip_group_check=True)
                mm.then_inc(s["sliced"], 1)
            pairs(pe, sums, ahead)
            pe.wait_ge(s["sliced"], PAIRS + 2)
            pe.sem_inc(s["done"], 1)


def slice_mix(nc, G, tokens, norms, fold_out):
    A, ident = G["A"], G["ident"]
    with phase(nc, "slmix", dict(clear=0, load=0, v=0, a=0, p=0)) as (block, s, sb, ps):
        Wq, Wk, Wv = (sb(n, [128, 128]) for n in ("Wq", "Wk", "Wv"))
        Wo, bfx = sb("Wo", [128, SJ, D]), sb("bfx", [128, SJ])
        n1, n2 = sb("n1", [128, SJ, 128]), sb("n2", [128, SJ, 128])
        tok = sb("tok", [128, SJ, 128])
        qT, kT, vv = sb("qT", [128, SI]), sb("kT", [128, SI]), sb("vv", [128, SJ, 128])
        at, ab = sb("at", [128, SJ, SG]), sb("ab", [128, SJ, 128])
        abT, osT = sb("abT", [128, SJ, 128]), sb("osT", [128, SJ, 128])
        m, z = sb("m", [128, SJ]), sb("z", [128, SJ])
        p0, p1, p2, p3 = ps("p0"), ps("p1"), ps("p2"), ps("p3", 2)

        def blocks(bank):
            return bank[:, 0, :].rearrange("p (j g) -> p j g", j=SJ)

        @block.sync
        def _(sp):
            sp.wait_ge(s["clear"], 1)
            loads = [(w[k * 64:(k + 1) * 64, k * 64:(k + 1) * 64], A[n]) for w, n in
                     ((Wq, "L1_ffn_W_q"), (Wk, "L1_ffn_W_k"), (Wv, "L1_ffn_W_v")) for k in range(2)]
            loads += [(Wo[:], A["L1_ffn_W_out"].rearrange("(j p) d -> p j d", p=128)),
                      (bfx[:], A["L1_ffn_b_fx"].rearrange("(j p) -> p j", p=128))]
            for dst, src in loads:
                sp.dma_start(dst, src, allow_slow_non_contiguous=True).then_inc(s["load"], 16)

        @block.vector
        def _(v):
            count = [0]

            def link(ins):
                count[0] += 1
                ins.then_inc(s["v"], 1)
                v.wait_ge(s["v"], count[0])

            def each(t):
                return t[:].unsqueeze(2).to_broadcast([128, SJ, SG])

            v.memset(ab[:], 0.0)
            v.memset(Wq[:], 0.0)
            v.memset(Wk[:], 0.0)
            v.memset(Wv[:], 0.0).then_inc(s["clear"], 1)
            v.wait_ge(s["clear"], 1)
            v.wait_ge(s["load"], 16 * 8)
            v.wait_ge(s["p"], 1)
            link(v.tensor_copy(n1[:], blocks(p0)))
            link(v.tensor_scalar(n2[:], n1[:], 1e-5, None, ALU.add))
            link(v.reciprocal(n2[:], n2[:]))
            for j in range(SJ):
                d = v.scalar_tensor_tensor(out=tok[:, j, :], in0=n1[:, j, :], scalar=bfx[:, j:j + 1],
                                           in1=tokens[:, j, :], op0=ALU.mult, op1=ALU.add)
            link(d)
            link(v.tensor_tensor(tok[:], tok[:], n2[:], ALU.mult))
            link(v.tensor_tensor(tok[:], tok[:], G["mask64"][:].unsqueeze(1).to_broadcast([128, SJ, 128]), ALU.mult))
            v.wait_ge(s["p"], 2)
            v.tensor_copy(qT[:], p0[:, 0, :])
            v.tensor_copy(kT[:], p1[:, 0, :])
            link(v.tensor_copy(vv[:], blocks(p2)))
            v.wait_ge(s["p"], 3)
            for k in range(2):
                rows = slice(64 * k, 64 * k + 64)
                d = v.tensor_scalar(at[rows], blocks(p0)[rows, :, rows], SD ** -0.5, None, ALU.mult)
            link(d)
            link(v.tensor_reduce(m[:], at[:], X_AXIS, ALU.max))
            link(v.tensor_tensor(at[:], at[:], each(m), ALU.subtract))
            v.wait_ge(s["a"], 1)
            link(v.tensor_reduce(z[:], at[:], X_AXIS, ALU.add))
            link(v.reciprocal(z[:], z[:]))
            for k in range(2):
                rows = slice(64 * k, 64 * k + 64)
                d = v.tensor_tensor(ab[rows, :, rows], at[rows], z[rows].unsqueeze(2).to_broadcast([64, SJ, SG]), ALU.mult)
            link(d)
            v.wait_ge(s["p"], 4)
            link(v.tensor_copy(abT[:], blocks(p1)))
            v.wait_ge(s["p"], 5)
            link(v.tensor_copy(osT[:], blocks(p2)))
            v.wait_ge(s["p"], 6)
            v.tensor_copy(fold_out[:].rearrange("p (a j) d -> p a (j d)", a=2), p3[:])

        @block.scalar
        def _(act):
            act.wait_ge(s["v"], 10)
            act.activation(at[:], at[:], ACT.Exp).then_inc(s["a"], 1)

        @block.tensor
        def _(pe):
            pe.matmul(p0[:, 0, :], G["ones"][0:TP, :], norms[:], start=True, stop=True).then_inc(s["p"], 1)
            pe.wait_ge(s["v"], 6)
            pe.matmul(p0[:, 0, :], Wq[:], tok[:].rearrange("p j g -> p (j g)"), start=True, stop=True)
            pe.matmul(p1[:, 0, :], Wk[:], tok[:].rearrange("p j g -> p (j g)"), start=True, stop=True)
            for j in range(SJ):
                mm = pe.matmul(blocks(p2)[:, j, :], tok[:, j, :], Wv[:], start=True, stop=True)
            mm.then_inc(s["p"], 1)
            pe.wait_ge(s["v"], 7)
            for j in range(SJ):
                cols = slice(j * 128, (j + 1) * 128)
                mm = pe.matmul(blocks(p0)[:, j, :], qT[:, cols], kT[:, cols], start=True, stop=True)
            mm.then_inc(s["p"], 1)
            pe.wait_ge(s["v"], 13)
            for j in range(SJ):
                mm = pe.transpose(blocks(p1)[:, j, :], ab[:, j, :], ident[:])
            mm.then_inc(s["p"], 1)
            pe.wait_ge(s["v"], 14)
            for j in range(SJ):
                mm = pe.matmul(blocks(p2)[:, j, :], vv[:, j, :], abT[:, j, :], start=True, stop=True)
            mm.then_inc(s["p"], 1)
            pe.wait_ge(s["v"], 15)
            for j in range(SJ):
                mm = pe.matmul(p3[:, j // 2, j % 2 * D:(j % 2 + 1) * D], osT[:, j, :], Wo[:, j, :], start=True, stop=True)
            mm.then_inc(s["p"], 1)


def slice_out(nc, G, W, fold_out):
    A, hold, X = G["A"], G["hold"], G["X"]
    out_v = G["out"].rearrange("(n t p) d -> n p t d", t=2, p=TP)
    sems = dict(load=0, wc=0, w_turned=2, wT=2, o=2, biased=0, y=2, out0=16, out1=16)
    with phase(nc, "slout", sems) as (block, s, sb, ps):
        wc, wT = sb("wc", [TP, 2, 2, SI]), sb("wT", [128, 2, 2, SI])
        bo, y = sb("bo", [TP, D]), sb("y", [TP, 2, 2, D])
        psT, o = ps("psT", 4), ps("o", 2)

        @block.sync
        def _(sp):
            sp.dma_start(bo[:], row_of(A["L1_ffn_b_out"], D)).then_inc(s["load"], 16)

            def save(p, b):
                hold(sp, s["y"], p + 3)
                sp.dma_start(out_v[bass.ds(p, 1)].rearrange("n p t d -> (n p) t d"), y[:, b]).then_inc(s[f"out{b}"], 16)
            pairs(sp, save)
            sp.wait_ge(s["out0"], 16 * (PAIRS // 2 + 2))
            sp.wait_ge(s["out1"], 16 * (PAIRS // 2 + 1))

        @block.gpsimd
        def _(pool):
            pool.wait_ge(s["load"], 16)

            def bias(p, b):
                Xp = pair_of(X, p)
                pool.tensor_tensor(Xp, Xp, bo[:].unsqueeze(1).to_broadcast([TP, 2, D]), ALU.add).then_inc(s["biased"], 1)
            pairs(pool, bias)

        @block.vector
        def _(v):
            def copy(p, b):
                hold(v, s["w_turned"], p + 1)
                v.tensor_copy(wc[:, b], pair_of(W, p)).then_inc(s["wc"], 1)

            def add(p, b):
                v.wait_ge(s["o"], p + 3)
                v.wait_ge(s["biased"], p + 1)
                v.wait_ge(s[f"out{b}"], 16 * (p // 2) + 16)
                v.tensor_tensor(y[:, b], pair_of(X, p), o[0:TP, b].rearrange("p (t d) -> p t d", t=2), ALU.add
                                ).then_inc(s["y"], 1)
            pairs(v, add, early=copy)

        @block.scalar
        def _(act):
            def evacuate(p, b):
                act.wait_ge(s["w_turned"], p + 3)
                act.wait_ge(s["o"], p + 1)
                for t in range(2):
                    last = act.copy(wT[:, b, t, 0:SJ * TP], psT[:, 2 * b + t, 0:SJ * TP])
                last.then_inc(s["wT"], 1)
            pairs(act, evacuate)

        @block.tensor
        def _(pe):
            def turn(p, b):
                pe.wait_ge(s["wc"], p + 1)
                pe.wait_ge(s["wT"], p + 1)
                for t in range(2):
                    for j in range(SJ):
                        mm = pe.transpose(psT[:, 2 * b + t, j * TP:(j + 1) * TP], wc[:, b, t, j * 128:(j + 1) * 128],
                                          G["ident"][0:TP, 0:TP])
                mm.then_inc(s["w_turned"], 1)

            def product(p, b):
                pe.wait_ge(s["wT"], p + 3)
                pe.wait_ge(s["y"], p + 1)
                for t in range(2):
                    for j in range(SJ):
                        mm = pe.matmul(o[0:TP, b, t * D:(t + 1) * D], wT[:, b, t, j * TP:(j + 1) * TP], fold_out[:, j, :],
                                       start=(j == 0), stop=(j == SJ - 1))
                mm.then_inc(s["o"], 1)
            pairs(pe, product, turn)


def kernel(**inputs):
    import numpy as np
    import concourse.bacc as bacc
    from concourse import mybir
    from concourse.bass_utils import run_bass_kernel_spmd

    nc = bacc.Bacc("TRN2", target_bir_lowering=False, num_devices=1)
    arrays, A = {}, {}
    for name, value in inputs.items():
        a = np.ascontiguousarray(value)
        if a.ndim == 0:
            a = a.reshape(1)
        arrays[f"in_{name}_dram"] = a
        A[name] = nc.dram_tensor(f"in_{name}_dram", a.shape, mybir.dt.from_np(a.dtype), kind="ExternalInput").ap()
    out = nc.dram_tensor("out_0_dram", (NODES, D), mybir.dt.float32, kind="ExternalOutput").ap()
    build(nc, A, out)
    r = run_bass_kernel_spmd(nc, [arrays], core_ids=[0])
    return r.results[0]["out_0_dram"]
```
